# Optimizing a Trainium2 kernel written in Bass

```python
import numpy as np
import jax
import jax.numpy as jnp

def _softmax(x, axis=-1):
    return jax.nn.softmax(x, axis=axis)

def _gelu(x):
    return jax.nn.gelu(x, approximate=True)

def _silu(x):
    return jax.nn.silu(x)

def _sigmoid(x):
    return jax.nn.sigmoid(x)

def _layernorm(x, axis=-1, eps=1e-05):
    m = jnp.mean(x, axis=axis, keepdims=True)
    v = jnp.var(x, axis=axis, keepdims=True)
    return (x - m) / jnp.sqrt(v + eps)

def _scatter_add(tgt, idx, src, axis=0):
    return tgt.at[idx].add(src)

def _segment_sum(src, seg, n):
    return jax.ops.segment_sum(src, seg, n)
kernel_name = 'mk_gnn_ffn_d2_gnn_r8_498573'

def setup_inputs(seed: int=0):
    np.random.seed(seed)
    _w = jnp.asarray

    def _rec_inputs():
        import jax
        import jax.numpy as jnp
        _gk = jax.random.key(seed)
        x = -8.776e-05 + 1 * jax.random.normal(jax.random.fold_in(_gk, 1), (6250, 256), jnp.float32)
        src = jax.random.randint(jax.random.fold_in(_gk, 2), (100000,), 0, 6250, jnp.int32)
        dst = jax.random.randint(jax.random.fold_in(_gk, 3), (100000,), 0, 6250, jnp.int32)
        _o = jnp.argsort(dst, stable=True)
        src = src[_o]
        dst = dst[_o]
        return (x, src, dst)
    x, src, dst = _rec_inputs()

    def _L0_gnn_setup():
        import jax, jax.numpy as jnp
        import numpy as np
        N = 2500
        E = 40000
        IN = 256
        HID = 256
        OUT = 256
        H1 = 8
        D1 = HID // H1
        H2 = 1

        def gat_conv(h, src, dst, fc_w, attn_l, attn_r, bias, heads, out_feats):
            n = h.shape[0]
            feat = (h @ fc_w.T).reshape(n, heads, out_feats)
            el = jnp.sum(feat * attn_l, axis=-1)
            er = jnp.sum(feat * attn_r, axis=-1)
            e = jax.nn.leaky_relu(el[src] + er[dst], 0.2)
            m = jax.ops.segment_max(e, dst, num_segments=n)
            m = jnp.where(jnp.isfinite(m), m, 0.0)
            ex = jnp.exp(e - m[dst])
            ssum = jax.ops.segment_sum(ex, dst, num_segments=n)
            a = ex / ssum[dst]
            rst = jax.ops.segment_sum(feat[src] * a[..., None], dst, num_segments=n)
            return rst + bias.reshape(heads, out_feats)
        key = jax.random.key(seed)
        ks = jax.random.split(key, 16)
        s = 0.05
        inputs = jax.random.normal(ks[0], (N, IN), jnp.float32)
        src = jax.random.randint(ks[1], (E,), 0, N, jnp.int32)
        dst = jax.random.randint(ks[2], (E,), 0, N, jnp.int32)
        return {'inputs': inputs, 'src': src, 'dst': dst, 'fc1_w': jax.random.normal(ks[3], (H1 * D1, IN), jnp.float32) * s, 'attn_l1': jax.random.normal(ks[4], (H1, D1), jnp.float32) * s, 'attn_r1': jax.random.normal(ks[5], (H1, D1), jnp.float32) * s, 'bias1': jax.random.normal(ks[6], (H1 * D1,), jnp.float32) * s, 'fc2_w': jax.random.normal(ks[7], (H2 * OUT, HID), jnp.float32) * s, 'attn_l2': jax.random.normal(ks[8], (H2, OUT), jnp.float32) * s, 'attn_r2': jax.random.normal(ks[9], (H2, OUT), jnp.float32) * s, 'bias2': jax.random.normal(ks[10], (H2 * OUT,), jnp.float32) * s, 'wb0': jax.random.normal(ks[11], (HID, IN), jnp.float32) * s, 'bb0': jax.random.normal(ks[12], (HID,), jnp.float32) * s, 'wb1': jax.random.normal(ks[13], (OUT, IN + HID), jnp.float32) * s, 'bb1': jax.random.normal(ks[14], (OUT,), jnp.float32) * s}
    _L0_gnn_all = _L0_gnn_setup()
    _L0_gnn_in = {k: v for k, v in _L0_gnn_all.items() if k in ('fc1_w', 'attn_l1', 'attn_r1', 'bias1', 'fc2_w', 'attn_l2', 'attn_r2', 'bias2', 'wb0', 'bb0', 'wb1', 'bb1')}
    del _L0_gnn_all

    def _L0_ffn_setup():
        import math
        import jax, jax.numpy as jnp
        import numpy as np
        CAPACITY_FACTOR = 1.25
        key = jax.random.key(seed)
        ks = jax.random.split(key, 5)
        B, L, D, F, E = (8, 1024, 256, 1024, 8)
        h = jax.random.normal(ks[0], (B, L, D), dtype=jnp.float32)
        gate_w = jax.random.normal(ks[1], (D, E), dtype=jnp.float32) * 0.02
        gate_b = jnp.zeros((E,), dtype=jnp.float32)
        w1 = jax.random.normal(ks[2], (E, D, F), dtype=jnp.float32) * (1.0 / math.sqrt(D))
        b1 = jnp.zeros((E, F), dtype=jnp.float32)
        w2 = jax.random.normal(ks[3], (E, F, D), dtype=jnp.float32) * (1.0 / math.sqrt(F))
        b2 = jnp.zeros((E, D), dtype=jnp.float32)
        return {'h': h, 'gate_w': gate_w, 'gate_b': gate_b, 'w1': w1, 'b1': b1, 'w2': w2, 'b2': b2}
    _L0_ffn_all = _L0_ffn_setup()
    _L0_ffn_in = {k: v for k, v in _L0_ffn_all.items() if k in ('gate_w', 'gate_b', 'w1', 'b1', 'w2', 'b2')}
    del _L0_ffn_all

    def _L1_gnn_setup():
        import jax, jax.numpy as jnp
        import numpy as np
        N = 6250
        E_RAND = 100000
        IN, HID, H, OUT = (256, 64, 4, 256)
        NEG_SLOPE = 0.2

        def gat_layer(h, W, a_src, a_dst, src, dst, concat):
            n = h.shape[0]
            nh, nf = a_src.shape
            hp = (h @ W.T).reshape(n, nh, nf)
            e = (hp[src] * a_src).sum(-1) + (hp[dst] * a_dst).sum(-1)
            e = jnp.where(e > 0, e, NEG_SLOPE * e)
            e_max = jax.ops.segment_max(e, dst, num_segments=n)
            ex = jnp.exp(e - e_max[dst])
            e_sum = jax.ops.segment_sum(ex, dst, num_segments=n)
            alpha = ex / (e_sum[dst] + 1e-16)
            out = jax.ops.segment_sum(hp[src] * alpha[..., None], dst, num_segments=n)
            return out.reshape(n, nh * nf) if concat else out.mean(axis=1)
        key = jax.random.key(seed)
        ks = jax.random.split(key, 8)
        x = jax.random.normal(ks[0], (N, IN), dtype=jnp.float32)
        er = jax.random.randint(ks[1], (2, E_RAND), 0, N, dtype=jnp.int32)
        loops = jnp.arange(N, dtype=jnp.int32)
        edge_index = jnp.concatenate([er, jnp.stack([loops, loops])], axis=1)
        W1 = jax.random.normal(ks[2], (H * HID, IN), jnp.float32) * (2.0 / (IN + H * HID)) ** 0.5
        a1_src = jax.random.normal(ks[3], (H, HID), jnp.float32) * 0.1
        a1_dst = jax.random.normal(ks[4], (H, HID), jnp.float32) * 0.1
        W2 = jax.random.normal(ks[5], (OUT, H * HID), jnp.float32) * (2.0 / (H * HID + OUT)) ** 0.5
        a2_src = jax.random.normal(ks[6], (1, OUT), jnp.float32) * 0.1
        a2_dst = jax.random.normal(ks[7], (1, OUT), jnp.float32) * 0.1
        return {'x': x, 'edge_index': edge_index, 'W1': W1, 'a1_src': a1_src, 'a1_dst': a1_dst, 'W2': W2, 'a2_src': a2_src, 'a2_dst': a2_dst}
    _L1_gnn_all = _L1_gnn_setup()
    _L1_gnn_in = {k: v for k, v in _L1_gnn_all.items() if k in ('W1', 'a1_src', 'a1_dst', 'W2', 'a2_src', 'a2_dst')}
    del _L1_gnn_all

    def _L1_ffn_setup():
        import jax, jax.numpy as jnp
        import numpy as np
        B, N, D = (16, 512, 256)
        NUM_EXPERTS, TOP_K, HEADS = (4, 2, 4)
        N_EDGES = 131072
        LN_EPS = 1e-05

        def _layernorm(x, g, b):
            mu = x.mean(-1, keepdims=True)
            var = ((x - mu) ** 2).mean(-1, keepdims=True)
            return (x - mu) * jax.lax.rsqrt(var + LN_EPS) * g + b

        def _forward(x, edge_index, W_gat, att_src, att_dst, b_gat, ln_gamma, ln_beta, W1, b1, W2, b2):
            Bc, Nc, Dc = x.shape
            M = Bc * Nc
            x_flat = x.reshape(M, Dc)
            h = (x_flat @ W_gat).reshape(M, HEADS, NUM_EXPERTS)
            loops = jnp.arange(M, dtype=edge_index.dtype)
            src = jnp.concatenate([edge_index[0], loops])
            dst = jnp.concatenate([edge_index[1], loops])
            a_src = (h * att_src).sum(-1)
            a_dst = (h * att_dst).sum(-1)
            e = jax.nn.leaky_relu(a_src[src] + a_dst[dst], negative_slope=0.2)
            e_max = jax.ops.segment_max(e, dst, num_segments=M)
            ee = jnp.exp(e - e_max[dst])
            denom = jax.ops.segment_sum(ee, dst, num_segments=M)
            alpha = ee / (denom[dst] + 1e-16)
            msg = h[src] * alpha[:, :, None]
            agg = jax.ops.segment_sum(msg, dst, num_segments=M).reshape(M, HEADS * NUM_EXPERTS) + b_gat
            scores = _layernorm(agg, ln_gamma, ln_beta).reshape(M, HEADS, NUM_EXPERTS).mean(1)
            scores = scores.reshape(Bc, Nc, NUM_EXPERTS)
            topk_s, topk_i = jax.lax.top_k(scores, TOP_K)
            w = jax.nn.softmax(topk_s, axis=-1)
            out = jnp.zeros_like(x)
            for ei in range(NUM_EXPERTS):
                g = jnp.where(topk_i == ei, w, 0.0).sum(-1)
                hh = jax.nn.gelu(x @ W1[ei] + b1[ei], approximate=False)
                out = out + g[..., None] * (hh @ W2[ei] + b2[ei])
            return out
        key = jax.random.key(seed)
        ks = jax.random.split(key, 8)
        s = 0.05
        return {'x': jax.random.normal(ks[0], (B, N, D), jnp.float32), 'W_gat': jax.random.normal(ks[1], (D, HEADS * NUM_EXPERTS), jnp.float32) * s, 'att_src': jax.random.normal(ks[2], (HEADS, NUM_EXPERTS), jnp.float32) * s, 'att_dst': jax.random.normal(ks[3], (HEADS, NUM_EXPERTS), jnp.float32) * s, 'b_gat': jnp.zeros((HEADS * NUM_EXPERTS,), jnp.float32), 'ln_gamma': jnp.ones((HEADS * NUM_EXPERTS,), jnp.float32), 'ln_beta': jnp.zeros((HEADS * NUM_EXPERTS,), jnp.float32), 'W1': jax.random.normal(ks[4], (NUM_EXPERTS, D, 2 * D), jnp.float32) * s, 'b1': jnp.zeros((NUM_EXPERTS, 2 * D), jnp.float32), 'W2': jax.random.normal(ks[5], (NUM_EXPERTS, 2 * D, D), jnp.float32) * s, 'b2': jnp.zeros((NUM_EXPERTS, D), jnp.float32), 'edge_index': jax.random.randint(ks[6], (2, N_EDGES), 0, B * N, jnp.int32)}
    _L1_ffn_all = _L1_ffn_setup()
    _L1_ffn_in = {k: v for k, v in _L1_ffn_all.items() if k in ('W_gat', 'att_src', 'att_dst', 'b_gat', 'ln_gamma', 'ln_beta', 'W1', 'b1', 'W2', 'b2', 'edge_index')}
    del _L1_ffn_all
    return {'x': x, 'src': src, 'dst': dst, 'L0_gnn_fc1_w': _L0_gnn_in['fc1_w'], 'L0_gnn_attn_l1': _L0_gnn_in['attn_l1'], 'L0_gnn_attn_r1': _L0_gnn_in['attn_r1'], 'L0_gnn_bias1': _L0_gnn_in['bias1'], 'L0_gnn_fc2_w': _L0_gnn_in['fc2_w'], 'L0_gnn_attn_l2': _L0_gnn_in['attn_l2'], 'L0_gnn_attn_r2': _L0_gnn_in['attn_r2'], 'L0_gnn_bias2': _L0_gnn_in['bias2'], 'L0_gnn_wb0': _L0_gnn_in['wb0'], 'L0_gnn_bb0': _L0_gnn_in['bb0'], 'L0_gnn_wb1': _L0_gnn_in['wb1'], 'L0_gnn_bb1': _L0_gnn_in['bb1'], 'L0_ffn_gate_w': _L0_ffn_in['gate_w'], 'L0_ffn_gate_b': _L0_ffn_in['gate_b'], 'L0_ffn_w1': _L0_ffn_in['w1'], 'L0_ffn_b1': _L0_ffn_in['b1'], 'L0_ffn_w2': _L0_ffn_in['w2'], 'L0_ffn_b2': _L0_ffn_in['b2'], 'L1_gnn_W1': _L1_gnn_in['W1'], 'L1_gnn_a1_src': _L1_gnn_in['a1_src'], 'L1_gnn_a1_dst': _L1_gnn_in['a1_dst'], 'L1_gnn_W2': _L1_gnn_in['W2'], 'L1_gnn_a2_src': _L1_gnn_in['a2_src'], 'L1_gnn_a2_dst': _L1_gnn_in['a2_dst'], 'L1_ffn_W_gat': _L1_ffn_in['W_gat'], 'L1_ffn_att_src': _L1_ffn_in['att_src'], 'L1_ffn_att_dst': _L1_ffn_in['att_dst'], 'L1_ffn_b_gat': _L1_ffn_in['b_gat'], 'L1_ffn_ln_gamma': _L1_ffn_in['ln_gamma'], 'L1_ffn_ln_beta': _L1_ffn_in['ln_beta'], 'L1_ffn_W1': _L1_ffn_in['W1'], 'L1_ffn_b1': _L1_ffn_in['b1'], 'L1_ffn_W2': _L1_ffn_in['W2'], 'L1_ffn_b2': _L1_ffn_in['b2'], 'L1_ffn_edge_index': _L1_ffn_in['edge_index']}

def reference(x, src, dst, L0_gnn_fc1_w, L0_gnn_attn_l1, L0_gnn_attn_r1, L0_gnn_bias1, L0_gnn_fc2_w, L0_gnn_attn_l2, L0_gnn_attn_r2, L0_gnn_bias2, L0_gnn_wb0, L0_gnn_bb0, L0_gnn_wb1, L0_gnn_bb1, L0_ffn_gate_w, L0_ffn_gate_b, L0_ffn_w1, L0_ffn_b1, L0_ffn_w2, L0_ffn_b2, L1_gnn_W1, L1_gnn_a1_src, L1_gnn_a1_dst, L1_gnn_W2, L1_gnn_a2_src, L1_gnn_a2_dst, L1_ffn_W_gat, L1_ffn_att_src, L1_ffn_att_dst, L1_ffn_b_gat, L1_ffn_ln_gamma, L1_ffn_ln_beta, L1_ffn_W1, L1_ffn_b1, L1_ffn_W2, L1_ffn_b2, L1_ffn_edge_index):
    import jax
    import jax.numpy as jnp

    def _L0_gnn_ref(inputs, src, dst, fc1_w, attn_l1, attn_r1, bias1, fc2_w, attn_l2, attn_r2, bias2, wb0, bb0, wb1, bb1):
        import jax, jax.numpy as jnp
        import numpy as np
        N = 2500
        E = 40000
        IN = 256
        HID = 256
        OUT = 256
        H1 = 8
        D1 = HID // H1
        H2 = 1

        def gat_conv(h, src, dst, fc_w, attn_l, attn_r, bias, heads, out_feats):
            n = h.shape[0]
            feat = (h @ fc_w.T).reshape(n, heads, out_feats)
            el = jnp.sum(feat * attn_l, axis=-1)
            er = jnp.sum(feat * attn_r, axis=-1)
            e = jax.nn.leaky_relu(el[src] + er[dst], 0.2)
            m = jax.ops.segment_max(e, dst, num_segments=n)
            m = jnp.where(jnp.isfinite(m), m, 0.0)
            ex = jnp.exp(e - m[dst])
            ssum = jax.ops.segment_sum(ex, dst, num_segments=n)
            a = ex / ssum[dst]
            rst = jax.ops.segment_sum(feat[src] * a[..., None], dst, num_segments=n)
            return rst + bias.reshape(heads, out_feats)
        n = inputs.shape[0]
        deg = jax.ops.segment_sum(jnp.ones_like(dst, jnp.float32), dst, num_segments=n)
        norm = (1.0 / jnp.clip(deg, 1.0, None))[:, None]
        h0 = gat_conv(inputs, src, dst, fc1_w, attn_l1, attn_r1, bias1, H1, D1)
        h0 = h0.reshape(n, H1 * D1)
        h1 = jax.nn.relu(h0 + norm * (inputs @ wb0.T + bb0))
        h2 = gat_conv(h1, src, dst, fc2_w, attn_l2, attn_r2, bias2, H2, OUT)
        h2 = h2.mean(axis=1)
        cat = jnp.concatenate([inputs, h1], axis=-1)
        return h2 + norm * (cat @ wb1.T + bb1)

    def _L0_ffn_ref(h, gate_w, gate_b, w1, b1, w2, b2):
        import math
        import jax, jax.numpy as jnp
        import numpy as np
        CAPACITY_FACTOR = 1.25
        B, L, D = h.shape
        E = gate_w.shape[1]
        T = B * L
        C = max(1, math.ceil(CAPACITY_FACTOR * T / E))
        x = h.reshape(T, D)
        logits = x @ gate_w + gate_b
        probs = jax.nn.softmax(logits, axis=-1)
        idx = jnp.argmax(probs, axis=-1)
        prb = jnp.take_along_axis(probs, idx[:, None], axis=1)[:, 0]
        one_hot = jax.nn.one_hot(idx, E, dtype=jnp.float32)
        pos = (jnp.cumsum(one_hot, axis=0) * one_hot).sum(-1).astype(jnp.int32) - 1
        kept = pos < C
        pos_safe = jnp.where(kept, pos, C)
        buf = jnp.zeros((E, C, D), dtype=h.dtype).at[idx, pos_safe].set(x, mode='drop')
        hmid = jax.nn.relu(jnp.einsum('ecd,edf->ecf', buf, w1) + b1[:, None, :])
        ybuf = jnp.einsum('ecf,efd->ecd', hmid, w2) + b2[:, None, :]
        pos_g = jnp.minimum(pos, C - 1)
        y_tok = ybuf[idx, pos_g] * (prb * kept)[:, None]
        y = y_tok.reshape(B, L, D)
        y = jnp.nan_to_num(y, nan=0.0, posinf=10000.0, neginf=-10000.0)
        return y

    def _L1_gnn_ref(x, edge_index, W1, a1_src, a1_dst, W2, a2_src, a2_dst):
        import jax, jax.numpy as jnp
        import numpy as np
        N = 6250
        E_RAND = 100000
        IN, HID, H, OUT = (256, 64, 4, 256)
        NEG_SLOPE = 0.2

        def gat_layer(h, W, a_src, a_dst, src, dst, concat):
            n = h.shape[0]
            nh, nf = a_src.shape
            hp = (h @ W.T).reshape(n, nh, nf)
            e = (hp[src] * a_src).sum(-1) + (hp[dst] * a_dst).sum(-1)
            e = jnp.where(e > 0, e, NEG_SLOPE * e)
            e_max = jax.ops.segment_max(e, dst, num_segments=n)
            ex = jnp.exp(e - e_max[dst])
            e_sum = jax.ops.segment_sum(ex, dst, num_segments=n)
            alpha = ex / (e_sum[dst] + 1e-16)
            out = jax.ops.segment_sum(hp[src] * alpha[..., None], dst, num_segments=n)
            return out.reshape(n, nh * nf) if concat else out.mean(axis=1)
        src, dst = (edge_index[0], edge_index[1])
        h = jax.nn.relu(gat_layer(x, W1, a1_src, a1_dst, src, dst, True))
        return gat_layer(h, W2, a2_src, a2_dst, src, dst, False)

    def _L1_ffn_ref(x, W_gat, att_src, att_dst, b_gat, ln_gamma, ln_beta, W1, b1, W2, b2, edge_index):
        import jax, jax.numpy as jnp
        import numpy as np
        B, N, D = (16, 512, 256)
        NUM_EXPERTS, TOP_K, HEADS = (4, 2, 4)
        N_EDGES = 131072
        LN_EPS = 1e-05

        def _layernorm(x, g, b):
            mu = x.mean(-1, keepdims=True)
            var = ((x - mu) ** 2).mean(-1, keepdims=True)
            return (x - mu) * jax.lax.rsqrt(var + LN_EPS) * g + b

        def _forward(x, edge_index, W_gat, att_src, att_dst, b_gat, ln_gamma, ln_beta, W1, b1, W2, b2):
            Bc, Nc, Dc = x.shape
            M = Bc * Nc
            x_flat = x.reshape(M, Dc)
            h = (x_flat @ W_gat).reshape(M, HEADS, NUM_EXPERTS)
            loops = jnp.arange(M, dtype=edge_index.dtype)
            src = jnp.concatenate([edge_index[0], loops])
            dst = jnp.concatenate([edge_index[1], loops])
            a_src = (h * att_src).sum(-1)
            a_dst = (h * att_dst).sum(-1)
            e = jax.nn.leaky_relu(a_src[src] + a_dst[dst], negative_slope=0.2)
            e_max = jax.ops.segment_max(e, dst, num_segments=M)
            ee = jnp.exp(e - e_max[dst])
            denom = jax.ops.segment_sum(ee, dst, num_segments=M)
            alpha = ee / (denom[dst] + 1e-16)
            msg = h[src] * alpha[:, :, None]
            agg = jax.ops.segment_sum(msg, dst, num_segments=M).reshape(M, HEADS * NUM_EXPERTS) + b_gat
            scores = _layernorm(agg, ln_gamma, ln_beta).reshape(M, HEADS, NUM_EXPERTS).mean(1)
            scores = scores.reshape(Bc, Nc, NUM_EXPERTS)
            topk_s, topk_i = jax.lax.top_k(scores, TOP_K)
            w = jax.nn.softmax(topk_s, axis=-1)
            out = jnp.zeros_like(x)
            for ei in range(NUM_EXPERTS):
                g = jnp.where(topk_i == ei, w, 0.0).sum(-1)
                hh = jax.nn.gelu(x @ W1[ei] + b1[ei], approximate=False)
                out = out + g[..., None] * (hh @ W2[ei] + b2[ei])
            return out
        return _forward(x, edge_index, W_gat, att_src, att_dst, b_gat, ln_gamma, ln_beta, W1, b1, W2, b2)
    edge_index = jnp.stack([src, dst])
    x = x + _L0_gnn_ref(_layernorm(x, axis=-1), src, dst, L0_gnn_fc1_w, L0_gnn_attn_l1, L0_gnn_attn_r1, L0_gnn_bias1, L0_gnn_fc2_w, L0_gnn_attn_l2, L0_gnn_attn_r2, L0_gnn_bias2, L0_gnn_wb0, L0_gnn_bb0, L0_gnn_wb1, L0_gnn_bb1)
    x = x + _L0_ffn_ref(_layernorm(x, axis=-1)[None], L0_ffn_gate_w, L0_ffn_gate_b, L0_ffn_w1, L0_ffn_b1, L0_ffn_w2, L0_ffn_b2)[0]
    x = x + _L1_gnn_ref(_layernorm(x, axis=-1), edge_index, L1_gnn_W1, L1_gnn_a1_src, L1_gnn_a1_dst, L1_gnn_W2, L1_gnn_a2_src, L1_gnn_a2_dst)
    x = x + _L1_ffn_ref(_layernorm(x, axis=-1)[None], L1_ffn_W_gat, L1_ffn_att_src, L1_ffn_att_dst, L1_ffn_b_gat, L1_ffn_ln_gamma, L1_ffn_ln_beta, L1_ffn_W1, L1_ffn_b1, L1_ffn_W2, L1_ffn_b2, L1_ffn_edge_index)[0]
    return x

_drawn_inputs = setup_inputs


def setup_inputs(seed=0):
    import zlib

    import numpy as np

    out = dict(_drawn_inputs(seed))
    spreads = {'L0_ffn_gate_b': (0.0, 0.1),
     'L0_ffn_b1': (0.0, 0.434),
     'L0_ffn_b2': (0.0, 0.323),
     'L1_ffn_b_gat': (0.0, 0.1),
     'L1_ffn_ln_gamma': (1.0, 0.2),
     'L1_ffn_ln_beta': (0.0, 0.1),
     'L1_ffn_b1': (0.0, 0.1),
     'L1_ffn_b2': (0.0, 0.1)}
    factors = {'L0_gnn_attn_r1': 86.956,
     'L0_gnn_attn_l2': 6.414,
     'L0_gnn_attn_r2': 86.446,
     'L0_gnn_wb0': 3.167,
     'L0_gnn_bb0': 4.949,
     'L0_gnn_bb1': 4.975,
     'L1_gnn_a1_dst': 29.54,
     'L1_gnn_a2_src': 5.058,
     'L1_gnn_a2_dst': 7.739,
     'L1_ffn_att_dst': 9.816}
    for name, (base, spread) in spreads.items():
        noise = np.random.default_rng([zlib.crc32(name.encode()), seed]).standard_normal(out[name].shape)
        drawn = base * np.exp(spread * noise) if base else spread * noise
        out[name] = jnp.asarray(drawn.astype(out[name].dtype))
    for name, factor in factors.items():
        out[name] = (out[name] * factor).astype(out[name].dtype)
    return out
```

```python
from contextlib import ExitStack

import numpy as np

import concourse.bass as bass
from concourse import mybir
from concourse.alu_op_type import AluOpType as ALU

F32 = mybir.dt.float32
I32 = mybir.dt.int32
ACT = mybir.ActivationFunctionType
AX = mybir.AxisListType.X
RED = bass.bass_isa.ReduceOp
DVE = mybir.EngineType.DVE
PE = mybir.EngineType.PE

P = 128
N = 6250
D = 256
T = (N + P - 1) // P
NPAD = T * P
LAST = N - (T - 1) * P
E = 100000
ROWS = (E + P - 1) // P
G = 8
R = 4
PAIRS = ROWS + T - 1
NG = -(-PAIRS // (G * R)) * R
Q = 7
assert Q * P >= (NG + 2) * G
TURNS = NG // R
BIG = 3.0e38
LN_EPS = 1e-5
E2 = 131072
ROWS2 = E2 // P
N2MAX = 8192

EXPERTS = 8
CAP = 977
CPAD = 1024
SLOTS = EXPERTS * CPAD
FF = 1024
EXPERTS2 = 4
FF2 = 512
HEADS2 = 4


class Steps:

    def __init__(self, eng, sem):
        self.eng, self.sem, self.n, self.base = eng, sem, 0, 0

    def __call__(self, ins):
        ins.then_inc(self.sem, 1)
        self.n += 1

    def point(self):
        return self.sem, self.base + self.n

    def wait(self):
        self.eng.wait_ge(*self.point())

    def turn(self, i, before, period):
        self.base, self.n = i * period + before, 0

    def leave(self, turns, before, period):
        self.base, self.n = 0, before + turns * period


def loop(eng, turns, body, *steps):
    before = [s.n for s in steps]
    body(0)
    periods = [s.n - b for s, b in zip(steps, before)]
    if turns > 1:
        with eng.Fori(1, turns) as i:
            for s, b, p in zip(steps, before, periods):
                s.turn(i, b, p)
            body(i)
    for s, b, p in zip(steps, before, periods):
        s.leave(turns, b, p)


def early(t):
    return isinstance(t, int) and t < 2


def tiles(body, eng):
    body(0, 0, 0)
    body(1, 1, 0)
    with eng.Fori(1, T // 2) as i:
        body(i * 2, 0, i)
        body(i * 2 + 1, 1, i)
    body(T - 1, 0, T // 2)


def place_rows(v, h, t, dst, s_rows, s_turned):
    if not early(t):
        v.wait_ge(s_turned, t - 1)
    v.tensor_copy(dst, h[:, at(t), :].rearrange("p a f -> p (a f)")).then_inc(s_rows, 1)


def at(i, n=1):
    return bass.ds(i, n)


class Chip:

    def __init__(self, nc, ctx):
        self.nc, self.ctx = nc, ctx
        self.sems = ctx.enter_context(ExitStack())
        self.lowest = self.next = min(nc.free_semaphores)
        self.highest = max(nc.free_semaphores)
        self.held = self.dma_sem("held")

    def sb(self, name, shape, dt=F32, ctx=None):
        return (ctx or self.ctx).enter_context(self.nc.sbuf_tensor(name, list(shape), dt))

    def ps(self, name, shape, ctx, dt=F32):
        return ctx.enter_context(self.nc.psum_tensor(name, list(shape), dt))

    def sem(self, name):
        self.next += 1
        return self.sems.enter_context(self.nc.semaphore(name, self.next - 1))

    def dma_sem(self, name):
        self.highest -= 1
        return self.ctx.enter_context(self.nc.semaphore(name, self.highest + 1))

    def hold(self, eng, sem, value):
        eng.wait_ge(sem, value)
        eng.sem_inc(self.held, 1)

    def renew(self):
        self.sems.close()
        used, self.next = range(self.lowest, self.next), self.lowest
        with self.nc.Block() as block:

            @block.gpsimd
            def _(pool):
                pool.sem_clear(used)


def prep(c, x_in, src_in, dst_in, K, X, slot_rows, ids_dram):
    nc = c.nc
    s_const, s_load, s_dve, s_cnt = c.sem("p_const"), c.sem("p_load"), c.sem("p_dve"), c.sem("p_cnt")
    s_rows, s_gath, s_turned = c.sem("p_rows"), c.dma_sem("p_gath"), c.sem("p_turned")
    s_ids, s_idsio, s_zero, s_zout = c.sem("p_ids"), c.sem("p_idsio"), c.sem("p_zero"), c.sem("p_zout")
    s_thr, s_pool, s_x = c.sem("p_thr"), c.sem("p_pool"), c.sem("p_x")
    mark = {}
    with ExitStack() as ctx:
        sb = lambda n, sh, dt=F32: c.sb(n, sh, dt, ctx)
        iota_i, part_i, k_i = sb("iota_i", [P, P], I32), sb("part_i", [P, 1], I32), sb("k_i", [P, Q], I32)
        thr_i, thr = sb("thr_i", [P, T + 1], I32), sb("thr", [P, T + 1])
        dst_i, dst_f, junk = sb("dst_i", [P, ROWS], I32), sb("dst_f", [P, ROWS]), sb("junk", [P, ROWS])
        cnt, start = sb("cnt", [P, T + 1]), sb("start", [P, T + 1])
        first_i, last_i = sb("first_i", [P, T], I32), sb("last_i", [P, T], I32)
        first, last, some, num = sb("first", [P, T]), sb("last", [P, T]), sb("some", [P, T]), sb("num", [P, T])
        cum, shift = sb("cum", [P, T]), sb("shift", [P, T])
        kf, tk, dk, row_f = sb("kf", [P, Q]), sb("tk", [P, Q]), sb("dk", [P, Q]), sb("row_f", [P, Q])
        row_i, base, tid = sb("row_i", [P, Q], I32), sb("base", [P, Q]), sb("tid", [P, Q])
        rows_s, rows_d = sb("rows_s", [P, Q, P], I32), sb("rows_d", [P, Q, P], I32)
        loc_s, loc_d = sb("loc_s", [P, Q, P]), sb("loc_d", [P, Q, P])
        ids_i, zero = sb("ids_i", [Q, P], I32), sb("zero", [P, 2048])
        ps_cnt, ps_ids = c.ps("ps_cnt", [P, 512], ctx), c.ps("ps_ids", [P, 512], ctx)
        ps_s, ps_d = c.ps("ps_s", [P, 2, 512], ctx), c.ps("ps_d", [P, 2, 512], ctx)
        with nc.Block() as block:

            @block.gpsimd
            def _(pool):
                pool.iota(iota_i[:], [[1, P]], base=0, channel_multiplier=0).then_inc(s_pool, 1)
                pool.iota(part_i[:], [[0, 1]], base=0, channel_multiplier=1).then_inc(s_pool, 1)
                pool.iota(k_i[:], [[P, Q]], base=0, channel_multiplier=1).then_inc(s_pool, 1)
                pool.iota(thr_i[:], [[P, T + 1]], base=0, channel_multiplier=0).then_inc(s_pool, 1)
                pool.memset(K.ident[:], 0.0).then_inc(s_zero, 1)
                pool.memset(K.ones[:], 1.0).then_inc(s_zero, 1)
                pool.memset(zero[:], 0.0).then_inc(s_zero, 1)
                pool.memset(X[:, T - 1, :], 0.0).then_inc(s_zero, 1)
                pool.wait_ge(s_zero, 4)
                pool.affine_select(out=K.ident[:], in_=K.ident[:], compare_op=ALU.not_equal, fill=1.0, base=0,
                                   pattern=[[-1, P]], channel_multiplier=1).then_inc(s_const, 1)
                pool.affine_select(out=K.upto[:], in_=K.ones[:], compare_op=ALU.is_ge, fill=0.0, base=0,
                                   pattern=[[1, P]], channel_multiplier=-1).then_inc(s_const, 1)
                pool.wait_ge(s_rows, 1)
                for q in range(Q):
                    for rows, edges in ((rows_s, src_in), (rows_d, dst_in)):
                        pool.indirect_dma_start(
                            out=rows[:, q, :], out_offset=None, in_=edges,
                            in_offset=bass.IndirectOffsetOnAxis(ap=row_i[:, q:q + 1], axis=0)).then_inc(s_gath, 16)

            @block.sync
            def _(sp):
                sp.dma_start(dst_i[:], dst_in.rearrange("r e -> (r e)").rearrange("(p j) -> p j", p=P)) \
                    .then_inc(s_load, 16)
                sp.dma_start(X[:, 0:T - 1, :], x_in[0:(T - 1) * P, :].rearrange("(t p) d -> p t d", p=P)).then_inc(s_x, 16)
                sp.wait_ge(s_zero, 4)
                sp.dma_start(X[0:LAST, T - 1, :], x_in[(T - 1) * P:N, :]).then_inc(s_x, 16)
                for n in range(SLOTS // 1024):
                    sp.dma_start(slot_rows[n * 1024:(n + 1) * 1024, :].rearrange("(p a) d -> p (a d)", p=P),
                                 zero[:]).then_inc(s_zout, 16)
                sp.wait_ge(s_ids, 1)
                sp.dma_start(ids_dram, ids_i[:]).then_inc(s_idsio, 16)
                sp.wait_ge(s_idsio, 16)
                sp.dma_start(K.ids[:], ids_dram.rearrange("q k -> (q k)").rearrange("(a k) -> a k", a=1)) \
                    .then_inc(s_idsio, 16)
                sp.wait_ge(s_idsio, 32)
                sp.wait_ge(s_x, 32)
                sp.wait_ge(s_zout, 16 * (SLOTS // 1024))

            @block.vector
            def _(v):
                st = Steps(v, s_dve)
                v.wait_ge(s_pool, 4)
                st(v.tensor_copy(K.iota[:], iota_i[:]))
                st(v.tensor_copy(K.part[:], part_i[:]))
                st(v.tensor_scalar(K.iota_low[:], iota_i[:], float(-P), None, ALU.add))
                st(v.tensor_copy(kf[:], k_i[:]))
                v.tensor_copy(thr[:], thr_i[:]).then_inc(s_thr, 1)
                v.wait_ge(s_load, 16)
                st(v.tensor_copy(dst_f[:], dst_i[:]))
                st.wait()
                v.wait_ge(s_thr, 1)

                def count(t):
                    st(v.tensor_scalar(junk[:], dst_f[:], thr[:, at(t)], 0.0, ALU.is_lt, ALU.add,
                                       accum_out=cnt[:, at(t)]))
                    st.wait()
                loop(v, T + 1, count, st)
                mark["counted"] = st.n
                v.wait_ge(s_cnt, 1)
                st(v.tensor_copy(start[:], ps_cnt[:, 0:T + 1]))
                st.wait()
                st(v.tensor_copy(first_i[:], start[:, 0:T]))
                st(v.tensor_scalar(last_i[:], start[:, 1:T + 1], float(P - 1), None, ALU.add))
                st(v.tensor_tensor(some[:], start[:, 1:T + 1], start[:, 0:T], ALU.is_gt))
                st.wait()
                st(v.tensor_scalar(first_i[:], first_i[:], 7, None, ALU.arith_shift_right))
                st(v.tensor_scalar(last_i[:], last_i[:], 7, None, ALU.arith_shift_right))
                st.wait()
                st(v.tensor_copy(first[:], first_i[:]))
                st(v.tensor_copy(last[:], last_i[:]))
                st.wait()
                st(v.tensor_tensor(num[:], last[:], first[:], ALU.subtract))
                st.wait()
                st(v.tensor_tensor(num[:], num[:], some[:], ALU.mult))
                st.wait()
                st(v.tensor_tensor_scan(cum[:], K.ones[:, 0:T], num[:], 0.0, ALU.mult, ALU.add))
                st.wait()
                st(v.tensor_tensor(shift[:], num[:], cum[:], ALU.subtract))
                st.wait()
                st(v.tensor_tensor(shift[:], shift[:], first[:], ALU.add))
                st.wait()
                for q in range(Q):
                    st(v.tensor_scalar(junk[:, 0:T], cum[:], kf[:, q:q + 1], 0.0, ALU.is_le, ALU.add,
                                       accum_out=tk[:, q:q + 1]))
                    st.wait()
                    st(v.scalar_tensor_tensor(junk[:, 0:T], K.iota[:, 0:T], tk[:, q:q + 1], shift[:],
                                              ALU.is_equal, ALU.mult, accum_out=dk[:, q:q + 1]))
                    st.wait()
                st(v.tensor_tensor(row_f[:], kf[:], dk[:], ALU.add))
                st(v.tensor_scalar(base[:], tk[:], float(P), None, ALU.mult))
                st(v.tensor_scalar(tid[:], tk[:], float(T - 1), None, ALU.min))
                st.wait()
                st(v.tensor_scalar(row_f[:], row_f[:], float(ROWS - 1), None, ALU.min))
                st.wait()
                v.tensor_copy(row_i[:], row_f[:]).then_inc(s_rows, 1)
                v.wait_ge(s_gath, 16 * 2 * Q)
                st(v.tensor_copy(loc_s[:], rows_s[:]))
                st(v.tensor_copy(loc_d[:], rows_d[:]))
                st.wait()
                for q in range(Q):
                    st(v.tensor_scalar(loc_d[:, q, :], loc_d[:, q, :], base[:, q:q + 1], None, ALU.subtract))
                mark["locals"] = st.n
                v.wait_ge(s_turned, 1)
                for q in range(Q):
                    st(v.tensor_copy(K.src_cols[:, q * P:(q + 1) * P], ps_s[:, q // 4, (q % 4) * P:(q % 4 + 1) * P]))
                    st(v.tensor_copy(K.dst_cols[:, q * P:(q + 1) * P], ps_d[:, q // 4, (q % 4) * P:(q % 4 + 1) * P]))
                v.tensor_copy(ids_i[:], ps_ids[0:Q, 0:P]).then_inc(s_ids, 1)

            @block.tensor
            def _(pe):
                pe.wait_ge(s_const, 2)
                pe.wait_ge(s_dve, mark["counted"])
                pe.matmul(ps_cnt[:, 0:T + 1], K.ones[:], cnt[:], start=True, stop=True).then_inc(s_cnt, 1)
                pe.wait_ge(s_dve, mark["locals"])
                for q in range(Q):
                    for ps, loc in ((ps_s, loc_s), (ps_d, loc_d)):
                        pe.transpose(ps[:, q // 4, (q % 4) * P:(q % 4 + 1) * P], loc[:, q, :], K.ident[:])
                pe.transpose(ps_ids[0:Q, 0:P], tid[:], K.ident[:]).then_inc(s_turned, 1)


class Base:

    def __init__(self, weights, bias, out):
        self.weights, self.bias, self.out, self.n = weights, bias, out, out.shape[1]


def project(c, name, K, h, w_t, w_nat, attn_dram, heads, table, base=None):
    nc = c.nc
    one = heads == 1
    width = table.shape[1]
    nb = base.n if base else 0
    sem = lambda n: c.sem(name + n)
    s_w, s_fold, s_folded, s_beside, s_hT, s_hTc = sem("w"), sem("fold"), sem("folded"), sem("beside"), sem("hT"), sem("hTc")
    s_mm, s_out, s_store, s_dve, s_max, s_aux = sem("mm"), sem("out"), [sem("store0"), sem("store1")], sem("dve"), sem("max"), sem("aux")
    s_rows = sem("rows")
    nout = 3 + (1 if one else 0) + (1 if base else 0)
    nf = D + 2 * heads
    with ExitStack() as ctx:
        sb = lambda n, sh, dt=F32: c.sb(name + n, sh, dt, ctx)
        w = sb("w", [P, 2, nf])
        wn, attn = sb("wn", [P, 2, D]), sb("attn", [P, 2, 2])
        fold, off_i, off, ge = sb("fold", [P, 2, 2, heads]), sb("off_i", [P, 2, heads], I32), sb("off", [P, 2, heads]), sb("ge", [P, 2, heads])
        rows, hT, stage = sb("rows", [P, 2, D]), sb("hT", [P, 2, D]), sb("stage", [P, 2, width])
        elv, elm, gmax = sb("elv", [P, T, heads]), sb("elm", [P, heads]), sb("gmax", [P, heads])
        vm = sb("vm", [P, 2])
        if nb:
            wb, bstage = sb("wb", [P, 2, nb]), sb("bstage", [P, 2, nb])
            bias = sb("bias", [1, nb]) if base.bias is not None else None
        ps_t = [c.ps(f"{name}pt{i}", [P, D], ctx) for i in range(2)]
        ps_f = [c.ps(f"{name}pf{i}", [P, 512], ctx) for i in range(2)]
        ps_b = [c.ps(f"{name}pb{i}", [P, 512], ctx) for i in range(2)] if nb else None
        nload = 16 * (3 + (1 if nb else 0) + (1 if nb and bias is not None else 0))
        with nc.Block() as block:

            @block.sync
            def _(sp):
                sp.dma_start(w[:, :, 0:D], w_t.rearrange("(c p) n -> p c n", p=P)).then_inc(s_w, 16)
                sp.dma_start(wn[:], w_nat.rearrange("(c p) n -> p c n", p=P)).then_inc(s_w, 16)
                sp.dma_start(attn[:], attn_dram).then_inc(s_w, 16)
                if nb:
                    sp.dma_start(wb[:], base.weights.rearrange("(c p) n -> p c n", p=P)).then_inc(s_w, 16)
                    if bias is not None:
                        sp.dma_start(bias[:], base.bias).then_inc(s_w, 16)
                per = 32 if nb else 16

                def store(t, s, i):
                    sp.wait_ge(s_out, (t + 1) * nout)
                    sp.dma_start(table[at(t * P, P), :], stage[:, s, :]).then_inc(s_store[s], 16)
                    if nb:
                        sp.dma_start(base.out[at(t * P, P), :], bstage[:, s, :]).then_inc(s_store[s], 16)
                tiles(store, sp)
                for s in range(2):
                    sp.wait_ge(s_store[s], per * ((T + 1 - s) // 2))

            @block.gpsimd
            def _(pool):
                pool.iota(off_i[:], [[P, 2], [-(D // heads), heads]], base=0, channel_multiplier=1).then_inc(s_aux, 1)
                pool.memset(stage[:], 1.0).then_inc(s_aux, 1)
                pool.wait_ge(s_max, 1)
                pool.partition_all_reduce(gmax[:], elm[:], P, RED.max).then_inc(s_max, 1)

            @block.vector
            def _(v):
                st = Steps(v, s_dve)
                v.wait_ge(s_aux, 2)
                st(v.tensor_copy(off[:], off_i[:]))
                v.wait_ge(s_w, nload)
                st.wait()
                st(v.tensor_scalar(ge[:], off[:], 0.0, None, ALU.is_ge))
                st(v.tensor_scalar(off[:], off[:], float(D // heads), None, ALU.is_lt))
                st.wait()
                st(v.tensor_tensor(ge[:], ge[:], off[:], ALU.mult))
                st.wait()
                for side in range(2):
                    ins = v.tensor_tensor(fold[:, side], ge[:], attn[:, :, side:side + 1].to_broadcast([P, 2, heads]), ALU.mult)
                    ins.then_inc(s_fold, 1)
                tiles(lambda t, s, i: place_rows(v, h, t, rows[:, s, :], s_rows, s_hT), v)
                v.wait_ge(s_out, T * nout)
                st(v.tensor_scalar(vm[:, 0:1], K.part[:], float(LAST), None, ALU.is_lt))
                st.wait()
                st(v.tensor_scalar(vm[:, 1:2], vm[:, 0:1], BIG, -BIG, ALU.mult, ALU.add))
                st.wait()
                st(v.tensor_scalar(elv[:, T - 1, :], elv[:, T - 1, :], vm[:, 0:1], vm[:, 1:2], ALU.mult, ALU.add))
                st.wait()
                v.tensor_reduce(elm[:], elv[:].rearrange("p t h -> p h t"), AX, ALU.max).then_inc(s_max, 1)
                v.wait_ge(s_max, 2)
                m = K.er[:, :, heads:2 * heads]
                st(v.tensor_tensor(m, K.er[:, :, 0:heads], gmax[:].unsqueeze(1).to_broadcast([P, T, heads]), ALU.add))
                st.wait()
                st(v.scalar_tensor_tensor(m, m, 0.2, m, ALU.mult, ALU.max))

            @block.tensor
            def _(pe):
                pe.wait_ge(s_fold, 2)
                pe.wait_ge(s_w, nload)
                for k in range(2):
                    for side in range(2):
                        for o in range(2):
                            mm = pe.matmul(ps_f[0][:, (2 * k + side) * heads:(2 * k + side + 1) * heads],
                                           wn[:, o, k * P:(k + 1) * P], fold[:, side, o, :], start=(o == 0), stop=(o == 1))
                mm.then_inc(s_folded, 1)
                pe.wait_ge(s_beside, 4)

                def tile(t, s, i):
                    pe.wait_ge(s_rows, t + 1)
                    if not early(t):
                        pe.wait_ge(s_hTc, t - 1)
                    for k in range(2):
                        mm = pe.transpose(ps_t[s][:, k * P:(k + 1) * P], rows[:, s, k * P:(k + 1) * P], K.ident[:])
                    mm.then_inc(s_hT, 1)
                    pe.wait_ge(s_hTc, t + 1)
                    if not early(t):
                        pe.wait_ge(s_out, (t - 1) * nout)
                    for k in range(2):
                        mm = pe.matmul(ps_f[s][:, 0:nf], hT[:, s, k * P:(k + 1) * P], w[:, k, :], start=(k == 0), stop=(k == 1))
                    if nb:
                        for k in range(2):
                            mm = pe.matmul(ps_b[s][:, 0:nb], hT[:, s, k * P:(k + 1) * P], wb[:, k, :], start=(k == 0), stop=(k == 1 and bias is None))
                        if bias is not None:
                            mm = pe.matmul(ps_b[s][:, 0:nb], K.ones[0:1, :], bias[:], start=False, stop=True)
                    mm.then_inc(s_mm, 1)
                tiles(tile, pe)

            @block.scalar
            def _(act):
                act.wait_ge(s_folded, 1)
                for k in range(2):
                    for side in range(2):
                        ins = act.copy(w[:, k, D + side * heads:D + (side + 1) * heads],
                                       ps_f[0][:, (2 * k + side) * heads:(2 * k + side + 1) * heads])
                        ins.then_inc(s_beside, 1)

                def tile(t, s, i):
                    act.wait_ge(s_hT, t + 1)
                    if not early(t):
                        act.wait_ge(s_mm, t - 1)
                    act.copy(hT[:, s, :], ps_t[s][:]).then_inc(s_hTc, 1)
                    act.wait_ge(s_mm, t + 1)
                    if isinstance(t, int) and t == 0:
                        act.wait_ge(s_aux, 2)
                    if not early(t):
                        act.wait_ge(s_store[s], i * (32 if nb else 16))
                    if one:
                        ins = [act.copy(stage[:, s, 0:D], ps_f[s][:, 0:D]), act.copy(stage[:, s, D + 1:D + 2], ps_f[s][:, D:D + 1])]
                    else:
                        ins = [act.copy(stage[:, s, 0:D + heads], ps_f[s][:, 0:D + heads])]
                    ins += [act.copy(elv[:, at(t), :], ps_f[s][:, D:D + heads].unsqueeze(1)),
                            act.copy(K.er[:, at(t), 0:heads], ps_f[s][:, D + heads:D + 2 * heads].unsqueeze(1))]
                    if nb:
                        ins += [act.copy(bstage[:, s, :], ps_b[s][:, 0:nb])]
                    for x in ins:
                        x.then_inc(s_out, 1)
                tiles(tile, act)


def attend(c, name, K, table, heads, acc):
    nc = c.nc
    one = heads == 1
    width = table.shape[1]
    nr = D + 1 if one else D + heads + 1
    el = D + 1 if one else D
    slot = D + heads + 1 if not one else D + 2
    sem = lambda n: c.sem(name + n)
    s_stage, s_M, s_T, s_MT, s_er, s_z, s_w = sem("stage"), sem("M"), sem("T"), sem("MT"), sem("er"), sem("z"), sem("w")
    s_sc, s_main, s_add, s_init = sem("sc"), sem("main"), sem("add"), sem("init")
    s_gat = [c.dma_sem(f"{name}gat{r}") for r in range(R)]
    s_zd = sem("zd")
    with ExitStack() as ctx:
        sb = lambda n, sh, dt=F32: c.sb(name + n, sh, dt, ctx)
        idx = sb("idx", [P, R, G], I32)
        ring = sb("ring", [P, R, G, slot])
        M, MT = sb("M", [P, 2, G, P]), sb("MT", [P, 2, G, P])
        z, wt = sb("z", [P, 2, G, heads]), sb("wt", [P, 2, G, 1])
        ps_T = [c.ps(f"{name}pT{i}", [P, 4, P], ctx) for i in range(2)]
        ps_e = [c.ps(f"{name}pe{i}", [P, G, 2 * heads], ctx) for i in range(2)]
        ps_o = [c.ps(f"{name}po{i}", [P, 512], ctx) for i in range(4)]
        first = lambda i: isinstance(i, int)
        with nc.Block() as block:

            @block.gpsimd
            def _(pool):
                def turn(i):
                    for r in range(R):
                        g = i * R + r
                        c.hold(pool, s_stage, g + 1)
                        if not first(i):
                            c.hold(pool, s_main, (g - R + 1) * G)
                        else:
                            pool.wait_ge(s_init, 1)
                        for k in range(G):
                            pool.indirect_dma_start(
                                out=ring[:, r, k, 0:width], out_offset=None, in_=table,
                                in_offset=bass.IndirectOffsetOnAxis(ap=idx[:, r, k:k + 1], axis=0)).then_inc(s_gat[r], 16)
                loop(pool, TURNS, turn)

            @block.scalar
            def _(act):
                def stage(g, r):
                    act.copy(idx[:, r, :], K.src_cols[:, at(g * G, G)]).then_inc(s_stage, 1)

                def turned(g, b):
                    for half in range(2):
                        act.wait_ge(s_T, g * 2 + half + 1)
                        act.copy(MT[:, b, 4 * half:4 * half + 4, :], ps_T[half][:]).then_inc(s_MT, 1)
                stage(0, 0)
                stage(1, 1)
                turned(0, 0)

                def turn(i):
                    for r in range(R):
                        g = i * R + r
                        r2 = (r + 2) % R
                        if not (first(i) and r < 2):
                            act.wait_ge(s_gat[r2], (i + (1 if r >= 2 else 0)) * 16 * G)
                        stage(g + 2, r2)
                        act.wait_ge(s_z, g + 1)
                        if one:
                            act.activation(wt[:, r % 2], z[:, r % 2], ACT.Exp).then_inc(s_w, 1)
                        else:
                            act.activation(ring[:, r, :, D:D + heads], z[:, r % 2], ACT.Exp).then_inc(s_w, 1)
                        turned(g + 1, (r + 1) % 2)
                loop(act, TURNS, turn)

            @block.tensor
            def _(pe):
                def turn_hots(g, b):
                    for k in range(G):
                        pe.wait_ge(s_M, g * G + k + 1)
                        if k % 4 == 0 and not (first(g) and g == 0):
                            pe.wait_ge(s_MT, g * 2 - 1 + k // 4)
                        mm = pe.transpose(ps_T[k // 4][:, k % 4, :], M[:, b, k, :], K.ident[:])
                        if k % 4 == 3:
                            mm.then_inc(s_T, 1)

                def dest_terms(g, b):
                    _, ids = nc.values_load_multi_w_load_instructions(
                        K.ids[0:1, at(g * G, G)], engines=[PE], min_val=0, max_val=T - 1,
                        skip_runtime_bounds_check_because="tile numbers are cut to T - 1")
                    if not (first(g) and g < 2):
                        pe.wait_ge(s_z, g - 1)
                    for k in range(G):
                        if k % 4 == 0:
                            pe.wait_ge(s_MT, g * 2 + k // 4 + 1)
                        mm = pe.matmul(ps_e[b][:, k, :], MT[:, b, k, :],
                                       K.er[:, at(ids[k]), 0:2 * heads].rearrange("p a h -> p (a h)"), start=True, stop=True)
                    mm.then_inc(s_er, 1)
                turn_hots(0, 0)
                dest_terms(0, 0)

                def turn(i):
                    for r in range(R):
                        g = i * R + r
                        turn_hots(g + 1, (r + 1) % 2)
                        dest_terms(g + 1, (r + 1) % 2)
                        for k in range(G):
                            if k % 4 == 0:
                                pe.wait_ge(s_sc, g * 2 + k // 4 + 1)
                            if not (first(i) and r == 0 and k < 4):
                                pe.wait_ge(s_add, g * G + k - 3)
                            pe.matmul(ps_o[k % 4][:, 0:nr], M[:, r % 2, k, :], ring[:, r, k, 0:nr],
                                      start=True, stop=True).then_inc(s_main, 1)
                loop(pe, TURNS, turn)

            @block.vector
            def _(v):
                st = Steps(v, s_zd)
                v.memset(ring[:], 1.0).then_inc(s_init, 1)
                st(v.memset(acc[:], 0.0))

                def hot(g, b, k):
                    v.tensor_scalar(M[:, b, k, :], K.iota[:], K.dst_cols[:, at(g * G + k)], None, ALU.is_equal).then_inc(s_M, 1)

                def load_ids(g):
                    return nc.values_load_multi_w_load_instructions(
                        K.ids[0:1, at(g * G, G)], engines=[DVE], min_val=0, max_val=T - 1,
                        skip_runtime_bounds_check_because="tile numbers are cut to T - 1")[1]

                def add(g, k, tid):
                    v.wait_ge(s_main, g * G + k + 1)
                    if not (first(g) and g == 0 and k == 0):
                        v.wait_ge(s_add, g * G + k)
                    a = acc[:, at(tid), 0:nr].rearrange("p a f -> p (a f)")
                    v.tensor_tensor(a, a, ps_o[k % 4][:, 0:nr], ALU.add).then_inc(s_add, 1)

                for k in range(G):
                    hot(0, 0, k)

                def turn(i):
                    for r in range(R):
                        g, b = i * R + r, r % 2
                        v.wait_ge(s_gat[r], (i + 1) * 16 * G)
                        v.wait_ge(s_er, g + 1)
                        if not (first(i) and r == 0):
                            ids = load_ids(g - 1)
                        zb = z[:, b]
                        st(v.tensor_tensor(zb, ring[:, r, :, el:el + heads], ps_e[b][:, :, 0:heads], ALU.add))
                        st.wait()
                        st(v.scalar_tensor_tensor(zb, zb, 0.2, zb, ALU.mult, ALU.max))
                        st.wait()
                        v.tensor_tensor(zb, zb, ps_e[b][:, :, heads:2 * heads], ALU.subtract).then_inc(s_z, 1)
                        for k in range(G):
                            if not (first(i) and r == 0):
                                add(g - 1, k, ids[k])
                            hot(g + 1, 1 - b, k)
                        v.wait_ge(s_w, g + 1)
                        for half in range(2):
                            hs = slice(4 * half, 4 * half + 4)
                            if one:
                                v.tensor_tensor(M[:, b, hs, :], M[:, b, hs, :], wt[:, b, hs, :].to_broadcast([P, 4, P]),
                                                ALU.mult).then_inc(s_sc, 1)
                            else:
                                f = ring[:, r, hs, 0:D].rearrange("p k (h f) -> p k h f", h=heads)
                                v.tensor_tensor(f, f, ring[:, r, hs, D:D + heads].unsqueeze(3).to_broadcast([P, 4, heads, D // heads]),
                                                ALU.mult).then_inc(s_sc, 1)
                st.wait()
                loop(v, TURNS, turn, st)
                ids = load_ids(NG - 1)
                for k in range(G):
                    add(NG - 1, k, ids[k])


def combine(c, name, K, acc, heads, out, bias=None, bases=(), residual=False, relu=False, degree=False):
    nc = c.nc
    C = 7
    sem = lambda n: c.sem(name + n)
    s_bias, s_dve, s_load = sem("bias"), sem("dve"), [sem("load0"), sem("load1")]
    per = {}
    with ExitStack() as ctx:
        sb = lambda n, sh, dt=F32: c.sb(name + n, sh, dt, ctx)
        rs = sb("rs", [P, T, heads])
        brow = sb("brow", [P, D]) if bias is not None else None
        ld = sb("ld", [P, 2, len(bases), C, D]) if bases else None
        with nc.Block() as block:

            @block.vector
            def _(v):
                st = Steps(v, s_dve)
                st(v.tensor_scalar(rs[:], acc[:, :, D:D + heads], 1e-37, None, ALU.max))
                if degree:
                    st(v.tensor_scalar(K.norm[:], acc[:, :, D + heads], 1.0, None, ALU.max))
                st.wait()
                st(v.reciprocal(rs[:], rs[:]))
                if degree:
                    st(v.reciprocal(K.norm[:], K.norm[:]))
                if bias is not None:
                    v.wait_ge(s_bias, 16)
                st.wait()
                per["before"] = st.n

                def seven(i, s):
                    y = acc[:, at(i * C, C), 0:D]
                    yh = y.rearrange("p t (h f) -> p t h f", h=heads)
                    st(v.tensor_tensor(yh, yh, rs[:, at(i * C, C), :].unsqueeze(3).to_broadcast([P, C, heads, D // heads]), ALU.mult))
                    st.wait()
                    if bias is not None:
                        st(v.tensor_tensor(y, y, brow[:].unsqueeze(1).to_broadcast([P, C, D]), ALU.add))
                    if bases:
                        v.wait_ge(s_load[s], (i // 2 + 1) * 16 * len(bases))
                        b = ld[:, s, 0]
                        if len(bases) > 1:
                            st(v.tensor_tensor(b, b, ld[:, s, 1], ALU.add))
                            st.wait()
                        st(v.tensor_tensor(b, b, K.norm[:, at(i * C, C)].unsqueeze(2).to_broadcast([P, C, D]), ALU.mult))
                        st.wait()
                        st(v.tensor_tensor(y, y, b, ALU.add))
                    st.wait()
                    o = out[:, at(i * C, C), :]
                    if relu:
                        st(v.tensor_scalar(o, y, 0.0, None, ALU.max))
                    elif residual:
                        st(v.tensor_tensor(o, o, y, ALU.add))
                    st.wait()
                for i in range(T // C):
                    seven(i, i % 2)
                    per.setdefault("period", st.n - per["before"])
            if bias is not None or bases:
                @block.sync
                def _(sp):
                    if bias is not None:
                        sp.dma_start(brow[:], bias.partition_broadcast(P)).then_inc(s_bias, 16)
                    for i in range(T // C) if bases else ():
                        if i >= 2:
                            sp.wait_ge(s_dve, per["before"] + (i - 1) * per["period"])
                        for n, b in enumerate(bases):
                            sp.dma_start(ld[:, i % 2, n], b[i * C * P:(i + 1) * C * P, :].rearrange("(t p) d -> p t d", p=P)) \
                                .then_inc(s_load[i % 2], 16)
                    if bias is not None:
                        sp.wait_ge(s_bias, 16)


def layernorm(c, name, X, H):
    nc = c.nc
    s_dve, s_sqrt = c.sem(name + "dve"), c.sem(name + "sqrt")
    mark = {}
    with ExitStack() as ctx:
        stats = c.sb(name + "stats", [P, T, 6], F32, ctx)
        mean, m2, rstd = (c.sb(name + x, [P, T], F32, ctx) for x in ("mean", "m2", "rstd"))
        with nc.Block() as block:

            @block.vector
            def _(v):
                st = Steps(v, s_dve)
                rows = lambda A, t: A[:, at(t), :].rearrange("p a f -> p (a f)")
                loop(v, T, lambda t: st(v.bn_stats(rows(stats, t), rows(X, t))), st)
                st.wait()
                st(v.tensor_tensor(mean[:], stats[:, :, 1], stats[:, :, 4], ALU.add))
                st(v.tensor_tensor(rstd[:], stats[:, :, 1], stats[:, :, 4], ALU.subtract))
                st(v.tensor_tensor(m2[:], stats[:, :, 2], stats[:, :, 5], ALU.add))
                st.wait()
                st(v.tensor_scalar(mean[:], mean[:], 0.5, None, ALU.mult))
                st(v.tensor_tensor(rstd[:], rstd[:], rstd[:], ALU.mult))
                st(v.tensor_scalar(m2[:], m2[:], 1.0 / D, LN_EPS, ALU.mult, ALU.add))
                st.wait()
                st(v.scalar_tensor_tensor(rstd[:], rstd[:], 0.25, m2[:], ALU.mult, ALU.add))
                mark["var"] = st.n
                v.wait_ge(s_sqrt, 1)
                st(v.reciprocal(rstd[:], rstd[:]))
                st.wait()

                def scale(t):
                    st(v.tensor_scalar(rows(H, t), rows(X, t), mean[:, at(t)], rstd[:, at(t)], ALU.subtract, ALU.mult))
                loop(v, T, scale, st)
                st.wait()

            @block.scalar
            def _(act):
                act.wait_ge(s_dve, mark["var"])
                act.activation(rstd[:], rstd[:], ACT.Sqrt).then_inc(s_sqrt, 1)


def narrow(c, name, K, h, weights, out):
    nc = c.nc
    n = weights.shape[1]
    s_w, s_hT, s_hTc, s_mm, s_out, s_rows = (c.sem(name + x) for x in ("w", "hT", "hTc", "mm", "out", "rows"))
    with ExitStack() as ctx:
        w, hT = c.sb(name + "w", [P, 2, n], F32, ctx), c.sb(name + "hT", [P, 2, D], F32, ctx)
        rows = c.sb(name + "rows", [P, 2, D], F32, ctx)
        ps_t = [c.ps(f"{name}pt{i}", [P, D], ctx) for i in range(2)]
        ps_f = [c.ps(f"{name}pf{i}", [P, n], ctx) for i in range(2)]
        with nc.Block() as block:

            @block.sync
            def _(sp):
                sp.dma_start(w[:], weights.rearrange("(c p) n -> p c n", p=P)).then_inc(s_w, 16)
                sp.wait_ge(s_w, 16)

            @block.vector
            def _(v):
                tiles(lambda t, s, i: place_rows(v, h, t, rows[:, s, :], s_rows, s_hT), v)

            @block.tensor
            def _(pe):
                pe.wait_ge(s_w, 16)

                def tile(t, s, i):
                    pe.wait_ge(s_rows, t + 1)
                    if not early(t):
                        pe.wait_ge(s_hTc, t - 1)
                    for k in range(2):
                        mm = pe.transpose(ps_t[s][:, k * P:(k + 1) * P], rows[:, s, k * P:(k + 1) * P], K.ident[:])
                    mm.then_inc(s_hT, 1)
                    pe.wait_ge(s_hTc, t + 1)
                    if not early(t):
                        pe.wait_ge(s_out, t - 1)
                    for k in range(2):
                        mm = pe.matmul(ps_f[s][:], hT[:, s, k * P:(k + 1) * P], w[:, k, :], start=(k == 0), stop=(k == 1))
                    mm.then_inc(s_mm, 1)
                tiles(tile, pe)

            @block.scalar
            def _(act):
                def tile(t, s, i):
                    act.wait_ge(s_hT, t + 1)
                    if not early(t):
                        act.wait_ge(s_mm, t - 1)
                    act.copy(hT[:, s, :], ps_t[s][:]).then_inc(s_hTc, 1)
                    act.wait_ge(s_mm, t + 1)
                    act.copy(out[:, at(t), :], ps_f[s][:].unsqueeze(1)).then_inc(s_out, 1)
                tiles(tile, act)


def first_of_best(v, st, K, val, n, best, eq, low):
    v_b = lambda a: a.unsqueeze(2).to_broadcast([P, T, n])
    io = K.iota_low[:, P - n:P].unsqueeze(1).to_broadcast([P, T, n])
    st(v.tensor_reduce(best, val, AX, ALU.max))
    st.wait()
    st(v.tensor_tensor(eq, val, v_b(best), ALU.is_equal))
    st.wait()
    st(v.tensor_tensor(eq, eq, io, ALU.mult))
    st.wait()
    st(v.tensor_reduce(low, eq, AX, ALU.min))
    st.wait()
    st(v.tensor_tensor(eq, io, v_b(low), ALU.is_equal))
    st.wait()


def route(c, K, lg, gate_b, H, slot_rows):
    nc = c.nc
    n = EXPERTS
    C = 7
    s_b, s_dve, s_exp, s_cum, s_stage = (c.sem("r_" + x) for x in ("b", "dve", "exp", "cum", "stage"))
    s_sent = c.dma_sem("r_sent")
    mark = {}
    with ExitStack() as ctx:
        sb = lambda nm, sh, dt=F32: c.sb("r_" + nm, sh, dt, ctx)
        gb, pr, eq = sb("gb", [P, n]), sb("pr", [P, T, n]), sb("eq", [P, T, n])
        mx, low, sm = sb("mx", [P, T]), sb("low", [P, T]), sb("sm", [P, T])
        exc, pos, kept, slot = sb("exc", [P, T, n]), sb("pos", [P, T]), sb("kept", [P, T]), sb("slot", [P, T])
        send, stage, idx = sb("send", [P, T]), sb("stage", [P, C, D]), sb("idx", [P, C], I32)
        ps_cum, ps_tot = c.ps("ps_cum", [P, T * n], ctx), c.ps("ps_tot", [P, T * n], ctx)
        b3 = lambda a: a.unsqueeze(2).to_broadcast([P, T, n])
        with nc.Block() as block:

            @block.sync
            def _(sp):
                sp.dma_start(gb[:], gate_b.partition_broadcast(P)).then_inc(s_b, 16)
                sp.wait_ge(s_b, 16)

            @block.vector
            def _(v):
                st = Steps(v, s_dve)
                v.wait_ge(s_b, 16)
                st(v.tensor_tensor(lg[:], lg[:], gb[:].unsqueeze(1).to_broadcast([P, T, n]), ALU.add))
                st.wait()
                st(v.tensor_reduce(mx[:], lg[:], AX, ALU.max))
                st.wait()
                st(v.tensor_tensor(lg[:], lg[:], b3(mx[:]), ALU.subtract))
                mark["exp"] = st.n
                v.wait_ge(s_exp, 1)
                st(v.tensor_reduce(sm[:], pr[:], AX, ALU.add))
                st.wait()
                st(v.reciprocal(sm[:], sm[:]))
                st.wait()
                st(v.tensor_tensor(pr[:], pr[:], b3(sm[:]), ALU.mult))
                st.wait()
                first_of_best(v, st, K, pr[:], n, mx[:], eq[:], low[:])
                mark["hot"] = st.n
                v.wait_ge(s_cum, 1)
                for e in range(n):
                    st(v.tensor_tensor_scan(exc[:, :, e], K.ones[:, 0:T], ps_tot[:].rearrange("p (t n) -> p t n", n=n)[:, :, e],
                                            0.0, ALU.mult, ALU.add))
                st.wait()
                st(v.tensor_tensor(exc[:], exc[:], ps_tot[:].rearrange("p (t n) -> p t n", n=n), ALU.subtract))
                st.wait()
                st(v.tensor_tensor(exc[:], exc[:], ps_cum[:].rearrange("p (t n) -> p t n", n=n), ALU.add))
                st.wait()
                st(v.tensor_tensor(exc[:], exc[:], eq[:], ALU.mult))
                st.wait()
                st(v.tensor_reduce(pos[:], exc[:], AX, ALU.add))
                st.wait()
                st(v.tensor_scalar(pos[:], pos[:], -1.0, None, ALU.add))
                st(v.tensor_scalar(slot[:], low[:], float(CPAD), float(CPAD * n), ALU.mult, ALU.add))
                st.wait()
                st(v.tensor_scalar(kept[:], pos[:], float(CAP), None, ALU.is_lt))
                st(v.tensor_tensor(slot[:], slot[:], pos[:], ALU.add))
                st.wait()
                st(v.tensor_scalar(sm[:, 0:1], K.part[:], float(LAST), None, ALU.is_lt))
                st.wait()
                st(v.tensor_tensor(kept[:, T - 1:T], kept[:, T - 1:T], sm[:, 0:1], ALU.mult))
                st.wait()
                st(v.tensor_scalar(send[:], slot[:], float(-SLOTS), None, ALU.add))
                st(v.tensor_tensor(slot[:], slot[:], kept[:], ALU.mult))
                st.wait()
                st(v.tensor_tensor(send[:], send[:], kept[:], ALU.mult))
                st(v.tensor_copy(K.slot[:], slot[:]))
                st(v.tensor_tensor(K.share[:], mx[:], kept[:], ALU.mult))
                st.wait()
                st(v.tensor_scalar(send[:], send[:], float(SLOTS), None, ALU.add))
                st.wait()

                def turn(i):
                    if not isinstance(i, int):
                        v.wait_ge(s_sent, i * 16 * C)
                    v.tensor_copy(idx[:], send[:, at(i * C, C)]).then_inc(s_stage, 1)
                    v.tensor_copy(stage[:], H[:, at(i * C, C), :]).then_inc(s_stage, 1)
                loop(v, T // C, turn)

            @block.scalar
            def _(act):
                act.wait_ge(s_dve, mark["exp"])
                act.activation(pr[:], lg[:], ACT.Exp).then_inc(s_exp, 1)

            @block.tensor
            def _(pe):
                pe.wait_ge(s_dve, mark["hot"])
                hot = eq[:].rearrange("p t n -> p (t n)")
                pe.matmul(ps_cum[:], K.upto[:], hot, start=True, stop=True)
                pe.matmul(ps_tot[:], K.ones[:], hot, start=True, stop=True).then_inc(s_cum, 1)

            @block.gpsimd
            def _(pool):
                def turn(i):
                    c.hold(pool, s_stage, (i + 1) * 2)
                    for k in range(C):
                        pool.indirect_dma_start(out=slot_rows, out_offset=bass.IndirectOffsetOnAxis(ap=idx[:, k:k + 1], axis=0),
                                                in_=stage[:, k, :], in_offset=None, bounds_check=SLOTS - 1,
                                                oob_is_err=False).then_inc(s_sent, 16)
                loop(pool, T // C, turn)
                pool.wait_ge(s_sent, 16 * T)


def experts(c, slot_rows, slot_out, w1, b1, w2, b2, K):
    nc = c.nc
    NF = FF // P
    sem = lambda x: c.sem("e_" + x)
    s_b, s_T, s_xT, s_h, s_relu, s_y, s_ys = (sem(x) for x in ("b", "T", "xT", "h", "relu", "y", "ys"))
    s_w, s_rows = ([c.dma_sem(f"e_{x}0"), c.dma_sem(f"e_{x}1")] for x in ("w", "rows"))
    s_store = [sem("store0"), sem("store1")]
    with ExitStack() as ctx:
        sb = lambda nm, sh, dt=F32: c.sb("e_" + nm, sh, dt, ctx)
        w1s, w2s = sb("w1s", [P, 2, 2, FF]), sb("w2s", [P, 2, NF, D])
        b1s, b2s = sb("b1s", [P, EXPERTS, NF]), sb("b2s", [P, EXPERTS, D])
        rows, xT, hT, ys = sb("rows", [P, 2, 4, D]), sb("xT", [P, 2, 2, 512]), sb("hT", [P, NF, 512]), sb("ys", [P, 2, 4, D])
        ps_x = [c.ps(f"e_px{i}", [P, 512], ctx) for i in range(2)]
        ps_h = [c.ps(f"e_ph{i}", [P, 512], ctx) for i in range(2)]
        ps_y = [c.ps(f"e_py{i}", [P, 512], ctx) for i in range(2)]
        TURNS_E = EXPERTS // 2
        first = lambda i: isinstance(i, int)
        units = lambda i: [(i * 4 + j, j % 2, i * 2 + j // 2, j // 2, j) for j in range(4)]
        with nc.Block() as block:

            @block.sync
            def _(sp):
                sp.dma_start(b1s[:], b1).then_inc(s_b, 16)
                sp.dma_start(b2s[:], b2.partition_broadcast(P)).then_inc(s_b, 16)

                def turn(i):
                    for u, s, e, se, j in units(i):
                        sp.wait_ge(s_ys, (u + 1) * 4)
                        sp.dma_start(slot_out[at(u * 512, 512), :].rearrange("(t p) d -> p t d", p=P), ys[:, s]) \
                            .then_inc(s_store[s], 16)
                loop(sp, TURNS_E, turn)
                for s in range(2):
                    sp.wait_ge(s_store[s], 16 * EXPERTS)
                sp.wait_ge(s_b, 32)

            @block.gpsimd
            def _(pool):
                def turn(i):
                    for u, s, e, se, j in units(i):
                        if j % 2 == 0:
                            if not first(i):
                                c.hold(pool, s_y, (u - 2) * 4)
                            pool.dma_start(w1s[:, se], w1[at(e), :, :].rearrange("a (c p) f -> p (a c) f", p=P)).then_inc(s_w[se], 16)
                            pool.dma_start(w2s[:, se], w2[at(e), :, :].rearrange("a (c p) d -> p (a c) d", p=P)).then_inc(s_w[se], 16)
                        if not (first(i) and j < 2):
                            c.hold(pool, s_T, u - 1)
                        pool.dma_start(rows[:, s], slot_rows[at(u * 512, 512), :].rearrange("(t p) d -> p t d", p=P)) \
                            .then_inc(s_rows[s], 16)
                loop(pool, TURNS_E, turn)

            @block.tensor
            def _(pe):
                def turn(i):
                    for u, s, e, se, j in units(i):
                        pe.wait_ge(s_rows[s], (i * 2 + j // 2 + 1) * 16)
                        if not (first(i) and j == 0):
                            pe.wait_ge(s_xT, u * 2)
                        for t in range(4):
                            for k in range(2):
                                mm = pe.transpose(ps_x[k][:, t * P:(t + 1) * P], rows[:, s, t, k * P:(k + 1) * P], K.ident[:])
                        mm.then_inc(s_T, 1)
                        if j % 2 == 0:
                            pe.wait_ge(s_w[se], (i + 1) * 32)
                        pe.wait_ge(s_xT, (u + 1) * 2)
                        for f in range(NF):
                            if not (first(i) and j == 0 and f < 2):
                                pe.wait_ge(s_relu, u * NF + f - 1)
                            for k in range(2):
                                mm = pe.matmul(ps_h[f % 2][:], w1s[:, se, k, f * P:(f + 1) * P], xT[:, s, k, :], start=(k == 0), stop=(k == 1))
                            mm.then_inc(s_h, 1)
                        pe.wait_ge(s_relu, (u + 1) * NF)
                        for t in range(4):
                            if not (first(i) and j == 0 and t < 2):
                                pe.wait_ge(s_ys, u * 4 + t - 1)
                            for f in range(NF):
                                mm = pe.matmul(ps_y[t % 2][:, 0:D], hT[:, f, t * P:(t + 1) * P], w2s[:, se, f, :], start=(f == 0), stop=(f == NF - 1))
                            mm.then_inc(s_y, 1)
                loop(pe, TURNS_E, turn)

            @block.scalar
            def _(act):
                act.wait_ge(s_b, 32)

                def turn(i):
                    for u, s, e, se, j in units(i):
                        act.wait_ge(s_T, u + 1)
                        if not (first(i) and j < 2):
                            act.wait_ge(s_h, (u - 1) * NF)
                        for k in range(2):
                            act.copy(xT[:, s, k, :], ps_x[k][:]).then_inc(s_xT, 1)
                        for f in range(NF):
                            if f == 0 and not (first(i) and j == 0):
                                act.wait_ge(s_y, u * 4)
                            c.hold(act, s_h, u * NF + f + 1)
                            act.activation(hT[:, f, :], ps_h[f % 2][:], ACT.Relu,
                                           bias=b1s[:, at(e), f:f + 1].rearrange("p a f -> p (a f)")).then_inc(s_relu, 1)
                loop(act, TURNS_E, turn)

            @block.vector
            def _(v):
                v.wait_ge(s_b, 32)

                def turn(i):
                    for u, s, e, se, j in units(i):
                        if not (first(i) and j < 2):
                            v.wait_ge(s_store[s], (i * 2 + j // 2) * 16)
                        for t in range(4):
                            v.wait_ge(s_y, u * 4 + t + 1)
                            v.tensor_tensor(ys[:, s, t, :], ps_y[t % 2][:, 0:D], b2s[:, at(e), :].rearrange("p a d -> p (a d)"),
                                            ALU.add).then_inc(s_ys, 1)
                loop(v, TURNS_E, turn)


def fetch_back(c, K, slot_out, X):
    nc = c.nc
    C = 7
    s_dve, s_idx, s_got = c.sem("b_dve"), c.sem("b_idx"), c.dma_sem("b_got")
    FMAX = float(np.finfo(np.float32).max)
    per = {}
    with ExitStack() as ctx:
        sb = lambda nm, sh, dt=F32: c.sb("b_" + nm, sh, dt, ctx)
        idx, y, z, m = sb("idx", [P, C], I32), sb("y", [P, C, D]), sb("z", [P, C, D]), sb("m", [P, C, D], I32)
        lim = sb("lim", [P, 2])
        with nc.Block() as block:

            @block.gpsimd
            def _(pool):
                def turn(i):
                    c.hold(pool, s_idx, i + 1)
                    for k in range(C):
                        pool.indirect_dma_start(out=y[:, k, :], out_offset=None, in_=slot_out,
                                                in_offset=bass.IndirectOffsetOnAxis(ap=idx[:, k:k + 1], axis=0)).then_inc(s_got, 16)
                loop(pool, T // C, turn)

            @block.vector
            def _(v):
                st = Steps(v, s_dve)
                st(v.memset(lim[:, 0:1], 10000.0))
                st(v.memset(lim[:, 1:2], -10000.0))

                def turn(i):
                    v.tensor_copy(idx[:], K.slot[:, at(i * C, C)]).then_inc(s_idx, 1)
                    st(v.memset(z[:], 0.0))
                    v.wait_ge(s_got, (i + 1) * 16 * C)
                    st(v.tensor_tensor(y[:], y[:], K.share[:, at(i * C, C)].unsqueeze(2).to_broadcast([P, C, D]), ALU.mult))
                    st.wait()
                    st(v.tensor_tensor(m[:], y[:], y[:], ALU.is_equal))
                    c.hold(v, *st.point())
                    st(v.copy_predicated(z[:], m[:], y[:]))
                    st.wait()
                    for k, (op, lim_) in enumerate(((ALU.is_gt, FMAX), (ALU.is_lt, -FMAX))):
                        st(v.tensor_scalar(m[:], y[:], lim_, None, op))
                        c.hold(v, *st.point())
                        st(v.copy_predicated(z[:], m[:], lim[:, k:k + 1].unsqueeze(2).to_broadcast([P, C, D])))
                        st.wait()
                    o = X[:, at(i * C, C), :]
                    st(v.tensor_tensor(o, o, z[:], ALU.add))
                    st.wait()
                loop(v, T // C, turn, st)


def gate_tables(c, K, hg, att, tab_s, tab_d, ad):
    nc = c.nc
    h = HEADS2
    s_ld, s_dve, s_pool, s_st = (c.sem("t_" + x) for x in ("ld", "dve", "pool", "st"))
    mark = {}
    with ExitStack() as ctx:
        sb = lambda nm, sh, dt=F32: c.sb("t_" + nm, sh, dt, ctx)
        av, tmp, elv = sb("av", [P, 2, 16]), sb("tmp", [P, T, 16]), sb("elv", [P, T, h])
        vm, elm, gmax = sb("vm", [P, 2]), sb("elm", [P, h]), sb("gmax", [P, h])
        with nc.Block() as block:

            @block.vector
            def _(v):
                st = Steps(v, s_dve)
                v.wait_ge(s_ld, 16)
                for side in range(2):
                    st(v.tensor_tensor(tmp[:], hg[:, :, 0:16], av[:, side, :].unsqueeze(1).to_broadcast([P, T, 16]), ALU.mult))
                    st.wait()
                    o = hg[:, :, 16:20] if side == 0 else ad[:, :, 0:h]
                    st(v.tensor_reduce(o, tmp[:].rearrange("p t (h e) -> p t h e", h=h), AX, ALU.add))
                    st.wait()
                st(v.tensor_copy(elv[:], hg[:, :, 16:20]))
                st(v.tensor_scalar(vm[:, 0:1], K.part[:], float(LAST), None, ALU.is_lt))
                st.wait()
                st(v.tensor_scalar(vm[:, 1:2], vm[:, 0:1], BIG, -BIG, ALU.mult, ALU.add))
                st.wait()
                st(v.tensor_scalar(elv[:, T - 1, :], elv[:, T - 1, :], vm[:, 0:1], vm[:, 1:2], ALU.mult, ALU.add))
                st.wait()
                st(v.tensor_reduce(elm[:], elv[:].rearrange("p t h -> p h t"), AX, ALU.max))
                mark["max"] = st.n
                v.wait_ge(s_pool, 1)
                m = ad[:, :, h:2 * h]
                st(v.tensor_tensor(m, ad[:, :, 0:h], gmax[:].unsqueeze(1).to_broadcast([P, T, h]), ALU.add))
                st.wait()
                st(v.scalar_tensor_tensor(m, m, 0.2, m, ALU.mult, ALU.max))
                mark["tab"] = st.n

            @block.sync
            def _(sp):
                sp.dma_start(av[:], att.partition_broadcast(P)).then_inc(s_ld, 16)
                sp.wait_ge(s_dve, mark["tab"])
                sp.dma_start(tab_s.rearrange("(t p) n -> p t n", p=P), hg[:]).then_inc(s_st, 16)
                sp.dma_start(tab_d.rearrange("(t p) n -> p t n", p=P), ad[:]).then_inc(s_st, 16)
                sp.wait_ge(s_st, 32)

            @block.gpsimd
            def _(pool):
                pool.wait_ge(s_dve, mark["max"])
                pool.partition_all_reduce(gmax[:], elm[:], P, RED.max).then_inc(s_pool, 1)


def attend_gate(c, K, src2, dst2, tab_s, tab_d, agg):
    nc = c.nc
    h, W, NGR = HEADS2, 20, ROWS2 // G
    TU = NGR // R
    HALF = 25
    sem = lambda x: c.sem("q_" + x)
    s_ld, s_prep, s_stage, s_pool, s_z, s_w, s_val, s_hot, s_zd, s_main, s_wide = (
        sem(x) for x in ("ld", "prep", "stage", "pool", "z", "w", "val", "hot", "zd", "main", "wide"))
    s_gat = [c.dma_sem(f"q_gat{r}") for r in range(R)]
    with ExitStack() as ctx:
        sb = lambda nm, sh, dt=F32: c.sb("q_" + nm, sh, dt, ctx)
        src_i, dst_i, di = sb("src_i", [P, ROWS2], I32), sb("dst_i", [P, ROWS2], I32), sb("di", [P, ROWS2], I32)
        df, pf, tf = sb("df", [P, ROWS2]), sb("pf", [P, ROWS2]), sb("tf", [P, ROWS2])
        idx = sb("idx", [P, R, 2, G], I32)
        rs, rd = sb("rs", [P, R, G, W]), sb("rd", [P, R, G, 2 * h])
        z, hp, ht = sb("z", [P, 2, G, h]), sb("hp", [P, 2, G, P]), sb("ht", [P, 2, G, T])
        wide = sb("wide", [P, 4, T, W])
        ps = [c.ps(f"q_ps{i}", [P, 512], ctx) for i in range(2)]
        first = lambda i: isinstance(i, int)
        with nc.Block() as block:

            @block.sync
            def _(sp):
                sp.dma_start(src_i[:], src2).then_inc(s_ld, 16)
                sp.dma_start(dst_i[:], dst2).then_inc(s_ld, 16)
                sp.wait_ge(s_ld, 32)

            @block.gpsimd
            def _(pool):
                def turn(i):
                    for r in range(R):
                        g = i * R + r
                        c.hold(pool, s_stage, (g + 1) * 2)
                        if not first(i):
                            c.hold(pool, s_main, (g - R + 1) * G)
                        for k in range(G):
                            for tile, tab, side in ((rs, tab_s, 0), (rd, tab_d, 1)):
                                pool.indirect_dma_start(
                                    out=tile[:, r, k, :], out_offset=None, in_=tab,
                                    in_offset=bass.IndirectOffsetOnAxis(ap=idx[:, r, side, k:k + 1], axis=0)).then_inc(s_gat[r], 16)
                loop(pool, TU, turn)

            @block.scalar
            def _(act):
                act.wait_ge(s_prep, 2)

                def turn(i):
                    for r in range(R):
                        g = i * R + r
                        if not first(i):
                            act.wait_ge(s_gat[r], i * 16 * 2 * G)
                        act.copy(idx[:, r, 0, :], src_i[:, at(g * G, G)]).then_inc(s_stage, 1)
                        act.copy(idx[:, r, 1, :], dst_i[:, at(g * G, G)]).then_inc(s_stage, 1)
                        act.wait_ge(s_z, g + 1)
                        act.activation(rs[:, r, :, 16:20], z[:, r % 2], ACT.Exp).then_inc(s_w, 1)
                loop(act, TU, turn)

            @block.tensor
            def _(pe):
                def turn(i):
                    for r in range(R):
                        g = i * R + r
                        pe.wait_ge(s_hot, g + 1)
                        for k in range(G):
                            pe.wait_ge(s_wide, g * G + k + 1)
                            lead = first(i) and r == 0 and k == 0
                            flat = wide[:, k % 4].rearrange("p t w -> p (t w)")
                            pe.matmul(ps[0][:, 0:HALF * W], hp[:, r % 2, k, :], flat[:, 0:HALF * W], start=lead, stop=False,
                                      skip_group_check=True)
                            pe.matmul(ps[1][:, 0:(T - HALF) * W], hp[:, r % 2, k, :], flat[:, HALF * W:T * W], start=lead, stop=False,
                                      skip_group_check=True).then_inc(s_main, 1)
                loop(pe, TU, turn)

            @block.vector
            def _(v):
                st = Steps(v, s_zd)
                v.wait_ge(s_ld, 32)
                st(v.tensor_copy(df[:], dst_i[:]))
                st(v.tensor_copy(pf[:], src_i[:]))
                st(v.tensor_scalar(di[:], dst_i[:], 7, None, ALU.arith_shift_right))
                st.wait()
                st(v.tensor_scalar(pf[:], pf[:], float(N - 1), None, ALU.min))
                st(v.tensor_copy(tf[:], di[:]))
                st.wait()
                v.tensor_copy(src_i[:], pf[:]).then_inc(s_prep, 1)
                st(v.tensor_scalar(di[:], df[:], float(N - 1), None, ALU.min))
                v.wait_ge(s_prep, 1)
                st(v.scalar_tensor_tensor(pf[:], tf[:], float(-P), df[:], ALU.mult, ALU.add))
                st.wait()
                v.tensor_copy(dst_i[:], di[:]).then_inc(s_prep, 1)

                def turn(i):
                    for r in range(R):
                        g, b = i * R + r, r % 2
                        if not (first(i) and r < 2):
                            v.wait_ge(s_main, (g - 1) * G)
                        v.tensor_tensor(hp[:, b], K.iota[:].unsqueeze(1).to_broadcast([P, G, P]),
                                        pf[:, at(g * G, G)].unsqueeze(2).to_broadcast([P, G, P]), ALU.is_equal).then_inc(s_hot, 1)
                        st(v.tensor_tensor(ht[:, b], K.iota[:, 0:T].unsqueeze(1).to_broadcast([P, G, T]),
                                           tf[:, at(g * G, G)].unsqueeze(2).to_broadcast([P, G, T]), ALU.is_equal))
                        v.wait_ge(s_gat[r], (i + 1) * 16 * 2 * G)
                        zb = z[:, b]
                        st(v.tensor_tensor(zb, rs[:, r, :, 16:20], rd[:, r, :, 0:h], ALU.add))
                        st.wait()
                        st(v.scalar_tensor_tensor(zb, zb, 0.2, zb, ALU.mult, ALU.max))
                        st.wait()
                        v.tensor_tensor(zb, zb, rd[:, r, :, h:2 * h], ALU.subtract).then_inc(s_z, 1)
                        v.wait_ge(s_w, g + 1)
                        f = rs[:, r, :, 0:16].rearrange("p k (h e) -> p k h e", h=h)
                        st(v.tensor_tensor(f, f, rs[:, r, :, 16:20].unsqueeze(3).to_broadcast([P, G, h, 4]), ALU.mult))
                        st.wait()
                        for k in range(G):
                            if not (first(i) and r == 0 and k < 4):
                                v.wait_ge(s_main, g * G + k - 3)
                            v.tensor_tensor(wide[:, k % 4], ht[:, b, k, :].unsqueeze(2).to_broadcast([P, T, W]),
                                            rs[:, r, k, :].unsqueeze(1).to_broadcast([P, T, W]), ALU.mult).then_inc(s_wide, 1)
                loop(v, TU, turn, st)
                v.wait_ge(s_main, ROWS2)
                a = agg[:].rearrange("p t w -> p (t w)")
                st(v.tensor_copy(a[:, 0:HALF * W], ps[0][:, 0:HALF * W]))
                st(v.tensor_copy(a[:, HALF * W:T * W], ps[1][:, 0:(T - HALF) * W]))


def gate_scores(c, K, hg, ad, agg, consts, gates):
    nc = c.nc
    h, n = HEADS2, EXPERTS2
    s_ld, s_dve, s_act = (c.sem("u_" + x) for x in ("ld", "dve", "act"))
    mark = {}
    with ExitStack() as ctx:
        sb = lambda nm, sh, dt=F32: c.sb("u_" + nm, sh, dt, ctx)
        cs = sb("cs", [P, 3, 16])
        z, w, o, q = sb("z", [P, T, h]), sb("w", [P, T, h]), sb("o", [P, T, 16]), sb("q", [P, T, 16])
        mu, var, sc = sb("mu", [P, T]), sb("var", [P, T]), sb("sc", [P, T, n])
        b1, b2, low, e1, e2 = sb("b1", [P, T]), sb("b2", [P, T]), sb("low", [P, T]), sb("e1", [P, T, n]), sb("e2", [P, T, n])
        wide = lambda a, k: a.unsqueeze(2).to_broadcast([P, T, k])
        heads = lambda a: a.unsqueeze(3).to_broadcast([P, T, h, 4])
        each = lambda a: a.rearrange("p t (h e) -> p t h e", h=h)
        row = lambda k: cs[:, k, :].unsqueeze(1).to_broadcast([P, T, 16])
        with nc.Block() as block:

            @block.vector
            def _(v):
                st = Steps(v, s_dve)

                def do(ins):
                    st(ins)
                    st.wait()
                do(v.tensor_tensor(z[:], hg[:, :, 16:20], ad[:, :, 0:h], ALU.add))
                do(v.scalar_tensor_tensor(z[:], z[:], 0.2, z[:], ALU.mult, ALU.max))
                do(v.tensor_tensor(z[:], z[:], ad[:, :, h:2 * h], ALU.subtract))
                mark["z"] = st.n
                v.wait_ge(s_act, 1)
                v.wait_ge(s_ld, 16)
                do(v.tensor_tensor(each(o[:]), each(hg[:, :, 0:16]), heads(w[:]), ALU.mult))
                do(v.tensor_tensor(o[:], o[:], agg[:, :, 0:16], ALU.add))
                do(v.tensor_tensor(w[:], w[:], agg[:, :, 16:20], ALU.add))
                do(v.reciprocal(w[:], w[:]))
                do(v.tensor_tensor(each(o[:]), each(o[:]), heads(w[:]), ALU.mult))
                do(v.tensor_tensor(o[:], o[:], row(0), ALU.add))
                do(v.tensor_reduce(mu[:], o[:], AX, ALU.add))
                do(v.tensor_scalar(mu[:], mu[:], 1.0 / 16, None, ALU.mult))
                do(v.tensor_tensor(o[:], o[:], wide(mu[:], 16), ALU.subtract))
                do(v.tensor_tensor(q[:], o[:], o[:], ALU.mult))
                do(v.tensor_reduce(var[:], q[:], AX, ALU.add))
                do(v.tensor_scalar(var[:], var[:], 1.0 / 16, LN_EPS, ALU.mult, ALU.add))
                mark["var"] = st.n
                v.wait_ge(s_act, 2)
                do(v.reciprocal(var[:], var[:]))
                do(v.tensor_tensor(o[:], o[:], wide(var[:], 16), ALU.mult))
                do(v.tensor_tensor(o[:], o[:], row(1), ALU.mult))
                do(v.tensor_tensor(o[:], o[:], row(2), ALU.add))
                do(v.tensor_reduce(sc[:], o[:].rearrange("p t (h e) -> p t e h", h=h), AX, ALU.add))
                do(v.tensor_scalar(sc[:], sc[:], 1.0 / h, None, ALU.mult))
                first_of_best(v, st, K, sc[:], n, b1[:], e1[:], low[:])
                do(v.scalar_tensor_tensor(sc[:], e1[:], -BIG, sc[:], ALU.mult, ALU.add))
                first_of_best(v, st, K, sc[:], n, b2[:], e2[:], low[:])
                do(v.tensor_tensor(b2[:], b2[:], b1[:], ALU.subtract))
                mark["gap"] = st.n
                v.wait_ge(s_act, 3)
                do(v.tensor_scalar(b1[:], b2[:], 1.0, None, ALU.add))
                do(v.reciprocal(b1[:], b1[:]))
                do(v.tensor_tensor(b2[:], b2[:], b1[:], ALU.mult))
                do(v.tensor_tensor(e1[:], e1[:], wide(b1[:], n), ALU.mult))
                do(v.tensor_tensor(e2[:], e2[:], wide(b2[:], n), ALU.mult))
                do(v.tensor_tensor(gates[:], e1[:], e2[:], ALU.add))

            @block.sync
            def _(sp):
                sp.dma_start(cs[:], consts.partition_broadcast(P)).then_inc(s_ld, 16)
                sp.wait_ge(s_ld, 16)

            @block.scalar
            def _(act):
                act.wait_ge(s_dve, mark["z"])
                act.activation(w[:], z[:], ACT.Exp).then_inc(s_act, 1)
                act.wait_ge(s_dve, mark["var"])
                act.activation(var[:], var[:], ACT.Sqrt).then_inc(s_act, 1)
                act.wait_ge(s_dve, mark["gap"])
                act.activation(b2[:], b2[:], ACT.Exp).then_inc(s_act, 1)


def experts_two(c, K, H, X, gates, w1, b1, w2, b2):
    nc = c.nc
    NF, NE = FF2 // P, EXPERTS2
    U = T // 4
    sem = lambda x: c.sem("v_" + x)
    s_ld, s_place, s_T, s_xT, s_h, s_act, s_y, s_sum = (sem(x) for x in ("ld", "place", "T", "xT", "h", "act", "y", "sum"))
    with ExitStack() as ctx:
        sb = lambda nm, sh, dt=F32: c.sb("v_" + nm, sh, dt, ctx)
        w1s, w2s, b1s, b2s = sb("w1s", [P, NE, 2, FF2]), sb("w2s", [P, NE, NF, D]), sb("b1s", [P, NE, NF]), sb("b2s", [1, NE, D])
        rows, xT, hT = sb("rows", [P, 4, D]), sb("xT", [P, 2, 512]), sb("hT", [P, 2, NF, 512])
        ps_x = [c.ps(f"v_px{i}", [P, 512], ctx) for i in range(2)]
        ps_h = [c.ps(f"v_ph{i}", [P, 512], ctx) for i in range(2)]
        ps_y = [c.ps(f"v_py{i}", [P, 512], ctx) for i in range(4)]
        def units(eng, body, *steps):
            loop(eng, U, lambda i: body(i, 4), *steps)
            body(U, 1)
        lead = lambda i: isinstance(i, int) and i == 0
        with nc.Block() as block:

            @block.sync
            def _(sp):
                sp.dma_start(w1s[:], w1).then_inc(s_ld, 16)
                sp.dma_start(w2s[:], w2).then_inc(s_ld, 16)
                sp.dma_start(b1s[:], b1).then_inc(s_ld, 16)
                sp.dma_start(b2s[:], b2).then_inc(s_ld, 16)
                sp.wait_ge(s_ld, 64)

            @block.tensor
            def _(pe):
                pe.wait_ge(s_ld, 64)

                def unit(i, nt):
                    w = nt * P
                    pe.wait_ge(s_place, i + 1)
                    if not lead(i):
                        pe.wait_ge(s_xT, i * 2)
                    for t in range(nt):
                        for k in range(2):
                            mm = pe.transpose(ps_x[k][:, t * P:(t + 1) * P], rows[:, t, k * P:(k + 1) * P], K.ident[:])
                    mm.then_inc(s_T, 1)
                    pe.wait_ge(s_xT, (i + 1) * 2)
                    for e in range(NE):
                        for f in range(NF):
                            if not (lead(i) and e == 0 and f < 2):
                                pe.wait_ge(s_act, (i * NE + e) * NF + f - 1)
                            for k in range(2):
                                mm = pe.matmul(ps_h[f % 2][:, 0:w], w1s[:, e, k, f * P:(f + 1) * P], xT[:, k, 0:w], start=(k == 0), stop=(k == 1))
                            mm.then_inc(s_h, 1)
                        pe.wait_ge(s_act, (i * NE + e + 1) * NF)
                        for t in range(nt):
                            if not (lead(i) and e == 0):
                                pe.wait_ge(s_sum, i * NE * 4 + (e - 1) * nt + t + 1 if e else (i - 1) * NE * 4 + 3 * 4 + t + 1)
                            for f in range(NF):
                                pe.matmul(ps_y[t][:, 0:D], hT[:, e % 2, f, t * P:(t + 1) * P], w2s[:, e, f, :], start=(f == 0), stop=False)
                            pe.matmul(ps_y[t][:, 0:D], K.ones[0:1, :], b2s[:, e, :], start=False, stop=True).then_inc(s_y, 1)
                units(pe, unit)

            @block.scalar
            def _(act):
                act.wait_ge(s_ld, 64)

                def unit(i, nt):
                    w = nt * P
                    act.wait_ge(s_T, i + 1)
                    if not lead(i):
                        act.wait_ge(s_h, i * NE * NF)
                    for k in range(2):
                        act.copy(xT[:, k, 0:w], ps_x[k][:, 0:w]).then_inc(s_xT, 1)
                    for e in range(NE):
                        for f in range(NF):
                            act.wait_ge(s_h, (i * NE + e) * NF + f + 1)
                            if f == 0 and not (lead(i) and e < 2):
                                act.wait_ge(s_y, i * NE * 4 + (e - 1) * nt if e >= 2 else i * NE * 4 - (1 - e) * 4)
                            act.activation(hT[:, e % 2, f, 0:w], ps_h[f % 2][:, 0:w], ACT.Gelu, bias=b1s[:, e, f:f + 1]).then_inc(s_act, 1)
                units(act, unit)

            @block.vector
            def _(v):
                def unit(i, nt):
                    if not lead(i):
                        v.wait_ge(s_T, i)
                    v.tensor_copy(rows[:, 0:nt, :], H[:, at(i * 4, nt), :]).then_inc(s_place, 1)
                    for e in range(NE):
                        for t in range(nt):
                            v.wait_ge(s_y, i * NE * 4 + e * nt + t + 1)
                            if e:
                                v.wait_ge(s_sum, i * NE * 4 + (e - 1) * nt + t + 1)
                            o = X[:, at(i * 4 + t), :].rearrange("p a d -> p (a d)")
                            v.scalar_tensor_tensor(o, ps_y[t][:, 0:D], gates[:, at(i * 4 + t), e], o, ALU.mult, ALU.add).then_inc(s_sum, 1)
                units(v, unit)


def build(nc, a, out, upto=99):
    with ExitStack() as ctx:
        c = Chip(nc, ctx)

        class K:
            ident, ones, upto, iota = (c.sb(n, [P, P]) for n in ("ident", "ones", "upto_", "iota"))
            part = c.sb("part", [P, 1])
            iota_low = c.sb("iota_low", [P, P])
            norm, share, slot = c.sb("norm", [P, T]), c.sb("share", [P, T]), c.sb("slot", [P, T], I32)
        dram = lambda n, sh, dt=F32: nc.dram_tensor(n, list(sh), dt).ap()
        slot_rows, slot_out = dram("slot_rows", [SLOTS, D]), dram("slot_out", [SLOTS, D])
        ids_dram = dram("ids_dram", [Q, P], I32)
        table8, table4, table1 = dram("table8", [NPAD, D + 8]), dram("table4", [NPAD, D + 4]), dram("table1", [NPAD, D + 2])
        tab_s, tab_d = dram("tab_s", [NPAD, 20]), dram("tab_d", [NPAD, 8])
        base_a, base_b = dram("base_a", [NPAD, 2 * D]), dram("base_b", [NPAD, D])
        X, acc = c.sb("X", [P, T, D]), c.sb("acc", [P, T, D + 9])
        H = acc[:, :, 0:D]
        with ExitStack() as graph:
            K.er = c.sb("er", [P, T, 16], F32, graph)
            K.src_cols, K.dst_cols = c.sb("src_cols", [P, Q * P], I32, graph), c.sb("dst_cols", [P, Q * P], F32, graph)
            K.ids = c.sb("ids", [1, Q * P], I32, graph)
            prep(c, a["x"], a["src"], a["dst"], K, X, slot_rows, ids_dram)
            if upto in (1,) or upto >= 1:
                layernorm(c, "n1_", X, H)
                project(c, "a1_", K, H, a["L0_gnn_fc1_wT"], a["L0_gnn_fc1_w"], a["attn_a1"], 8,
                        table8, Base(a["w_base"], a["b_base"], base_a))
            if upto >= 2:
                attend(c, "g1_", K, table8, 8, acc)
                combine(c, "c1_", K, acc, 8, H, a["L0_gnn_bias1"], (base_a[:, 0:D],), relu=True, degree=True)
            if upto >= 3:
                project(c, "a2_", K, H, a["L0_gnn_fc2_wT"], a["L0_gnn_fc2_w"], a["attn_a2"], 1,
                        table1, Base(a["w_base2"], None, base_b))
                attend(c, "g2_", K, table1, 1, acc)
                combine(c, "c2_", K, acc, 1, X, a["L0_gnn_bias2"], (base_a[:, D:2 * D], base_b), residual=True)
            c.renew()
            if upto >= 4:
                layernorm(c, "n2_", X, H)
                with ExitStack() as gate:
                    lg = c.sb("lg", [P, T, EXPERTS], F32, gate)
                    narrow(c, "r1_", K, H, a["L0_ffn_gate_w"], lg)
                    route(c, K, lg, a["L0_ffn_gate_b"], H, slot_rows)
                experts(c, slot_rows, slot_out, a["L0_ffn_w1"], a["L0_ffn_b1"], a["L0_ffn_w2"], a["L0_ffn_b2"], K)
                fetch_back(c, K, slot_out, X)
            c.renew()
            if upto >= 5:
                layernorm(c, "n3_", X, H)
                project(c, "b1_", K, H, a["L1_gnn_W1T"], a["L1_gnn_W1"], a["attn_c1"], 4, table4)
                attend(c, "g3_", K, table4, 4, acc)
                combine(c, "c3_", K, acc, 4, H, relu=True)
                project(c, "b2_", K, H, a["L1_gnn_W2T"], a["L1_gnn_W2"], a["attn_c2"], 1, table1)
                attend(c, "g4_", K, table1, 1, acc)
                combine(c, "c4_", K, acc, 1, X, residual=True)
        c.renew()
        if upto >= 6:
            layernorm(c, "n4_", X, H)
            hg, ad, agg = c.sb("hg", [P, T, 20]), c.sb("ad", [P, T, 8]), c.sb("agg", [P, T, 20])
            gates = c.sb("gates", [P, T, EXPERTS2])
            narrow(c, "r2_", K, H, a["L1_ffn_W_gat"], hg[:, :, 0:16])
            gate_tables(c, K, hg, a["gate_att"], tab_s, tab_d, ad)
            attend_gate(c, K, a["src2"], a["dst2"], tab_s, tab_d, agg)
            gate_scores(c, K, hg, ad, agg, a["gate_norm"], gates)
            experts_two(c, K, H, X, gates, a["L1_ffn_W1"], a["L1_ffn_b1"], a["L1_ffn_W2"], a["L1_ffn_b2"])
        s_end = c.sem("end")
        with nc.Block() as block:

            @block.sync
            def _(sp):
                sp.dma_start(out[0:(T - 1) * P, :].rearrange("(t p) d -> p t d", p=P), X[:, 0:T - 1, :]).then_inc(s_end, 16)
                sp.dma_start(out[(T - 1) * P:N, :], X[0:LAST, T - 1, :]).then_inc(s_end, 16)
                sp.wait_ge(s_end, 32)


def _layout(inputs):
    a = {k: np.ascontiguousarray(v) for k, v in inputs.items()}
    o = {"x": a["x"]}
    o["src"] = np.pad(a["src"], (0, ROWS * P - E)).reshape(ROWS, P)
    o["dst"] = np.pad(a["dst"], (0, ROWS * P - E), constant_values=1 << 20).reshape(ROWS, P)
    o["L0_gnn_fc1_w"], o["L0_gnn_fc1_wT"] = a["L0_gnn_fc1_w"], a["L0_gnn_fc1_w"].T
    o["L0_gnn_fc2_w"], o["L0_gnn_fc2_wT"] = a["L0_gnn_fc2_w"], a["L0_gnn_fc2_w"].T
    for n, l, r in (("a1", "L0_gnn_attn_l1", "L0_gnn_attn_r1"), ("a2", "L0_gnn_attn_l2", "L0_gnn_attn_r2"),
                    ("c1", "L1_gnn_a1_src", "L1_gnn_a1_dst"), ("c2", "L1_gnn_a2_src", "L1_gnn_a2_dst")):
        o["attn_" + n] = np.stack([a[l].reshape(2, P).T, a[r].reshape(2, P).T], axis=2)
    o["w_base"] = np.concatenate([a["L0_gnn_wb0"].T, a["L0_gnn_wb1"][:, :D].T], axis=1)
    o["b_base"] = np.concatenate([a["L0_gnn_bb0"], a["L0_gnn_bb1"]]).reshape(1, 2 * D)
    o["w_base2"] = a["L0_gnn_wb1"][:, D:].T
    o["L0_gnn_bias1"], o["L0_gnn_bias2"] = a["L0_gnn_bias1"], a["L0_gnn_bias2"]
    for n in ("gate_w", "gate_b", "w1", "w2", "b2"):
        o["L0_ffn_" + n] = a["L0_ffn_" + n]
    o["L0_ffn_b1"] = a["L0_ffn_b1"].reshape(EXPERTS, FF // P, P).transpose(2, 0, 1)
    for n in ("W1", "W2"):
        o["L1_gnn_" + n], o["L1_gnn_" + n + "T"] = a["L1_gnn_" + n], a["L1_gnn_" + n].T
    o["L1_ffn_W_gat"] = a["L1_ffn_W_gat"]
    o["gate_att"] = np.stack([a["L1_ffn_att_src"].reshape(-1), a["L1_ffn_att_dst"].reshape(-1)])
    o["gate_norm"] = np.stack([a["L1_ffn_b_gat"], a["L1_ffn_ln_gamma"], a["L1_ffn_ln_beta"]])
    o["src2"], o["dst2"] = a["L1_ffn_edge_index"].reshape(2, P, ROWS2)
    o["L1_ffn_W1"] = a["L1_ffn_W1"].reshape(EXPERTS2, 2, P, FF2).transpose(2, 0, 1, 3)
    o["L1_ffn_W2"] = a["L1_ffn_W2"].reshape(EXPERTS2, FF2 // P, P, D).transpose(2, 0, 1, 3)
    o["L1_ffn_b1"] = a["L1_ffn_b1"].reshape(EXPERTS2, FF2 // P, P).transpose(2, 0, 1)
    o["L1_ffn_b2"] = a["L1_ffn_b2"].reshape(1, EXPERTS2, D)
    return {k: np.ascontiguousarray(v) for k, v in o.items()}


def kernel(**inputs):
    from concourse import bacc
    from concourse.bass_utils import run_bass_kernel_spmd

    nc = bacc.Bacc("TRN2", target_bir_lowering=False, num_devices=1)
    arrays = {f"in_{k}": v for k, v in _layout(inputs).items()}
    args = {k[3:]: nc.dram_tensor(k, v.shape, mybir.dt.from_np(v.dtype), kind="ExternalInput").ap() for k, v in arrays.items()}
    out = nc.dram_tensor("out", [N, D], F32, kind="ExternalOutput").ap()
    build(nc, args, out)
    return run_bass_kernel_spmd(nc, [arrays], core_ids=[0]).results[0]["out"]
```

```python
from contextlib import ExitStack

import numpy as np

import concourse.bass as bass
from concourse import mybir
from concourse.alu_op_type import AluOpType as ALU

F32 = mybir.dt.float32
I32 = mybir.dt.int32
ACT = mybir.ActivationFunctionType
AX = mybir.AxisListType.X
RED = bass.bass_isa.ReduceOp
DVE = mybir.EngineType.DVE
PE = mybir.EngineType.PE

P = 128
N = 6250
D = 256
T = (N + P - 1) // P
NPAD = T * P
LAST = N - (T - 1) * P
E = 100000
ROWS = (E + P - 1) // P
G = 8
AHEAD = 3
BIG = 3.0e38
LN_EPS = 1e-5
E2 = 131072
ROWS2 = E2 // P
N2MAX = 8192

EXPERTS = 8
CAP = 977
CPAD = 1024
SLOTS = EXPERTS * CPAD
FF = 1024
EXPERTS2 = 4
FF2 = 512
HEADS2 = 4


class Steps:

    def __init__(self, eng, sem):
        self.eng, self.sem, self.n, self.base = eng, sem, 0, 0

    def __call__(self, ins):
        ins.then_inc(self.sem, 1)
        self.n += 1

    def point(self):
        return self.sem, self.base + self.n

    def wait(self):
        self.eng.wait_ge(*self.point())

    def turn(self, i, before, period):
        self.base, self.n = i * period + before, 0

    def leave(self, turns, before, period):
        self.base, self.n = 0, before + turns * period


def loop(eng, turns, body, *steps, peel=False):
    before = [s.n for s in steps]
    body(0)
    periods = [s.n - b for s, b in zip(steps, before)]
    end = turns - 1 if peel else turns
    if end > 1:
        with eng.Fori(1, end) as i:
            for s, b, p in zip(steps, before, periods):
                s.turn(i, b, p)
            body(i)
    for s, b, p in zip(steps, before, periods):
        s.leave(end, b, p)
    if peel:
        body(end)


def early(t):
    return isinstance(t, int) and t < 2


def ahead_tiles(lead, body, eng):
    lead(0, 0, 0)

    def tile(t, s, i):
        if not (isinstance(t, int) and t == T - 1):
            lead(t + 1, 1 - s, i)
        body(t, s, i)
    tiles(tile, eng)


def tiles(body, eng, n=T):
    body(0, 0, 0)
    body(1, 1, 0)
    with eng.Fori(1, n // 2) as i:
        body(i * 2, 0, i)
        body(i * 2 + 1, 1, i)
    body(n - 1, 0, n // 2)


def place_rows(v, h, t, dst, s_rows, s_turned):
    if not early(t):
        v.wait_ge(s_turned, t - 1)
    v.tensor_copy(dst, h[:, at(t), :].rearrange("p a f -> p (a f)")).then_inc(s_rows, 1)


def at(i, n=1):
    return bass.ds(i, n)


class Chip:

    def __init__(self, nc, ctx):
        self.nc, self.ctx = nc, ctx
        self.sems = ctx.enter_context(ExitStack())
        self.lowest = self.next = min(nc.free_semaphores)
        self.highest = max(nc.free_semaphores)
        self.held = self.dma_sem("held")

    def sb(self, name, shape, dt=F32, ctx=None):
        return (ctx or self.ctx).enter_context(self.nc.sbuf_tensor(name, list(shape), dt))

    def ps(self, name, shape, ctx, dt=F32):
        return ctx.enter_context(self.nc.psum_tensor(name, list(shape), dt))

    def sem(self, name):
        self.next += 1
        return self.sems.enter_context(self.nc.semaphore(name, self.next - 1))

    def dma_sem(self, name):
        self.highest -= 1
        return self.ctx.enter_context(self.nc.semaphore(name, self.highest + 1))

    def hold(self, eng, sem, value):
        eng.wait_ge(sem, value)
        eng.sem_inc(self.held, 1)

    def renew(self):
        self.sems.close()
        used, self.next = range(self.lowest, self.next), self.lowest
        with self.nc.Block() as block:

            @block.gpsimd
            def _(pool):
                pool.sem_clear(used)


class Edges:

    def __init__(self, c, name, rows, groups_per_turn, ctx):
        self.name, self.rows, self.R = name, rows, groups_per_turn
        most = rows + T - 1
        self.NG = -(-most // (G * self.R)) * self.R
        self.Q = -(-(self.NG + AHEAD) * G // P)
        self.dram = c.nc.dram_tensor(name + "edges", [rows * P, 2], I32).ap()
        self.ids_dram = c.nc.dram_tensor(name + "ids", [self.Q, P], I32).ap()
        self.start = c.sb(name + "start", [P, T + 1], F32, ctx)
        self.first_slot = c.sb(name + "first_slot", [P, T + 1], F32, ctx)

    def columns(self, c, ctx):
        self.src_cols = c.sb(self.name + "src_cols", [P, self.Q * P], I32, ctx)
        self.dst_cols = c.sb(self.name + "dst_cols", [P, self.Q * P], F32, ctx)
        self.ids = c.sb(self.name + "ids_row", [1, self.Q * P], I32, ctx)


class Order:

    def __init__(self, c, name, e, tile_f, packed, ctx):
        self.e, self.tile_f, self.packed = e, tile_f, packed
        self.place, self.hot, self.run = (c.sb(name + x, [P, e.rows], F32, ctx) for x in ("place", "hot", "run"))

    STEPS = 4

    def begin(self, v, st):
        st(v.memset(self.place[:], 0.0))
        st.wait()

    def end(self, v, st):
        st(v.tensor_scalar(self.packed[:, 0:self.e.rows, 0], self.place[:], -1.0, None, ALU.add))
        st.wait()

    def tile(self, v, st, K, t):
        st(v.tensor_scalar(self.hot[:], self.tile_f, K.iota[:, at(t)], None, ALU.is_equal))
        st.wait()
        st(v.tensor_tensor_scan(self.run[:], self.hot[:], self.hot[:], self.e.first_slot[:, at(t)], ALU.add, ALU.max))
        st.wait()
        st(v.tensor_tensor(self.hot[:], self.hot[:], self.run[:], ALU.mult))
        st.wait()
        st(v.tensor_tensor(self.place[:], self.place[:], self.hot[:], ALU.add))


class Sender:

    def __init__(self, c, name, e, packed, ctx):
        self.c, self.e, self.packed, self.done = c, e, packed, 0
        self.stage = c.sb(name + "stage", [P, 2, G, 3], I32, ctx)
        self.sent = [c.dma_sem(f"{name}sent{s}") for s in range(2)]
        self.name = name

    def send(self, pool, turns, key):
        c, first, before = self.c, self.done, self.done * 16 * G
        s_staged = c.sem(f"{self.name}staged{key}")
        self.done += turns

        def turn(i):
            for s in range(2):
                if not (isinstance(i, int) and first == 0):
                    c.hold(pool, self.sent[s], i * (16 * G) + before)
                pool.tensor_copy(self.stage[:, s], self.packed[:, at((i * 2 + first * 2 + s) * G, G), :]).then_inc(s_staged, 1)
                c.hold(pool, s_staged, i * 2 + s + 1)
                for k in range(G):
                    pool.indirect_dma_start(
                        out=self.e.dram, out_offset=bass.IndirectOffsetOnAxis(ap=self.stage[:, s, k, 0:1], axis=0),
                        in_=self.stage[:, s, k, 1:3], in_offset=None, bounds_check=self.e.rows * P - 1,
                        oob_is_err=False).then_inc(self.sent[s], 16)
        loop(pool, turns, turn)

    def finish(self, pool):
        for s in range(2):
            pool.wait_ge(self.sent[s], self.done * 16 * G)


def prepare(c, a, K, X, acc, e1, e2, slot_rows, packed2, tile2):
    nc = c.nc
    sem = lambda x: c.sem("p_" + x)
    s_const, s_load, s_dve, s_sum, s_pool, s_zero = (sem(x) for x in ("const", "load", "dve", "sum", "pool", "zero"))
    s_x, s_zout, s_copy, s_act, s_load2, s_pre, s_flag = (sem(x) for x in ("x", "zout", "copy", "act", "load2", "pre", "flag"))
    s_general = sem("general")
    COLS = -(-ROWS // (2 * G)) * 2 * G
    mark = {}
    with ExitStack() as ctx:
        sb = lambda n, sh, dt=F32: c.sb("p_" + n, sh, dt, ctx)
        iota_i, part_i = sb("iota_i", [P, P], I32), sb("part_i", [P, 1], I32)
        thr, nthr = sb("thr", [P, T + 1]), sb("nthr", [P, T + 1])
        src_i, dst_i, next_i = (sb(x, [P, ROWS], I32) for x in ("src_i", "dst_i", "next_i"))
        whole_i = sb("whole_i", [P, ROWS], I32)
        dst_f, junk = sb("dst_f", [P, ROWS]), sb("junk", [P, ROWS])
        src2_i, dst2_i = sb("src2_i", [P, ROWS2], I32), sb("dst2_i", [P, ROWS2], I32)
        spare = acc[:].rearrange("p t f -> p (t f)")
        junk2, dst2_f, junk3 = (spare[:, k * ROWS2:(k + 1) * ROWS2] for k in range(3))
        zero = spare[:, 3 * ROWS2:3 * ROWS2 + 2048]
        cnt, own = sb("cnt", [P, 2, T + 1]), sb("own", [P, 2, T + 1])
        bad, bad_all, flag = sb("bad", [P, 1]), sb("bad_all", [P, 1]), sb("flag", [P, 1], I32)
        packed1 = sb("packed1", [P, COLS, 3], I32)
        order1 = Order(c, "p_o1", e1, dst_f[:], packed1, ctx)
        send1 = Sender(c, "p_s1", e1, packed1, ctx)
        ps_sum, ps_pre = c.ps("ps_sum", [P, 512], ctx), c.ps("ps_pre", [P, 512], ctx)
        with nc.Block() as block:

            @block.gpsimd
            def _(pool):
                pool.iota(iota_i[:], [[1, P]], base=0, channel_multiplier=0).then_inc(s_pool, 1)
                pool.iota(part_i[:], [[0, 1]], base=0, channel_multiplier=1).then_inc(s_pool, 1)
                pool.memset(K.ident[:], 0.0).then_inc(s_zero, 1)
                pool.memset(K.ones[:], 1.0).then_inc(s_zero, 1)
                pool.memset(zero, 0.0).then_inc(s_zero, 1)
                pool.memset(X[:, T - 1, :], 0.0).then_inc(s_zero, 1)
                pool.wait_ge(s_zero, 4)
                pool.affine_select(out=K.ident[:], in_=K.ident[:], compare_op=ALU.not_equal, fill=1.0, base=0,
                                   pattern=[[-1, P]], channel_multiplier=1).then_inc(s_const, 1)
                pool.affine_select(out=K.upto[:], in_=K.ones[:], compare_op=ALU.is_ge, fill=0.0, base=0,
                                   pattern=[[1, P]], channel_multiplier=-1).then_inc(s_const, 1)
                pool.wait_ge(s_flag, 1)
                pool.partition_all_reduce(bad_all[:], bad[:], P, RED.max).then_inc(s_flag, 1)

            @block.sync
            def _(sp):
                flat = lambda x, n: x.rearrange("r e -> (r e)")[n:n + ROWS * P].rearrange("(p j) -> p j", p=P)
                sp.dma_start(dst_i[:], flat(a["dst"], 0)).then_inc(s_load, 16)
                sp.dma_start(next_i[:], flat(a["dst"], 1)).then_inc(s_load, 16)
                sp.dma_start(dst2_i[:], a["dst2"]).then_inc(s_load2, 16)
                sp.dma_start(src2_i[:], a["src2"]).then_inc(s_load2, 16)
                sp.dma_start(src_i[:], flat(a["src"], 0)).then_inc(s_copy, 16)
                sp.dma_start(e1.dram.rearrange("(p n) e -> p (n e)", p=P), a["edges1"].rearrange("(p n) e -> p (n e)", p=P)).then_inc(s_copy, 16)
                sp.dma_start(X[:, 0:T - 1, :], a["x"][0:(T - 1) * P, :].rearrange("(t p) d -> p t d", p=P)).then_inc(s_x, 16)
                sp.wait_ge(s_zero, 4)
                sp.dma_start(X[0:LAST, T - 1, :], a["x"][(T - 1) * P:N, :]).then_inc(s_x, 16)
                for n in range(SLOTS // 1024):
                    sp.dma_start(slot_rows[n * 1024:(n + 1) * 1024, :].rearrange("(p a) d -> p (a d)", p=P),
                                 zero).then_inc(s_zout, 16)
                sp.wait_ge(s_copy, 32)
                sp.wait_ge(s_x, 32)
                sp.wait_ge(s_zout, 16 * (SLOTS // 1024))

            @block.vector
            def _(v):
                st = Steps(v, s_dve)
                v.wait_ge(s_pool, 2)
                st(v.tensor_copy(K.iota[:], iota_i[:]))
                st(v.tensor_copy(K.part[:], part_i[:]))
                st(v.tensor_scalar(K.iota_low[:], iota_i[:], float(-P), None, ALU.add))
                st.wait()
                st(v.tensor_scalar(thr[:], K.iota[:, 0:T + 1], float(P), None, ALU.mult))
                st(v.tensor_scalar(nthr[:], K.iota[:, 0:T + 1], float(-P), 0.5, ALU.mult, ALU.add))
                mark["thresholds"] = st.n
                v.wait_ge(s_load, 32)
                st(v.tensor_copy(dst_f[:], dst_i[:]))
                st.wait()
                st(v.tensor_copy(whole_i[:], dst_i[:]))
                st.wait()
                st(v.tensor_scalar(dst_i[:], dst_i[:], 7, None, ALU.arith_shift_right))
                st(v.tensor_scalar(next_i[:], next_i[:], 7, None, ALU.arith_shift_right))
                st.wait()
                st(v.tensor_tensor(junk[:], dst_i[:], next_i[:], ALU.is_gt))
                st.wait()
                v.tensor_reduce(bad[:], junk[:], AX, ALU.max).then_inc(s_flag, 1)
                v.wait_ge(s_flag, 1)

                def count(t):
                    st(v.tensor_scalar(junk[:], dst_f[:], thr[:, at(t)], 0.0, ALU.is_lt, ALU.add,
                                       accum_out=cnt[:, 0, at(t)]))
                    st.wait()
                loop(v, T + 1, count, st)
                v.wait_ge(s_act, T + 1)
                st(v.tensor_scalar(cnt[:, 1, :], cnt[:, 1, :], -0.5, ROWS2 / 2.0, ALU.mult, ALU.add))
                st.wait()
                st(v.tensor_tensor(own[:, :, 0:T], cnt[:, :, 1:T + 1], cnt[:, :, 0:T], ALU.subtract))
                st(v.tensor_scalar(own[:, 0, T:T + 1], cnt[:, 0, T:T + 1], -1.0, float(ROWS), ALU.mult, ALU.add))
                st(v.tensor_scalar(own[:, 1, T:T + 1], cnt[:, 1, T:T + 1], -1.0, float(ROWS2), ALU.mult, ALU.add))
                st.wait()
                mark["counts"] = st.n
                v.wait_ge(s_load2, 32)
                v.wait_ge(s_pre, 1)
                st(v.tensor_copy(packed2[:, :, 2], dst2_i[:]))
                st(v.tensor_copy(junk2, src2_i[:]))
                st(v.tensor_scalar(dst2_i[:], dst2_i[:], 7, None, ALU.arith_shift_right))
                st.wait()
                st(v.tensor_scalar(packed2[:, :, 1], junk2, float(N - 1), None, ALU.min))
                st(v.tensor_copy(tile2[:], dst2_i[:]))
                st.wait()
                st(v.tensor_scalar(tile2[:], tile2[:], float(T), None, ALU.min))
                v.wait_ge(s_sum, 1)
                for k, e in enumerate((e1, e2)):
                    st(v.tensor_copy(e.start[:], ps_sum[:, k * 64:k * 64 + T + 1]))
                    st(v.tensor_tensor(e.first_slot[:], ps_pre[:, k * 64:k * 64 + T + 1], own[:, k, :], ALU.subtract))
                    st.wait()
                    st(v.tensor_tensor(e.first_slot[:], e.first_slot[:], e.start[:], ALU.add))
                v.wait_ge(s_flag, 2)
                st(v.tensor_copy(flag[:], bad_all[:]))
                st.wait()

            @block.scalar
            def _(act):
                act.wait_ge(s_dve, mark["thresholds"])
                act.wait_ge(s_load2, 32)

                def count(t):
                    if not isinstance(t, int):
                        c.hold(act, s_act, t)
                    act.activation(junk3, dst2_f, ACT.Sign, bias=nthr[:, at(t)],
                                   accum_out=cnt[:, 1, at(t)]).then_inc(s_act, 1)
                act.copy(dst2_f, dst2_i[:]).then_inc(s_pre, 1)
                act.wait_ge(s_pre, 1)
                loop(act, T + 1, count)

            @block.tensor
            def _(pe):
                pe.wait_ge(s_const, 2)
                pe.wait_ge(s_dve, mark["counts"])
                for k in range(2):
                    pe.matmul(ps_sum[:, k * 64:k * 64 + T + 1], K.ones[:], cnt[:, k, :], start=True, stop=True)
                    mm = pe.matmul(ps_pre[:, k * 64:k * 64 + T + 1], K.upto[:], own[:, k, :], start=True, stop=True)
                mm.then_inc(s_sum, 1)

        with nc.Block() as block:

            @block.vector
            def _(v):
                disorder = v.value_load(flag[0:1, 0:1], min_val=0, max_val=1)
                with v.If(disorder > 0):
                    st = Steps(v, s_general)
                    st(v.tensor_copy(dst_f[:], dst_i[:]))
                    st(v.memset(packed1[:], 1 << 22))
                    st.wait()
                    st(v.tensor_scalar(dst_f[:], dst_f[:], float(T), None, ALU.min))
                    order1.begin(v, st)

                    def one(t):
                        order1.tile(v, st, K, t)
                        st.wait()
                    loop(v, T + 1, one, st)
                    order1.end(v, st)
                    st(v.tensor_copy(packed1[:, 0:ROWS, 1], src_i[:]))
                    v.tensor_copy(packed1[:, 0:ROWS, 2], whole_i[:]).then_inc(s_pool, 1)
                    st.wait()
                    mark["packed"] = st.n

            @block.gpsimd
            def _(pool):
                disorder = pool.value_load(flag[0:1, 0:1], min_val=0, max_val=1)
                with pool.If(disorder > 0):
                    pool.wait_ge(s_pool, 3)
                    pool.wait_ge(s_general, mark["packed"])
                    send1.send(pool, COLS // (2 * G), "")
                    send1.finish(pool)


def make_columns(c, K, e):
    nc = c.nc
    name, Q = e.name, e.Q
    sem = lambda x: c.sem(name + x)
    s_dve, s_rows, s_gath, s_turned, s_ids, s_io, s_k = sem("dve"), sem("rows"), c.dma_sem(name + "gath"), sem("turned"), sem("ids_"), sem("io"), sem("k")
    mark = {}
    with ExitStack() as ctx:
        sb = lambda n, sh, dt=F32: c.sb(name + n, sh, dt, ctx)
        k_i = sb("k_i", [P, Q], I32)
        first_i, last_i = sb("first_i", [P, T], I32), sb("last_i", [P, T], I32)
        first, last, some, num = (sb(x, [P, T]) for x in ("first", "last", "some", "num"))
        cum, shift, junk = sb("cum", [P, T]), sb("shift", [P, T]), sb("junk", [P, 2, T])
        kf, tk, dk, row_f, base, tid, past = (sb(x, [P, Q]) for x in ("kf", "tk", "dk", "row_f", "base", "tid", "past"))
        row_i, ids_i = sb("row_i", [P, Q], I32), sb("ids_i", [Q, P], I32)
        edges, loc = sb("edge_rows", [P, Q, 2 * P], I32), sb("loc", [P, Q, 2, P])
        banks = -(-Q // 4)
        ps = [c.ps(f"{name}ps{i}", [P, banks, 512], ctx) for i in range(2)]
        ps_ids = c.ps(name + "ps_ids", [P, 512], ctx)
        with nc.Block() as block:

            @block.gpsimd
            def _(pool):
                pool.iota(k_i[:], [[P, Q]], base=0, channel_multiplier=1).then_inc(s_k, 1)
                pool.wait_ge(s_rows, 1)
                for q in range(Q):
                    pool.indirect_dma_start(
                        out=edges[:, q, :], out_offset=None, in_=e.dram.rearrange("(r p) e -> r (p e)", p=P),
                        in_offset=bass.IndirectOffsetOnAxis(ap=row_i[:, q:q + 1], axis=0)).then_inc(s_gath, 16)

            @block.vector
            def _(v):
                st = Steps(v, s_dve)
                start = e.start

                def do(ins):
                    st(ins)
                    st.wait()
                v.wait_ge(s_k, 1)
                st(v.tensor_copy(kf[:], k_i[:]))
                st(v.tensor_copy(first_i[:], start[:, 0:T]))
                st(v.tensor_scalar(last_i[:], start[:, 1:T + 1], float(P - 1), None, ALU.add))
                st(v.tensor_tensor(some[:], start[:, 1:T + 1], start[:, 0:T], ALU.is_gt))
                st.wait()
                st(v.tensor_scalar(first_i[:], first_i[:], 7, None, ALU.arith_shift_right))
                st(v.tensor_scalar(last_i[:], last_i[:], 7, None, ALU.arith_shift_right))
                st.wait()
                st(v.tensor_copy(first[:], first_i[:]))
                st(v.tensor_copy(last[:], last_i[:]))
                st.wait()
                do(v.tensor_tensor(num[:], last[:], first[:], ALU.subtract))
                do(v.tensor_tensor(num[:], num[:], some[:], ALU.mult))
                do(v.tensor_tensor_scan(cum[:], K.ones[:, 0:T], num[:], 0.0, ALU.mult, ALU.add))
                do(v.tensor_tensor(shift[:], num[:], cum[:], ALU.subtract))
                do(v.tensor_tensor(shift[:], shift[:], first[:], ALU.add))
                for q in range(Q):
                    do(v.tensor_scalar(junk[:, q % 2, :], cum[:], kf[:, q:q + 1], 0.0, ALU.is_le, ALU.add,
                                       accum_out=tk[:, q:q + 1]))
                    do(v.scalar_tensor_tensor(junk[:, q % 2, :], K.iota[:, 0:T], tk[:, q:q + 1], shift[:],
                                              ALU.is_equal, ALU.mult, accum_out=dk[:, q:q + 1]))
                st(v.tensor_tensor(row_f[:], kf[:], dk[:], ALU.add))
                st(v.tensor_scalar(past[:], tk[:], float(T), float(1 << 22), ALU.is_ge, ALU.mult))
                st(v.tensor_scalar(base[:], tk[:], float(P), None, ALU.mult))
                st(v.tensor_scalar(tid[:], tk[:], float(T - 1), None, ALU.min))
                st.wait()
                st(v.tensor_tensor(base[:], base[:], past[:], ALU.add))
                do(v.tensor_scalar(row_f[:], row_f[:], float(e.rows - 1), None, ALU.min))
                v.tensor_copy(row_i[:], row_f[:]).then_inc(s_rows, 1)
                v.wait_ge(s_gath, 16 * Q)
                for side in range(2):
                    st(v.tensor_copy(loc[:, :, side, :], edges[:].rearrange("p q (e s) -> p q s e", s=2)[:, :, side, :]))
                st.wait()
                for q in range(Q):
                    st(v.tensor_scalar(loc[:, q, 1, :], loc[:, q, 1, :], base[:, q:q + 1], None, ALU.subtract))
                mark["locals"] = st.n
                v.wait_ge(s_turned, 1)
                for q in range(Q):
                    for side, cols in ((0, e.src_cols), (1, e.dst_cols)):
                        st(v.tensor_copy(cols[:, q * P:(q + 1) * P], ps[side][:, q // 4, (q % 4) * P:(q % 4 + 1) * P]))
                v.tensor_copy(ids_i[:], ps_ids[0:Q, 0:P]).then_inc(s_ids, 1)

            @block.sync
            def _(sp):
                sp.wait_ge(s_ids, 1)
                sp.dma_start(e.ids_dram, ids_i[:]).then_inc(s_io, 16)
                sp.wait_ge(s_io, 16)
                sp.dma_start(e.ids[:], e.ids_dram.rearrange("q k -> (q k)").rearrange("(a k) -> a k", a=1)).then_inc(s_io, 16)
                sp.wait_ge(s_io, 32)

            @block.tensor
            def _(pe):
                pe.wait_ge(s_dve, mark["locals"])
                for q in range(Q):
                    for side in range(2):
                        pe.transpose(ps[side][:, q // 4, (q % 4) * P:(q % 4 + 1) * P], loc[:, q, side, :], K.ident[:])
                pe.transpose(ps_ids[0:Q, 0:P], tid[:], K.ident[:]).then_inc(s_turned, 1)


class Base:

    def __init__(self, weights, bias, out):
        self.weights, self.bias, self.out, self.n = weights, bias, out, out.shape[1]


def project(c, name, K, h, w_t, w_nat, attn_dram, heads, table, base=None, spare=None, order=None):
    nc = c.nc
    one = heads == 1
    width = table.shape[1]
    nb = base.n if base else 0
    sem = lambda n: c.sem(name + n)
    s_w, s_fold, s_folded, s_beside, s_hT, s_hTc = sem("w"), sem("fold"), sem("folded"), sem("beside"), sem("hT"), sem("hTc")
    s_mm, s_out, s_store, s_dve, s_max, s_aux = sem("mm"), sem("out"), [sem("store0"), sem("store1")], sem("dve"), sem("max"), sem("aux")
    s_rows, mark = sem("rows"), {}
    nout = 3 + (1 if one else 0) + (1 if base else 0)
    nf = D + 2 * heads
    with ExitStack() as ctx:
        sb = lambda n, sh, dt=F32: c.sb(name + n, sh, dt, ctx)
        w = sb("w", [P, 2, nf])
        wn, attn = sb("wn", [P, 2, D]), sb("attn", [P, 2, 2])
        fold, off_i, off, ge = sb("fold", [P, 2, 2, heads]), sb("off_i", [P, 2, heads], I32), sb("off", [P, 2, heads]), sb("ge", [P, 2, heads])
        rows, hT, stage = sb("rows", [P, 2, D]), sb("hT", [P, 2, D]), sb("stage", [P, 2, width])
        elv, elm, gmax = sb("elv", [P, T, heads]), sb("elm", [P, heads]), sb("gmax", [P, heads])
        vm = sb("vm", [P, 2])
        if nb:
            wb, bstage = sb("wb", [P, 2, nb]), sb("bstage", [P, 2, nb])
            bias = sb("bias", [1, nb]) if base.bias is not None else None
        ps_t = [c.ps(f"{name}pt{i}", [P, D], ctx) for i in range(2)]
        ps_f = [c.ps(f"{name}pf{i}", [P, 512], ctx) for i in range(2)]
        ps_b = [c.ps(f"{name}pb{i}", [P, 512], ctx) for i in range(2)] if nb else None
        nload = 16 * (3 + (1 if nb else 0) + (1 if nb and bias is not None else 0))
        with nc.Block() as block:

            @block.sync
            def _(sp):
                sp.dma_start(w[:, :, 0:D], w_t.rearrange("(c p) n -> p c n", p=P)).then_inc(s_w, 16)
                sp.dma_start(wn[:], w_nat.rearrange("(c p) n -> p c n", p=P)).then_inc(s_w, 16)
                sp.dma_start(attn[:], attn_dram).then_inc(s_w, 16)
                if nb:
                    sp.dma_start(wb[:], base.weights.rearrange("(c p) n -> p c n", p=P)).then_inc(s_w, 16)
                    if bias is not None:
                        sp.dma_start(bias[:], base.bias).then_inc(s_w, 16)
                per = 32 if nb else 16

                def store(t, s, i):
                    sp.wait_ge(s_out, (t + 1) * nout)
                    sp.dma_start(table[at(t * P, P), :], stage[:, s, :]).then_inc(s_store[s], 16)
                    if nb:
                        sp.dma_start(base.out[at(t * P, P), :], bstage[:, s, :]).then_inc(s_store[s], 16)
                tiles(store, sp)
                for s in range(2):
                    sp.wait_ge(s_store[s], per * ((T + 1 - s) // 2))

            @block.gpsimd
            def _(pool):
                pool.iota(off_i[:], [[P, 2], [-(D // heads), heads]], base=0, channel_multiplier=1).then_inc(s_aux, 1)
                pool.memset(stage[:], 1.0).then_inc(s_aux, 1)
                if spare:
                    spare(pool)
                pool.wait_ge(s_max, 1)
                pool.partition_all_reduce(gmax[:], elm[:], P, RED.max).then_inc(s_max, 1)

            @block.vector
            def _(v):
                st = Steps(v, s_dve)
                v.wait_ge(s_aux, 2)
                st(v.tensor_copy(off[:], off_i[:]))
                v.wait_ge(s_w, nload)
                st.wait()
                st(v.tensor_scalar(ge[:], off[:], 0.0, None, ALU.is_ge))
                st(v.tensor_scalar(off[:], off[:], float(D // heads), None, ALU.is_lt))
                st.wait()
                st(v.tensor_tensor(ge[:], ge[:], off[:], ALU.mult))
                st.wait()
                for side in range(2):
                    ins = v.tensor_tensor(fold[:, side], ge[:], attn[:, :, side:side + 1].to_broadcast([P, 2, heads]), ALU.mult)
                    ins.then_inc(s_fold, 1)
                if order:
                    order.begin(v, st)
                    mark["ordered"] = st.n
                    steps = order.STEPS

                def rows_and_order(t, s, i):
                    place_rows(v, h, t, rows[:, s, :], s_rows, s_hT)
                    if order:
                        st.turn(t, mark["ordered"], steps)
                        order.tile(v, st, K, t)
                        st.wait()
                tiles(rows_and_order, v)
                if order:
                    st.leave(T, mark["ordered"], steps)
                    order.tile(v, st, K, T)
                    st.wait()
                    order.end(v, st)
                v.wait_ge(s_out, T * nout)
                st(v.tensor_scalar(vm[:, 0:1], K.part[:], float(LAST), None, ALU.is_lt))
                st.wait()
                st(v.tensor_scalar(vm[:, 1:2], vm[:, 0:1], BIG, -BIG, ALU.mult, ALU.add))
                st.wait()
                st(v.tensor_scalar(elv[:, T - 1, :], elv[:, T - 1, :], vm[:, 0:1], vm[:, 1:2], ALU.mult, ALU.add))
                st.wait()
                v.tensor_reduce(elm[:], elv[:].rearrange("p t h -> p h t"), AX, ALU.max).then_inc(s_max, 1)
                v.wait_ge(s_max, 2)
                m = K.er[:, :, heads:2 * heads]
                st(v.tensor_tensor(m, K.er[:, :, 0:heads], gmax[:].unsqueeze(1).to_broadcast([P, T, heads]), ALU.add))
                st.wait()
                st(v.scalar_tensor_tensor(m, m, 0.2, m, ALU.mult, ALU.max))

            @block.tensor
            def _(pe):
                pe.wait_ge(s_fold, 2)
                pe.wait_ge(s_w, nload)
                for k in range(2):
                    for side in range(2):
                        for o in range(2):
                            mm = pe.matmul(ps_f[0][:, (2 * k + side) * heads:(2 * k + side + 1) * heads],
                                           wn[:, o, k * P:(k + 1) * P], fold[:, side, o, :], start=(o == 0), stop=(o == 1))
                mm.then_inc(s_folded, 1)
                pe.wait_ge(s_beside, 4)

                def turn(t, s, i):
                    pe.wait_ge(s_rows, t + 1)
                    if not early(t):
                        pe.wait_ge(s_hTc, t - 1)
                    for k in range(2):
                        mm = pe.transpose(ps_t[s][:, k * P:(k + 1) * P], rows[:, s, k * P:(k + 1) * P], K.ident[:])
                    mm.then_inc(s_hT, 1)

                def tile(t, s, i):
                    pe.wait_ge(s_hTc, t + 1)
                    if not early(t):
                        pe.wait_ge(s_out, (t - 1) * nout)
                    for k in range(2):
                        mm = pe.matmul(ps_f[s][:, 0:nf], hT[:, s, k * P:(k + 1) * P], w[:, k, :], start=(k == 0), stop=(k == 1))
                    if nb:
                        for k in range(2):
                            mm = pe.matmul(ps_b[s][:, 0:nb], hT[:, s, k * P:(k + 1) * P], wb[:, k, :], start=(k == 0), stop=(k == 1 and bias is None))
                        if bias is not None:
                            mm = pe.matmul(ps_b[s][:, 0:nb], K.ones[0:1, :], bias[:], start=False, stop=True)
                    mm.then_inc(s_mm, 1)
                ahead_tiles(turn, tile, pe)

            @block.scalar
            def _(act):
                act.wait_ge(s_folded, 1)
                for k in range(2):
                    for side in range(2):
                        ins = act.copy(w[:, k, D + side * heads:D + (side + 1) * heads],
                                       ps_f[0][:, (2 * k + side) * heads:(2 * k + side + 1) * heads])
                        ins.then_inc(s_beside, 1)

                def turned(t, s, i):
                    act.wait_ge(s_hT, t + 1)
                    if not early(t):
                        act.wait_ge(s_mm, t - 1)
                    act.copy(hT[:, s, :], ps_t[s][:]).then_inc(s_hTc, 1)

                def tile(t, s, i):
                    act.wait_ge(s_mm, t + 1)
                    if isinstance(t, int) and t == 0:
                        act.wait_ge(s_aux, 2)
                    if not early(t):
                        act.wait_ge(s_store[s], i * (32 if nb else 16))
                    if one:
                        ins = [act.copy(stage[:, s, 0:D], ps_f[s][:, 0:D]), act.copy(stage[:, s, D + 1:D + 2], ps_f[s][:, D:D + 1])]
                    else:
                        ins = [act.copy(stage[:, s, 0:D + heads], ps_f[s][:, 0:D + heads])]
                    ins += [act.copy(elv[:, at(t), :], ps_f[s][:, D:D + heads].unsqueeze(1)),
                            act.copy(K.er[:, at(t), 0:heads], ps_f[s][:, D + heads:D + 2 * heads].unsqueeze(1))]
                    if nb:
                        ins += [act.copy(bstage[:, s, :], ps_b[s][:, 0:nb])]
                    for x in ins:
                        x.then_inc(s_out, 1)
                ahead_tiles(turned, tile, act)


def attend(c, name, K, edges, table, heads, F, er, acc, side=None):
    nc = c.nc
    one = heads == 1
    width = table.shape[1]
    nr = F + 1 if one else F + heads + 1
    el = F + 1 if one else F
    slot = F + heads + 1 if not one else F + 2
    R, NG = edges.R, edges.NG
    TURNS = NG // R
    helped = {8: 2, 4: 4}.get(heads, 0) if F == D else 0
    mid = (G - helped) // 2
    narrow_ = F < D
    MB = 4
    sem = lambda n: c.sem(name + n)
    s_stage, s_M, s_T, s_MT, s_er, s_z, s_w = sem("stage"), sem("M"), sem("T"), sem("MT"), sem("er"), sem("z"), sem("w")
    s_sc, s_main, s_add, s_init = sem("sc"), sem("main"), sem("add"), sem("init")
    s_gat = [c.dma_sem(f"{name}gat{r}") for r in range(R)]
    s_zd, s_sa = sem("zd"), sem("sa")
    with ExitStack() as ctx:
        sb = lambda n, sh, dt=F32: c.sb(name + n, sh, dt, ctx)
        idx = sb("idx", [P, R, G], I32)
        ring = sb("ring", [P, R, G, slot])
        M, MT = sb("M", [P, MB, G, P]), sb("MT", [P, 2, G, P])
        z, wt = sb("z", [P, 2, G, heads]), sb("wt", [P, 2, G, 1])
        ps_T = [c.ps(f"{name}pT{i}", [P, 4, P], ctx) for i in range(2)]
        if narrow_:
            ps_eo = [c.ps(f"{name}{x}", [P, 512], ctx) for x in ("pe", "po")]
            ps_e = 2 * [ps_eo[0][:, 0:G * 2 * heads].rearrange("p (g h) -> p g h", g=G)]
            ps_o = [ps_eo[1][:, k * 64:k * 64 + nr] for k in range(G)]
        else:
            ps_e = [c.ps(f"{name}pe{i}", [P, G, 2 * heads], ctx) for i in range(2)]
            ps_o = 2 * [c.ps(f"{name}po{i}", [P, 512], ctx) for i in range(4)]
        if side:
            side.place(c, ctx)
        first = lambda i: isinstance(i, int) and i == 0
        below = lambda g, n: isinstance(g, int) and g < n
        with nc.Block() as block:

            if side:
                @block.sync
                def _(sp):
                    side.sync(sp)

            @block.gpsimd
            def _(pool):
                def turn(i):
                    for r in range(R):
                        g = i * R + r
                        c.hold(pool, s_stage, g + 1)
                        if not first(i):
                            c.hold(pool, s_main, (g - R + 1) * G)
                        else:
                            pool.wait_ge(s_init, 1)
                        for k in range(G):
                            pool.indirect_dma_start(
                                out=ring[:, r, k, 0:width], out_offset=None, in_=table,
                                in_offset=bass.IndirectOffsetOnAxis(ap=idx[:, r, k:k + 1], axis=0)).then_inc(s_gat[r], 16)
                loop(pool, TURNS, turn, peel=bool(side))

            @block.scalar
            def _(act):
                def stage(g, r):
                    act.copy(idx[:, r, :], edges.src_cols[:, at(g * G, G)]).then_inc(s_stage, 1)

                def turned(g, b):
                    for half in range(2):
                        act.wait_ge(s_T, g * 2 + half + 1)
                        act.copy(MT[:, b, 4 * half:4 * half + 4, :], ps_T[half][:]).then_inc(s_MT, 1)
                for g in range(AHEAD):
                    stage(g, g)
                turned(0, 0)

                def turn(i):
                    for r in range(R):
                        g = i * R + r
                        r2 = (r + AHEAD) % R
                        if not (first(i) and r + AHEAD < R):
                            act.wait_ge(s_gat[r2], (i + (r + AHEAD) // R) * 16 * G)
                        stage(g + AHEAD, r2)
                        act.wait_ge(s_z, g + 1)
                        if one:
                            act.activation(wt[:, r % 2], z[:, r % 2], ACT.Exp).then_inc(s_w, 1)
                            act.wait_ge(s_T, g * 2 + 2)
                            act.wait_ge(s_w, g + 1)
                            for k in range(G):
                                act.activation(M[:, r % MB, k, :], M[:, r % MB, k, :], ACT.Copy, scale=wt[:, r % 2, k, :]).then_inc(s_sc, 1)
                        else:
                            act.activation(ring[:, r, :, F:F + heads], z[:, r % 2], ACT.Exp).then_inc(s_w, 1)
                            if helped:
                                act.wait_ge(s_w, g + 1)
                            for k in range(G - helped, G):
                                for h in range(heads):
                                    f = ring[:, r, k, h * (F // heads):(h + 1) * (F // heads)]
                                    act.activation(f, f, ACT.Copy, scale=ring[:, r, k, F + h:F + h + 1]).then_inc(s_sa, 1)
                        turned(g + 1, (r + 1) % 2)
                        if side:
                            side.scalar(act, i, r)
                loop(act, TURNS, turn, peel=bool(side))

            @block.tensor
            def _(pe):
                def turn_hots(g, m):
                    for k in range(G):
                        if k % 4 == 0:
                            pe.wait_ge(s_M, g * 2 + k // 4 + 1)
                            if not below(g, 1):
                                pe.wait_ge(s_MT, g * 2 - 1 + k // 4)
                        mm = pe.transpose(ps_T[k // 4][:, k % 4, :], M[:, m, k, :], K.ident[:])
                        if k % 4 == 3:
                            mm.then_inc(s_T, 1)

                def dest_terms(g, b):
                    _, ids = nc.values_load_multi_w_load_instructions(
                        edges.ids[0:1, at(g * G, G)], engines=[PE], min_val=0, max_val=T - 1,
                        skip_runtime_bounds_check_because="tile numbers are cut to T - 1")
                    if narrow_:
                        if not below(g, 1):
                            pe.wait_ge(s_z, g)
                    elif not below(g, 2):
                        pe.wait_ge(s_z, g - 1)
                    for k in range(G):
                        if k % 4 == 0:
                            pe.wait_ge(s_MT, g * 2 + k // 4 + 1)
                        mm = pe.matmul(ps_e[b][:, k, :], MT[:, b, k, :],
                                       er[:, at(ids[k]), 0:2 * heads].rearrange("p a h -> p (a h)"), start=True, stop=True)
                    mm.then_inc(s_er, 1)
                turn_hots(0, 0)
                dest_terms(0, 0)

                def turn(i):
                    for r in range(R):
                        g = i * R + r
                        turn_hots(g + 1, (r + 1) % MB)
                        if side:
                            side.tensor(pe, i, r, 0)
                        dest_terms(g + 1, (r + 1) % 2)
                        if side:
                            side.tensor(pe, i, r, 1)
                        for k in range(G):
                            if one:
                                pe.wait_ge(s_sc, g * G + k + 1)
                            elif k in (0, mid):
                                pe.wait_ge(s_sc, g * 2 + k // mid + 1)
                            elif k >= G - helped:
                                pe.wait_ge(s_sa, (g * helped + k - (G - helped) + 1) * heads)
                            if narrow_:
                                if k == 0 and not (first(i) and r == 0):
                                    pe.wait_ge(s_add, g * G)
                            elif not (first(i) and r == 0 and k < 4):
                                pe.wait_ge(s_add, g * G + k - 3)
                            pe.matmul(ps_o[k][:, 0:nr], M[:, r % MB, k, :], ring[:, r, k, 0:nr],
                                      start=True, stop=True).then_inc(s_main, 1)
                loop(pe, TURNS, turn, peel=bool(side))

            @block.vector
            def _(v):
                st = Steps(v, s_zd)
                v.memset(ring[:], 1.0).then_inc(s_init, 1)
                st(v.memset(acc[:], 0.0))

                def hots(g, m):
                    for half in range(2):
                        cols = edges.dst_cols[:, at(g * G + 4 * half, 4)].unsqueeze(2).to_broadcast([P, 4, P])
                        v.tensor_tensor(M[:, m, 4 * half:4 * half + 4, :], K.iota[:].unsqueeze(1).to_broadcast([P, 4, P]), cols,
                                        ALU.is_equal).then_inc(s_M, 1)

                def load_ids(g):
                    return nc.values_load_multi_w_load_instructions(
                        edges.ids[0:1, at(g * G, G)], engines=[DVE], min_val=0, max_val=T - 1,
                        skip_runtime_bounds_check_because="tile numbers are cut to T - 1")[1]

                def add(g, k, tid):
                    if not narrow_:
                        v.wait_ge(s_main, g * G + k + 1)
                    elif k == 0:
                        v.wait_ge(s_main, (g + 1) * G)
                    if not (below(g, 1) and k == 0):
                        v.wait_ge(s_add, g * G + k)
                    a = acc[:, at(tid), 0:nr].rearrange("p a f -> p (a f)")
                    v.tensor_tensor(a, a, ps_o[k][:, 0:nr], ALU.add).then_inc(s_add, 1)

                hots(0, 0)
                if MB == 4:
                    hots(1, 1)

                def turn(i):
                    for r in range(R):
                        g, b = i * R + r, r % 2
                        if not (first(i) and r == 0):
                            ids = load_ids(g - 1)
                        v.wait_ge(s_gat[r], (i + 1) * 16 * G)
                        v.wait_ge(s_er, g + 1)
                        zb = z[:, b]
                        st(v.tensor_tensor(zb, ring[:, r, :, el:el + heads], ps_e[b][:, :, 0:heads], ALU.add))
                        st.wait()
                        st(v.scalar_tensor_tensor(zb, zb, 0.2, zb, ALU.mult, ALU.max))
                        st.wait()
                        v.tensor_tensor(zb, zb, ps_e[b][:, :, heads:2 * heads], ALU.subtract).then_inc(s_z, 1)
                        if MB == 4:
                            hots(g + 2, (r + 2) % MB)
                        for k in range(G):
                            if not (first(i) and r == 0):
                                add(g - 1, k, ids[k])
                        if MB == 2:
                            hots(g + 1, (r + 1) % MB)
                        if side:
                            side.vector_rows(v, i, r)
                        if not one:
                            v.wait_ge(s_w, g + 1)
                            for half in range(2):
                                hs = slice(mid * half, mid * half + mid)
                                f = ring[:, r, hs, 0:F].rearrange("p k (h f) -> p k h f", h=heads)
                                v.tensor_tensor(f, f, ring[:, r, hs, F:F + heads].unsqueeze(3).to_broadcast([P, mid, heads, F // heads]),
                                                ALU.mult).then_inc(s_sc, 1)
                        if side:
                            side.vector_results(v, i, r)
                st.wait()
                loop(v, TURNS, turn, st, peel=bool(side))
                ids = load_ids(NG - 1)
                for k in range(G):
                    add(NG - 1, k, ids[k])
                if side:
                    side.vector_results(v, TURNS, 0)


def combine(c, name, K, acc, heads, out, bias=None, bases=(), residual=False, relu=False, degree=False, spare=None):
    nc = c.nc
    C = 7
    sem = lambda n: c.sem(name + n)
    s_bias, s_dve, s_load = sem("bias"), sem("dve"), [sem("load0"), sem("load1")]
    per = {}
    with ExitStack() as ctx:
        sb = lambda n, sh, dt=F32: c.sb(name + n, sh, dt, ctx)
        rs = sb("rs", [P, T, heads])
        brow = sb("brow", [P, D]) if bias is not None else None
        ld = sb("ld", [P, 2, len(bases), C, D]) if bases else None
        with nc.Block() as block:

            @block.vector
            def _(v):
                st = Steps(v, s_dve)
                st(v.tensor_scalar(rs[:], acc[:, :, D:D + heads], 1e-37, None, ALU.max))
                if degree:
                    st(v.tensor_scalar(K.norm[:], acc[:, :, D + heads], 1.0, None, ALU.max))
                st.wait()
                st(v.reciprocal(rs[:], rs[:]))
                if degree:
                    st(v.reciprocal(K.norm[:], K.norm[:]))
                if bias is not None:
                    v.wait_ge(s_bias, 16)
                st.wait()
                per["before"] = st.n

                def seven(i, s):
                    y = acc[:, at(i * C, C), 0:D]
                    yh = y.rearrange("p t (h f) -> p t h f", h=heads)
                    st(v.tensor_tensor(yh, yh, rs[:, at(i * C, C), :].unsqueeze(3).to_broadcast([P, C, heads, D // heads]), ALU.mult))
                    st.wait()
                    if bias is not None:
                        st(v.tensor_tensor(y, y, brow[:].unsqueeze(1).to_broadcast([P, C, D]), ALU.add))
                    if bases:
                        v.wait_ge(s_load[s], (i // 2 + 1) * 16 * len(bases))
                        b = ld[:, s, 0]
                        if len(bases) > 1:
                            st(v.tensor_tensor(b, b, ld[:, s, 1], ALU.add))
                            st.wait()
                        st(v.tensor_tensor(b, b, K.norm[:, at(i * C, C)].unsqueeze(2).to_broadcast([P, C, D]), ALU.mult))
                        st.wait()
                        st(v.tensor_tensor(y, y, b, ALU.add))
                    st.wait()
                    o = out[:, at(i * C, C), :]
                    if relu:
                        st(v.tensor_scalar(o, y, 0.0, None, ALU.max))
                    elif residual:
                        st(v.tensor_tensor(o, o, y, ALU.add))
                    st.wait()
                for i in range(T // C):
                    seven(i, i % 2)
                    per.setdefault("period", st.n - per["before"])
            if spare:
                @block.gpsimd
                def _(pool):
                    spare(pool)
            if bias is not None or bases:
                @block.sync
                def _(sp):
                    if bias is not None:
                        sp.dma_start(brow[:], bias.partition_broadcast(P)).then_inc(s_bias, 16)
                    for i in range(T // C) if bases else ():
                        if i >= 2:
                            sp.wait_ge(s_dve, per["before"] + (i - 1) * per["period"])
                        for n, b in enumerate(bases):
                            sp.dma_start(ld[:, i % 2, n], b[i * C * P:(i + 1) * C * P, :].rearrange("(t p) d -> p t d", p=P)) \
                                .then_inc(s_load[i % 2], 16)
                    if bias is not None:
                        sp.wait_ge(s_bias, 16)


def layernorm(c, name, X, H):
    nc = c.nc
    s_dve, s_sqrt = c.sem(name + "dve"), c.sem(name + "sqrt")
    mark = {}
    with ExitStack() as ctx:
        stats = c.sb(name + "stats", [P, T, 6], F32, ctx)
        mean, m2, rstd = (c.sb(name + x, [P, T], F32, ctx) for x in ("mean", "m2", "rstd"))
        with nc.Block() as block:

            @block.vector
            def _(v):
                st = Steps(v, s_dve)
                rows = lambda A, t: A[:, at(t), :].rearrange("p a f -> p (a f)")
                loop(v, T, lambda t: st(v.bn_stats(rows(stats, t), rows(X, t))), st)
                st.wait()
                st(v.tensor_tensor(mean[:], stats[:, :, 1], stats[:, :, 4], ALU.add))
                st(v.tensor_tensor(rstd[:], stats[:, :, 1], stats[:, :, 4], ALU.subtract))
                st(v.tensor_tensor(m2[:], stats[:, :, 2], stats[:, :, 5], ALU.add))
                st.wait()
                st(v.tensor_scalar(mean[:], mean[:], 0.5, None, ALU.mult))
                st(v.tensor_tensor(rstd[:], rstd[:], rstd[:], ALU.mult))
                st(v.tensor_scalar(m2[:], m2[:], 1.0 / D, LN_EPS, ALU.mult, ALU.add))
                st.wait()
                st(v.scalar_tensor_tensor(rstd[:], rstd[:], 0.25, m2[:], ALU.mult, ALU.add))
                mark["var"] = st.n
                v.wait_ge(s_sqrt, 1)
                st(v.reciprocal(rstd[:], rstd[:]))
                st.wait()

                def scale(t):
                    st(v.tensor_scalar(rows(H, t), rows(X, t), mean[:, at(t)], rstd[:, at(t)], ALU.subtract, ALU.mult))
                loop(v, T, scale, st)
                st.wait()

            @block.scalar
            def _(act):
                act.wait_ge(s_dve, mark["var"])
                act.activation(rstd[:], rstd[:], ACT.Sqrt).then_inc(s_sqrt, 1)


def narrow(c, name, K, h, weights, out, spare=None):
    nc = c.nc
    n = weights.shape[1]
    s_w, s_hT, s_hTc, s_mm, s_out, s_rows = (c.sem(name + x) for x in ("w", "hT", "hTc", "mm", "out", "rows"))
    with ExitStack() as ctx:
        w, hT = c.sb(name + "w", [P, 2, n], F32, ctx), c.sb(name + "hT", [P, 2, D], F32, ctx)
        rows = c.sb(name + "rows", [P, 2, D], F32, ctx)
        ps_t = [c.ps(f"{name}pt{i}", [P, D], ctx) for i in range(2)]
        ps_f = [c.ps(f"{name}pf{i}", [P, n], ctx) for i in range(2)]
        with nc.Block() as block:

            if spare:
                @block.gpsimd
                def _(pool):
                    spare(pool)

            @block.sync
            def _(sp):
                sp.dma_start(w[:], weights.rearrange("(c p) n -> p c n", p=P)).then_inc(s_w, 16)
                sp.wait_ge(s_w, 16)

            @block.vector
            def _(v):
                tiles(lambda t, s, i: place_rows(v, h, t, rows[:, s, :], s_rows, s_hT), v)

            @block.tensor
            def _(pe):
                pe.wait_ge(s_w, 16)

                def turn(t, s, i):
                    pe.wait_ge(s_rows, t + 1)
                    if not early(t):
                        pe.wait_ge(s_hTc, t - 1)
                    for k in range(2):
                        mm = pe.transpose(ps_t[s][:, k * P:(k + 1) * P], rows[:, s, k * P:(k + 1) * P], K.ident[:])
                    mm.then_inc(s_hT, 1)

                def tile(t, s, i):
                    pe.wait_ge(s_hTc, t + 1)
                    if not early(t):
                        pe.wait_ge(s_out, t - 1)
                    for k in range(2):
                        mm = pe.matmul(ps_f[s][:], hT[:, s, k * P:(k + 1) * P], w[:, k, :], start=(k == 0), stop=(k == 1))
                    mm.then_inc(s_mm, 1)
                ahead_tiles(turn, tile, pe)

            @block.scalar
            def _(act):
                def turned(t, s, i):
                    act.wait_ge(s_hT, t + 1)
                    if not early(t):
                        act.wait_ge(s_mm, t - 1)
                    act.copy(hT[:, s, :], ps_t[s][:]).then_inc(s_hTc, 1)

                def tile(t, s, i):
                    act.wait_ge(s_mm, t + 1)
                    act.copy(out[:, at(t), :], ps_f[s][:].unsqueeze(1)).then_inc(s_out, 1)
                ahead_tiles(turned, tile, act)


def first_of_best(v, st, K, val, n, best, eq, low):
    v_b = lambda a: a.unsqueeze(2).to_broadcast([P, T, n])
    io = K.iota_low[:, P - n:P].unsqueeze(1).to_broadcast([P, T, n])
    st(v.tensor_reduce(best, val, AX, ALU.max))
    st.wait()
    st(v.tensor_tensor(eq, val, v_b(best), ALU.is_equal))
    st.wait()
    st(v.tensor_tensor(eq, eq, io, ALU.mult))
    st.wait()
    st(v.tensor_reduce(low, eq, AX, ALU.min))
    st.wait()
    st(v.tensor_tensor(eq, io, v_b(low), ALU.is_equal))
    st.wait()


def route(c, K, lg, gate_b, H, slot_rows):
    nc = c.nc
    n = EXPERTS
    C = 7
    s_b, s_dve, s_exp, s_cum, s_stage = (c.sem("r_" + x) for x in ("b", "dve", "exp", "cum", "stage"))
    s_sent = c.dma_sem("r_sent")
    mark = {}
    with ExitStack() as ctx:
        sb = lambda nm, sh, dt=F32: c.sb("r_" + nm, sh, dt, ctx)
        gb, pr, eq = sb("gb", [P, n]), sb("pr", [P, T, n]), sb("eq", [P, T, n])
        mx, low, sm = sb("mx", [P, T]), sb("low", [P, T]), sb("sm", [P, T])
        exc, pos, kept, slot = sb("exc", [P, T, n]), sb("pos", [P, T]), sb("kept", [P, T]), sb("slot", [P, T])
        send, stage, idx = sb("send", [P, T]), sb("stage", [P, C, D]), sb("idx", [P, C], I32)
        ps_cum, ps_tot = c.ps("ps_cum", [P, T * n], ctx), c.ps("ps_tot", [P, T * n], ctx)
        b3 = lambda a: a.unsqueeze(2).to_broadcast([P, T, n])
        with nc.Block() as block:

            @block.sync
            def _(sp):
                sp.dma_start(gb[:], gate_b.partition_broadcast(P)).then_inc(s_b, 16)
                sp.wait_ge(s_b, 16)

            @block.vector
            def _(v):
                st = Steps(v, s_dve)
                v.wait_ge(s_b, 16)
                st(v.tensor_tensor(lg[:], lg[:], gb[:].unsqueeze(1).to_broadcast([P, T, n]), ALU.add))
                st.wait()
                st(v.tensor_reduce(mx[:], lg[:], AX, ALU.max))
                st.wait()
                st(v.tensor_tensor(lg[:], lg[:], b3(mx[:]), ALU.subtract))
                mark["exp"] = st.n
                v.wait_ge(s_exp, 1)
                st(v.tensor_reduce(sm[:], pr[:], AX, ALU.add))
                st.wait()
                st(v.reciprocal(sm[:], sm[:]))
                st.wait()
                st(v.tensor_tensor(pr[:], pr[:], b3(sm[:]), ALU.mult))
                st.wait()
                first_of_best(v, st, K, pr[:], n, mx[:], eq[:], low[:])
                mark["hot"] = st.n
                v.wait_ge(s_cum, 1)
                for e in range(n):
                    st(v.tensor_tensor_scan(exc[:, :, e], K.ones[:, 0:T], ps_tot[:].rearrange("p (t n) -> p t n", n=n)[:, :, e],
                                            0.0, ALU.mult, ALU.add))
                st.wait()
                st(v.tensor_tensor(exc[:], exc[:], ps_tot[:].rearrange("p (t n) -> p t n", n=n), ALU.subtract))
                st.wait()
                st(v.tensor_tensor(exc[:], exc[:], ps_cum[:].rearrange("p (t n) -> p t n", n=n), ALU.add))
                st.wait()
                st(v.tensor_tensor(exc[:], exc[:], eq[:], ALU.mult))
                st.wait()
                st(v.tensor_reduce(pos[:], exc[:], AX, ALU.add))
                st.wait()
                st(v.tensor_scalar(pos[:], pos[:], -1.0, None, ALU.add))
                st(v.tensor_scalar(slot[:], low[:], float(CPAD), float(CPAD * n), ALU.mult, ALU.add))
                st.wait()
                st(v.tensor_scalar(kept[:], pos[:], float(CAP), None, ALU.is_lt))
                st(v.tensor_tensor(slot[:], slot[:], pos[:], ALU.add))
                st.wait()
                st(v.tensor_scalar(sm[:, 0:1], K.part[:], float(LAST), None, ALU.is_lt))
                st.wait()
                st(v.tensor_tensor(kept[:, T - 1:T], kept[:, T - 1:T], sm[:, 0:1], ALU.mult))
                st.wait()
                st(v.tensor_scalar(send[:], slot[:], float(-SLOTS), None, ALU.add))
                st(v.tensor_tensor(slot[:], slot[:], kept[:], ALU.mult))
                st.wait()
                st(v.tensor_tensor(send[:], send[:], kept[:], ALU.mult))
                st(v.tensor_copy(K.slot[:], slot[:]))
                st(v.tensor_tensor(K.share[:], mx[:], kept[:], ALU.mult))
                st.wait()
                st(v.tensor_scalar(send[:], send[:], float(SLOTS), None, ALU.add))
                st.wait()

                def turn(i):
                    if not isinstance(i, int):
                        v.wait_ge(s_sent, i * 16 * C)
                    v.tensor_copy(idx[:], send[:, at(i * C, C)]).then_inc(s_stage, 1)
                    v.tensor_copy(stage[:], H[:, at(i * C, C), :]).then_inc(s_stage, 1)
                loop(v, T // C, turn)

            @block.scalar
            def _(act):
                act.wait_ge(s_dve, mark["exp"])
                act.activation(pr[:], lg[:], ACT.Exp).then_inc(s_exp, 1)

            @block.tensor
            def _(pe):
                pe.wait_ge(s_dve, mark["hot"])
                hot = eq[:].rearrange("p t n -> p (t n)")
                pe.matmul(ps_cum[:], K.upto[:], hot, start=True, stop=True)
                pe.matmul(ps_tot[:], K.ones[:], hot, start=True, stop=True).then_inc(s_cum, 1)

            @block.gpsimd
            def _(pool):
                def turn(i):
                    c.hold(pool, s_stage, (i + 1) * 2)
                    for k in range(C):
                        pool.indirect_dma_start(out=slot_rows, out_offset=bass.IndirectOffsetOnAxis(ap=idx[:, k:k + 1], axis=0),
                                                in_=stage[:, k, :], in_offset=None, bounds_check=SLOTS - 1,
                                                oob_is_err=False).then_inc(s_sent, 16)
                loop(pool, T // C, turn)
                pool.wait_ge(s_sent, 16 * T)


def experts(c, slot_rows, slot_out, w1, b1, w2, b2, K, acc, spare):
    nc = c.nc
    NF = FF // P
    sem = lambda x: c.sem("e_" + x)
    s_b, s_T, s_xT, s_h, s_relu, s_y, s_ys = (sem(x) for x in ("b", "T", "xT", "h", "relu", "y", "ys"))
    s_w, s_rows = ([sem(f"{x}0"), sem(f"{x}1")] for x in ("w", "rows"))
    s_store = [sem("store0"), sem("store1")]
    with ExitStack() as ctx:
        sb = lambda nm, sh, dt=F32: c.sb("e_" + nm, sh, dt, ctx)
        w1s, w2s = sb("w1s", [P, 2, 2, FF]), sb("w2s", [P, 2, NF, D])
        b1s, b2s = sb("b1s", [P, EXPERTS, NF]), sb("b2s", [P, EXPERTS, D])
        xT = sb("xT", [P, 2, 2, 512])
        free = acc[:].rearrange("p t f -> p (t f)")
        hT = free[:, 0:2 * NF * 512].rearrange("p (s f n) -> p s f n", s=2, f=NF)
        rows, ys = (free[:, 2 * NF * 512 + k * 8 * D:2 * NF * 512 + (k + 1) * 8 * D].rearrange("p (s t d) -> p s t d", s=2, t=4)
                    for k in range(2))
        ps_x = [c.ps(f"e_px{i}", [P, 512], ctx) for i in range(2)]
        ps_h = [c.ps(f"e_ph{i}", [P, 512], ctx) for i in range(2)]
        ps_y = [c.ps(f"e_py{i}", [P, 512], ctx) for i in range(4)]
        TURNS_E = EXPERTS // 2
        first = lambda i: isinstance(i, int) and i == 0

        def turns(eng, turn):
            turn(0, False)
            with eng.Fori(1, TURNS_E - 1) as i:
                turn(i, False)
            turn(TURNS_E - 1, True)
        units = lambda i: [(i * 4 + j, j % 2, i * 2 + j // 2, j // 2, j) for j in range(4)]
        with nc.Block() as block:

            @block.sync
            def _(sp):
                sp.dma_start(b1s[:], b1).then_inc(s_b, 16)
                sp.dma_start(b2s[:], b2.partition_broadcast(P)).then_inc(s_b, 16)

                def weights(e, se, u):
                    if not (isinstance(e, int) and e < 2):
                        sp.wait_ge(s_y, (u - 2) * 4)
                    sp.dma_start(w1s[:, se], w1[at(e), :, :].rearrange("a (c p) f -> p (a c) f", p=P)).then_inc(s_w[se], 16)
                    sp.dma_start(w2s[:, se], w2[at(e), :, :].rearrange("a (c p) d -> p (a c) d", p=P)).then_inc(s_w[se], 16)

                def unit_rows(u, s):
                    if not (isinstance(u, int) and u < 2):
                        sp.wait_ge(s_T, u - 1)
                    sp.dma_start(rows[:, s], slot_rows[at(u * 512, 512), :].rearrange("(t p) d -> p t d", p=P)).then_inc(s_rows[s], 16)

                def store(u, s):
                    sp.wait_ge(s_ys, (u + 1) * 4)
                    sp.dma_start(slot_out[at(u * 512, 512), :].rearrange("(t p) d -> p t d", p=P), ys[:, s]).then_inc(s_store[s], 16)

                def turn(i, last):
                    for u, s, e, se, j in units(i):
                        if not (last and j == 3):
                            unit_rows(u + 1, 1 - s)
                        if not (first(i) and j == 0):
                            store(u - 1, 1 - s)
                        if j % 2 == 0 and not (last and j == 2):
                            weights(e + 1, 1 - se, u + 2)
                unit_rows(0, 0)
                weights(0, 0, 0)
                turns(sp, turn)
                store(2 * EXPERTS - 1, 1)
                for s in range(2):
                    sp.wait_ge(s_store[s], 16 * EXPERTS)
                sp.wait_ge(s_b, 32)

            @block.gpsimd
            def _(pool):
                spare(pool)

            @block.tensor
            def _(pe):
                def turn_rows(i, j):
                    s = j % 2
                    pe.wait_ge(s_rows[s], (i * 2 + j // 2 + 1) * 16)
                    if not (first(i) and j == 0):
                        pe.wait_ge(s_xT, (i * 4 + j) * 2)
                    for t in range(4):
                        for k in range(2):
                            mm = pe.transpose(ps_x[k][:, t * P:(t + 1) * P], rows[:, s, t, k * P:(k + 1) * P], K.ident[:])
                    mm.then_inc(s_T, 1)

                def turn(i, last):
                    for u, s, e, se, j in units(i):
                        if j % 2 == 0:
                            pe.wait_ge(s_w[se], (i + 1) * 32)
                        pe.wait_ge(s_xT, (u + 1) * 2)
                        for f in range(NF):
                            if not (first(i) and j == 0 and f < 2):
                                pe.wait_ge(s_relu, u * NF + f - 1)
                            for k in range(2):
                                mm = pe.matmul(ps_h[f % 2][:], w1s[:, se, k, f * P:(f + 1) * P], xT[:, s, k, :], start=(k == 0), stop=(k == 1))
                            mm.then_inc(s_h, 1)
                        if not (last and j == 3):
                            turn_rows(i, j + 1)
                        pe.wait_ge(s_relu, (u + 1) * NF)
                        for t in range(4):
                            if not (first(i) and j == 0):
                                pe.wait_ge(s_ys, u * 4 + t - 3)
                            for f in range(NF):
                                mm = pe.matmul(ps_y[t][:, 0:D], hT[:, s, f, t * P:(t + 1) * P], w2s[:, se, f, :], start=(f == 0), stop=(f == NF - 1))
                            mm.then_inc(s_y, 1)
                turn_rows(0, 0)
                turns(pe, turn)

            @block.scalar
            def _(act):
                act.wait_ge(s_b, 32)

                def turned(u, s):
                    act.wait_ge(s_T, u + 1)
                    for k in range(2):
                        act.copy(xT[:, s, k, :], ps_x[k][:]).then_inc(s_xT, 1)

                def turn(i, last):
                    for u, s, e, se, j in units(i):
                        if not (first(i) and j < 2):
                            act.wait_ge(s_y, (u - 1) * 4)
                        for f in range(NF):
                            c.hold(act, s_h, u * NF + f + 1)
                            act.activation(hT[:, s, f, :], ps_h[f % 2][:], ACT.Relu,
                                           bias=b1s[:, at(e), f:f + 1].rearrange("p a f -> p (a f)")).then_inc(s_relu, 1)
                        if not (last and j == 3):
                            turned(u + 1, 1 - s)
                turned(0, 0)
                turns(act, turn)

            @block.vector
            def _(v):
                v.wait_ge(s_b, 32)

                def turn(i, last):
                    for u, s, e, se, j in units(i):
                        if not (first(i) and j < 2):
                            v.wait_ge(s_store[s], (i * 2 + j // 2) * 16)
                        for t in range(4):
                            v.wait_ge(s_y, u * 4 + t + 1)
                            v.tensor_tensor(ys[:, s, t, :], ps_y[t][:, 0:D], b2s[:, at(e), :].rearrange("p a d -> p (a d)"),
                                            ALU.add).then_inc(s_ys, 1)
                turns(v, turn)


def fetch_back(c, K, slot_out, X):
    nc = c.nc
    C = 7
    s_dve, s_idx, s_got = c.sem("b_dve"), c.sem("b_idx"), c.dma_sem("b_got")
    FMAX = float(np.finfo(np.float32).max)
    per = {}
    with ExitStack() as ctx:
        sb = lambda nm, sh, dt=F32: c.sb("b_" + nm, sh, dt, ctx)
        idx, y, z, m = sb("idx", [P, C], I32), sb("y", [P, C, D]), sb("z", [P, C, D]), sb("m", [P, C, D], I32)
        lim = sb("lim", [P, 2])
        with nc.Block() as block:

            @block.gpsimd
            def _(pool):
                def turn(i):
                    c.hold(pool, s_idx, i + 1)
                    for k in range(C):
                        pool.indirect_dma_start(out=y[:, k, :], out_offset=None, in_=slot_out,
                                                in_offset=bass.IndirectOffsetOnAxis(ap=idx[:, k:k + 1], axis=0)).then_inc(s_got, 16)
                loop(pool, T // C, turn)

            @block.vector
            def _(v):
                st = Steps(v, s_dve)
                st(v.memset(lim[:, 0:1], 10000.0))
                st(v.memset(lim[:, 1:2], -10000.0))

                def turn(i):
                    v.tensor_copy(idx[:], K.slot[:, at(i * C, C)]).then_inc(s_idx, 1)
                    st(v.memset(z[:], 0.0))
                    v.wait_ge(s_got, (i + 1) * 16 * C)
                    st(v.tensor_tensor(y[:], y[:], K.share[:, at(i * C, C)].unsqueeze(2).to_broadcast([P, C, D]), ALU.mult))
                    st.wait()
                    st(v.tensor_tensor(m[:], y[:], y[:], ALU.is_equal))
                    c.hold(v, *st.point())
                    st(v.copy_predicated(z[:], m[:], y[:]))
                    st.wait()
                    for k, (op, lim_) in enumerate(((ALU.is_gt, FMAX), (ALU.is_lt, -FMAX))):
                        st(v.tensor_scalar(m[:], y[:], lim_, None, op))
                        c.hold(v, *st.point())
                        st(v.copy_predicated(z[:], m[:], lim[:, k:k + 1].unsqueeze(2).to_broadcast([P, C, D])))
                        st.wait()
                    o = X[:, at(i * C, C), :]
                    st(v.tensor_tensor(o, o, z[:], ALU.add))
                    st.wait()
                loop(v, T // C, turn, st)


def gate_tables(c, K, hg, att, tab_s, ad):
    nc = c.nc
    h = HEADS2
    s_ld, s_dve, s_pool, s_st = (c.sem("t_" + x) for x in ("ld", "dve", "pool", "st"))
    mark = {}
    with ExitStack() as ctx:
        sb = lambda nm, sh, dt=F32: c.sb("t_" + nm, sh, dt, ctx)
        av, tmp, elv = sb("av", [P, 2, 16]), sb("tmp", [P, T, 16]), sb("elv", [P, T, h])
        vm, elm, gmax = sb("vm", [P, 2]), sb("elm", [P, h]), sb("gmax", [P, h])
        with nc.Block() as block:

            @block.vector
            def _(v):
                st = Steps(v, s_dve)
                v.wait_ge(s_ld, 16)
                for side in range(2):
                    st(v.tensor_tensor(tmp[:], hg[:, :, 0:16], av[:, side, :].unsqueeze(1).to_broadcast([P, T, 16]), ALU.mult))
                    st.wait()
                    o = hg[:, :, 16:20] if side == 0 else ad[:, :, 0:h]
                    st(v.tensor_reduce(o, tmp[:].rearrange("p t (h e) -> p t h e", h=h), AX, ALU.add))
                    st.wait()
                st(v.tensor_copy(elv[:], hg[:, :, 16:20]))
                st(v.tensor_scalar(vm[:, 0:1], K.part[:], float(LAST), None, ALU.is_lt))
                st.wait()
                st(v.tensor_scalar(vm[:, 1:2], vm[:, 0:1], BIG, -BIG, ALU.mult, ALU.add))
                st.wait()
                st(v.tensor_scalar(elv[:, T - 1, :], elv[:, T - 1, :], vm[:, 0:1], vm[:, 1:2], ALU.mult, ALU.add))
                st.wait()
                st(v.tensor_reduce(elm[:], elv[:].rearrange("p t h -> p h t"), AX, ALU.max))
                mark["max"] = st.n
                v.wait_ge(s_pool, 1)
                m = ad[:, :, h:2 * h]
                st(v.tensor_tensor(m, ad[:, :, 0:h], gmax[:].unsqueeze(1).to_broadcast([P, T, h]), ALU.add))
                st.wait()
                st(v.scalar_tensor_tensor(m, m, 0.2, m, ALU.mult, ALU.max))
                mark["tab"] = st.n

            @block.sync
            def _(sp):
                sp.dma_start(av[:], att.partition_broadcast(P)).then_inc(s_ld, 16)
                sp.wait_ge(s_dve, mark["tab"])
                sp.dma_start(tab_s.rearrange("(t p) n -> p t n", p=P), hg[:]).then_inc(s_st, 16)
                sp.wait_ge(s_st, 16)

            @block.gpsimd
            def _(pool):
                pool.wait_ge(s_dve, mark["max"])
                pool.partition_all_reduce(gmax[:], elm[:], P, RED.max).then_inc(s_pool, 1)


def gate_scores(c, K, hg, ad, agg, consts, gates):
    nc = c.nc
    h, n = HEADS2, EXPERTS2
    s_ld, s_dve, s_act = (c.sem("u_" + x) for x in ("ld", "dve", "act"))
    mark = {}
    with ExitStack() as ctx:
        sb = lambda nm, sh, dt=F32: c.sb("u_" + nm, sh, dt, ctx)
        cs = sb("cs", [P, 3, 16])
        z, w, o, q = sb("z", [P, T, h]), sb("w", [P, T, h]), sb("o", [P, T, 16]), sb("q", [P, T, 16])
        mu, var, sc = sb("mu", [P, T]), sb("var", [P, T]), sb("sc", [P, T, n])
        b1, b2, low, e1, e2 = sb("b1", [P, T]), sb("b2", [P, T]), sb("low", [P, T]), sb("e1", [P, T, n]), sb("e2", [P, T, n])
        wide = lambda a, k: a.unsqueeze(2).to_broadcast([P, T, k])
        heads = lambda a: a.unsqueeze(3).to_broadcast([P, T, h, 4])
        each = lambda a: a.rearrange("p t (h e) -> p t h e", h=h)
        row = lambda k: cs[:, k, :].unsqueeze(1).to_broadcast([P, T, 16])
        with nc.Block() as block:

            @block.vector
            def _(v):
                st = Steps(v, s_dve)

                def do(ins):
                    st(ins)
                    st.wait()
                do(v.tensor_tensor(z[:], hg[:, :, 16:20], ad[:, :, 0:h], ALU.add))
                do(v.scalar_tensor_tensor(z[:], z[:], 0.2, z[:], ALU.mult, ALU.max))
                do(v.tensor_tensor(z[:], z[:], ad[:, :, h:2 * h], ALU.subtract))
                mark["z"] = st.n
                v.wait_ge(s_act, 1)
                v.wait_ge(s_ld, 16)
                do(v.tensor_tensor(each(o[:]), each(hg[:, :, 0:16]), heads(w[:]), ALU.mult))
                do(v.tensor_tensor(o[:], o[:], agg[:, :, 0:16], ALU.add))
                do(v.tensor_tensor(w[:], w[:], agg[:, :, 16:20], ALU.add))
                do(v.reciprocal(w[:], w[:]))
                do(v.tensor_tensor(each(o[:]), each(o[:]), heads(w[:]), ALU.mult))
                do(v.tensor_tensor(o[:], o[:], row(0), ALU.add))
                do(v.tensor_reduce(mu[:], o[:], AX, ALU.add))
                do(v.tensor_scalar(mu[:], mu[:], 1.0 / 16, None, ALU.mult))
                do(v.tensor_tensor(o[:], o[:], wide(mu[:], 16), ALU.subtract))
                do(v.tensor_tensor(q[:], o[:], o[:], ALU.mult))
                do(v.tensor_reduce(var[:], q[:], AX, ALU.add))
                do(v.tensor_scalar(var[:], var[:], 1.0 / 16, LN_EPS, ALU.mult, ALU.add))
                mark["var"] = st.n
                v.wait_ge(s_act, 2)
                do(v.reciprocal(var[:], var[:]))
                do(v.tensor_tensor(o[:], o[:], wide(var[:], 16), ALU.mult))
                do(v.tensor_tensor(o[:], o[:], row(1), ALU.mult))
                do(v.tensor_tensor(o[:], o[:], row(2), ALU.add))
                do(v.tensor_reduce(sc[:], o[:].rearrange("p t (h e) -> p t e h", h=h), AX, ALU.add))
                do(v.tensor_scalar(sc[:], sc[:], 1.0 / h, None, ALU.mult))
                first_of_best(v, st, K, sc[:], n, b1[:], e1[:], low[:])
                do(v.scalar_tensor_tensor(sc[:], e1[:], -BIG, sc[:], ALU.mult, ALU.add))
                first_of_best(v, st, K, sc[:], n, b2[:], e2[:], low[:])
                do(v.tensor_tensor(b2[:], b2[:], b1[:], ALU.subtract))
                mark["gap"] = st.n
                v.wait_ge(s_act, 3)
                do(v.tensor_scalar(b1[:], b2[:], 1.0, None, ALU.add))
                do(v.reciprocal(b1[:], b1[:]))
                do(v.tensor_tensor(b2[:], b2[:], b1[:], ALU.mult))
                do(v.tensor_tensor(e1[:], e1[:], wide(b1[:], n), ALU.mult))
                do(v.tensor_tensor(e2[:], e2[:], wide(b2[:], n), ALU.mult))
                do(v.tensor_tensor(gates[:], e1[:], e2[:], ALU.add))

            @block.sync
            def _(sp):
                sp.dma_start(cs[:], consts.partition_broadcast(P)).then_inc(s_ld, 16)
                sp.wait_ge(s_ld, 16)

            @block.scalar
            def _(act):
                act.wait_ge(s_dve, mark["z"])
                act.activation(w[:], z[:], ACT.Exp).then_inc(s_act, 1)
                act.wait_ge(s_dve, mark["var"])
                act.activation(var[:], var[:], ACT.Sqrt).then_inc(s_act, 1)
                act.wait_ge(s_dve, mark["gap"])
                act.activation(b2[:], b2[:], ACT.Exp).then_inc(s_act, 1)


class ExpertsTwo:

    def __init__(self, K, H, w1, b1, w2, b2, y_dram):
        self.K, self.H, self.w1, self.b1, self.w2, self.b2, self.y_dram = K, H, w1, b1, w2, b2, y_dram

    TILES, NF, NE = 3, FF2 // P, EXPERTS2
    UNITS = -(-T // TILES)
    LEFT = T - (UNITS - 1) * TILES

    def place(self, c, ctx):
        sb = lambda nm, sh, dt=F32: c.sb("v_" + nm, sh, dt, ctx)
        NE, NF, n = self.NE, self.NF, self.TILES
        self.w1s, self.w2s = sb("w1s", [P, NE, 2, FF2]), sb("w2s", [P, NE, NF, D])
        self.b1s, self.b2s = sb("b1s", [P, NE, NF]), sb("b2s", [P, NE, D])
        self.rows, self.xT, self.hT, self.ys = sb("rows", [P, n, D]), sb("xT", [P, 2, n * P]), sb("hT", [P, NF, n * P]), sb("ys", [P, n, D])
        self.ps_h = [c.ps(f"v_ph{i}", [P, 512], ctx) for i in range(2)]
        self.ps_y = [c.ps(f"v_py{i}", [P, 2, D], ctx) for i in range(2)]
        sem = lambda x: c.sem("v_" + x)
        (self.s_ld, self.s_place, self.s_T, self.s_xT, self.s_h, self.s_act, self.s_y, self.s_ys) = (
            sem(x) for x in ("ld", "place", "T", "xT", "h", "act", "y", "ys"))
        self.s_store = sem("store")

    def count(self, i):
        return (self.LEFT, 1) if isinstance(i, int) and i == self.UNITS - 1 else (self.TILES, 2)

    def sync(self, sp):
        for tile, source in ((self.w1s, self.w1), (self.w2s, self.w2), (self.b1s, self.b1)):
            sp.dma_start(tile[:], source).then_inc(self.s_ld, 16)
        sp.dma_start(self.b2s[:], self.b2.partition_broadcast(P)).then_inc(self.s_ld, 16)

        def unit(i):
            n, adds = self.count(i)
            for e in range(self.NE):
                sp.wait_ge(self.s_ys, i * 2 * self.NE + (e + 1) * adds)
                sp.dma_start(self.y_dram[e, at(i * self.TILES * P, n * P), :].rearrange("(t p) d -> p t d", p=P),
                             self.ys[:, 0:n, :]).then_inc(self.s_store, 16)
        loop(sp, self.UNITS, unit, peel=True)
        sp.wait_ge(self.s_store, 16 * self.UNITS * self.NE)
        sp.wait_ge(self.s_ld, 64)

    def vector_rows(self, v, i, r):
        if r == 0:
            n, _ = self.count(i)
            if not (isinstance(i, int) and i == 0):
                v.wait_ge(self.s_T, i)
            v.tensor_copy(self.rows[:, 0:n, :], self.H[:, at(i * self.TILES, n), :]).then_inc(self.s_place, 1)

    def vector_results(self, v, i, r):
        if r % 2 or (isinstance(i, int) and i == 0 and r == 0):
            return
        e = (r // 2 - 1) % self.NE
        unit = i if r else i - 1
        n, adds = self.count(unit)
        start = isinstance(i, int) and i == 0
        if start and r == 2:
            v.wait_ge(self.s_ld, 64)
        v.wait_ge(self.s_y, unit * self.NE + e + 1)
        if not (start and e == 0):
            v.wait_ge(self.s_store, (unit * self.NE + e) * 16)
        bias = self.b2s[:, e, :].unsqueeze(1)
        for half in range(adds):
            m = min(2, n - 2 * half)
            v.tensor_tensor(self.ys[:, 2 * half:2 * half + m, :], self.ps_y[half][:, 0:m, :],
                            bias.to_broadcast([P, m, D]), ALU.add).then_inc(self.s_ys, 1)

    def tensor(self, pe, i, r, part):
        K, NF, NE, e = self.K, self.NF, self.NE, r // 2
        n, adds = self.count(i)
        w = n * P
        start = isinstance(i, int) and i == 0
        if r == 0 and part == 0:
            if start:
                pe.wait_ge(self.s_ld, 64)
            else:
                pe.wait_ge(self.s_act, i * NE * NF)
            pe.wait_ge(self.s_place, i + 1)
            for t in range(n):
                for k in range(2):
                    mm = pe.transpose(self.ps_h[k][:, t * P:(t + 1) * P], self.rows[:, t, k * P:(k + 1) * P], K.ident[:])
            mm.then_inc(self.s_T, 1)
            pe.wait_ge(self.s_xT, (i + 1) * 2)
        if r % 2 == 0:
            for f in range(part * NF // 2, (part + 1) * NF // 2):
                if not (e == 0 and f < 2):
                    pe.wait_ge(self.s_act, (i * NE + e) * NF + f - 1)
                for k in range(2):
                    mm = pe.matmul(self.ps_h[f % 2][:, 0:w], self.w1s[:, e, k, f * P:(f + 1) * P], self.xT[:, k, 0:w], start=(k == 0), stop=(k == 1))
                mm.then_inc(self.s_h, 1)
        else:
            if part == 0:
                pe.wait_ge(self.s_act, (i * NE + e + 1) * NF)
                if not (start and e == 0):
                    pe.wait_ge(self.s_ys, i * 2 * NE + e * adds)
            for t in range(0, min(n, 2)) if part == 0 else range(2, n):
                for f in range(NF):
                    mm = pe.matmul(self.ps_y[t // 2][:, t % 2, :], self.hT[:, f, t * P:(t + 1) * P], self.w2s[:, e, f, :], start=(f == 0), stop=(f == NF - 1))
            if part == (n > 2):
                mm.then_inc(self.s_y, 1)

    def scalar(self, act, i, r):
        NF, NE, e = self.NF, self.NE, r // 2
        w = self.count(i)[0] * P
        start = isinstance(i, int) and i == 0
        if r == 0:
            act.wait_ge(self.s_T, i + 1)
            for k in range(2):
                act.copy(self.xT[:, k, 0:w], self.ps_h[k][:, 0:w]).then_inc(self.s_xT, 1)
        if r % 2 == 0:
            if start and e == 0:
                act.wait_ge(self.s_ld, 64)
            else:
                act.wait_ge(self.s_y, i * NE + e)
            for f in range(NF):
                act.wait_ge(self.s_h, (i * NE + e) * NF + f + 1)
                act.activation(self.hT[:, f, 0:w], self.ps_h[f % 2][:, 0:w], ACT.Gelu, bias=self.b1s[:, e, f:f + 1]).then_inc(self.s_act, 1)


def mix(c, X, gates, y_dram, out):
    nc = c.nc
    C, NE = 7, EXPERTS2
    s_y, s_dve, s_out = [c.sem("m_y0"), c.sem("m_y1")], c.sem("m_dve"), c.sem("m_out")
    with ExitStack() as ctx:
        y = c.sb("m_y", [P, 2, NE, C, D], F32, ctx)
        with nc.Block() as block:

            @block.scalar
            def _(act):
                def seven(j, s, i):
                    if not early(j):
                        act.wait_ge(s_dve, (j - 1) * NE * C)
                    for e in range(NE):
                        act.dma_start(y[:, s, e], y_dram[e, at(j * C * P, C * P), :].rearrange("(t p) d -> p t d", p=P)).then_inc(s_y[s], 16)
                tiles(seven, act, T // C)

            @block.vector
            def _(v):
                def seven(j, s, i):
                    v.wait_ge(s_y[s], (i + 1) * 16 * NE)
                    for e in range(NE):
                        if e:
                            v.wait_ge(s_dve, j * NE * C + e * C)
                        for t in range(C):
                            o = X[:, at(j * C + t), :].rearrange("p a d -> p (a d)")
                            v.scalar_tensor_tensor(o, y[:, s, e, t, :], gates[:, at(j * C + t), e], o, ALU.mult, ALU.add).then_inc(s_dve, 1)
                tiles(seven, v, T // C)

            @block.sync
            def _(sp):
                def seven(j, s, i):
                    sp.wait_ge(s_dve, (j + 1) * NE * C)
                    whole = C - 1 if isinstance(j, int) and j == T // C - 1 else C
                    sp.dma_start(out[at(j * C * P, whole * P), :].rearrange("(t p) d -> p t d", p=P), X[:, at(j * C, whole), :]).then_inc(s_out, 16)
                tiles(seven, sp, T // C)
                sp.dma_start(out[(T - 1) * P:N, :], X[0:LAST, T - 1, :]).then_inc(s_out, 16)
                sp.wait_ge(s_out, 16 * (T // C + 1))


def build(nc, a, out, upto=99):
    with ExitStack() as ctx:
        c = Chip(nc, ctx)

        class K:
            ident, ones, upto, iota = (c.sb(n, [P, P]) for n in ("ident", "ones", "upto_", "iota"))
            part = c.sb("part", [P, 1])
            iota_low = c.sb("iota_low", [P, P])
            norm, share, slot = c.sb("norm", [P, T]), c.sb("share", [P, T]), c.sb("slot", [P, T], I32)
        dram = lambda n, sh, dt=F32: nc.dram_tensor(n, list(sh), dt).ap()
        slot_rows, slot_out = dram("slot_rows", [SLOTS, D]), dram("slot_out", [SLOTS, D])
        table8, table4, table1 = dram("table8", [NPAD, D + 8]), dram("table4", [NPAD, D + 4]), dram("table1", [NPAD, D + 2])
        tab_s, y_dram = dram("tab_s", [NPAD, 20]), dram("y_dram", [EXPERTS2, NPAD, D])
        base_a, base_b = dram("base_a", [NPAD, 2 * D]), dram("base_b", [NPAD, D])
        X, acc = c.sb("X", [P, T, D]), c.sb("acc", [P, T, D + 9])
        H = acc[:, :, 0:D]
        e2 = Edges(c, "e2", ROWS2, 8, ctx)
        graph = ctx.enter_context(ExitStack())
        e1 = Edges(c, "e1", ROWS, 4, graph)
        packed2 = c.sb("packed2", [P, ROWS2, 3], I32, graph)
        send2 = Sender(c, "s2", e2, packed2, graph)
        K.er = c.sb("er", [P, T, 16], F32, graph)
        e1.columns(c, graph)
        ordering = ExitStack()
        tile2 = c.sb("tile2", [P, ROWS2], F32, ordering)
        order2 = Order(c, "o2", e2, tile2[:], packed2, ordering)
        prepare(c, a, K, X, acc, e1, e2, slot_rows, packed2, tile2)
        layernorm(c, "n1_", X, H)
        project(c, "a1_", K, H, a["L0_gnn_fc1_wT"], a["L0_gnn_fc1_w"], a["attn_a1"], 8,
                table8, Base(a["w_base"], a["b_base"], base_a), order=order2)
        ordering.close()
        make_columns(c, K, e1)
        if upto >= 2:
            attend(c, "g1_", K, e1, table8, 8, D, K.er, acc)
            combine(c, "c1_", K, acc, 8, H, a["L0_gnn_bias1"], (base_a[:, 0:D],), relu=True, degree=True,
                    spare=lambda pool: send2.send(pool, 5, "a"))
        if upto >= 3:
            project(c, "a2_", K, H, a["L0_gnn_fc2_wT"], a["L0_gnn_fc2_w"], a["attn_a2"], 1,
                    table1, Base(a["w_base2"], None, base_b), spare=lambda pool: send2.send(pool, 6, "b"))
            attend(c, "g2_", K, e1, table1, 1, D, K.er, acc)
            combine(c, "c2_", K, acc, 1, X, a["L0_gnn_bias2"], (base_a[:, D:2 * D], base_b), residual=True,
                    spare=lambda pool: send2.send(pool, 4, "c"))
        if upto >= 4:
            c.renew()
            layernorm(c, "n2_", X, H)
            with ExitStack() as gate:
                lg = c.sb("lg", [P, T, EXPERTS], F32, gate)
                narrow(c, "r1_", K, H, a["L0_ffn_gate_w"], lg, spare=lambda pool: send2.send(pool, 5, "d"))
                route(c, K, lg, a["L0_ffn_gate_b"], H, slot_rows)
            experts(c, slot_rows, slot_out, a["L0_ffn_w1"], a["L0_ffn_b1"], a["L0_ffn_w2"], a["L0_ffn_b2"], K, acc,
                    spare=lambda pool: send2.send(pool, 27, "experts"))
            fetch_back(c, K, slot_out, X)
            c.renew()
        if upto >= 5:
            layernorm(c, "n3_", X, H)
            project(c, "b1_", K, H, a["L1_gnn_W1T"], a["L1_gnn_W1"], a["attn_c1"], 4, table4,
                    spare=lambda pool: send2.send(pool, 8, "e"))
            attend(c, "g3_", K, e1, table4, 4, D, K.er, acc)

            def last_edges(pool):
                send2.send(pool, ROWS2 // (2 * G) - send2.done, "g")
                send2.finish(pool)
            combine(c, "c3_", K, acc, 4, H, relu=True, spare=last_edges)
            project(c, "b2_", K, H, a["L1_gnn_W2T"], a["L1_gnn_W2"], a["attn_c2"], 1, table1)
            attend(c, "g4_", K, e1, table1, 1, D, K.er, acc)
            combine(c, "c4_", K, acc, 1, X, residual=True)
        graph.close()
        if upto >= 6:
            c.renew()
            layernorm(c, "n4_", X, H)
            hg, ad, agg = c.sb("hg", [P, T, 20]), c.sb("ad", [P, T, 8]), c.sb("agg", [P, T, 21])
            narrow(c, "r2_", K, H, a["L1_ffn_W_gat"], hg[:, :, 0:16])
            gate_tables(c, K, hg, a["gate_att"], tab_s, ad)
            with ExitStack() as lists:
                e2.columns(c, lists)
                make_columns(c, K, e2)
                assert e2.NG // e2.R == ExpertsTwo.UNITS and e2.R == 2 * EXPERTS2
                attend(c, "g5_", K, e2, tab_s, HEADS2, 16, ad, agg,
                       ExpertsTwo(K, H, a["L1_ffn_W1"], a["L1_ffn_b1"], a["L1_ffn_W2"], a["L1_ffn_b2"], y_dram))
            gates = c.sb("gates", [P, T, EXPERTS2])
            gate_scores(c, K, hg, ad, agg, a["gate_norm"], gates)
            mix(c, X, gates, y_dram, out)


def _layout(inputs):
    a = {k: np.ascontiguousarray(v) for k, v in inputs.items()}
    o = {"x": a["x"]}
    o["src"] = np.pad(a["src"], (0, ROWS * P - E)).reshape(ROWS, P)
    o["dst"] = np.pad(a["dst"], (0, (ROWS + 1) * P - E), constant_values=1 << 20).reshape(ROWS + 1, P)
    o["edges1"] = np.stack([o["src"].reshape(-1), o["dst"].reshape(-1)[:ROWS * P]], axis=1)
    o["L0_gnn_fc1_w"], o["L0_gnn_fc1_wT"] = a["L0_gnn_fc1_w"], a["L0_gnn_fc1_w"].T
    o["L0_gnn_fc2_w"], o["L0_gnn_fc2_wT"] = a["L0_gnn_fc2_w"], a["L0_gnn_fc2_w"].T
    for n, l, r in (("a1", "L0_gnn_attn_l1", "L0_gnn_attn_r1"), ("a2", "L0_gnn_attn_l2", "L0_gnn_attn_r2"),
                    ("c1", "L1_gnn_a1_src", "L1_gnn_a1_dst"), ("c2", "L1_gnn_a2_src", "L1_gnn_a2_dst")):
        o["attn_" + n] = np.stack([a[l].reshape(2, P).T, a[r].reshape(2, P).T], axis=2)
    o["w_base"] = np.concatenate([a["L0_gnn_wb0"].T, a["L0_gnn_wb1"][:, :D].T], axis=1)
    o["b_base"] = np.concatenate([a["L0_gnn_bb0"], a["L0_gnn_bb1"]]).reshape(1, 2 * D)
    o["w_base2"] = a["L0_gnn_wb1"][:, D:].T
    o["L0_gnn_bias1"], o["L0_gnn_bias2"] = a["L0_gnn_bias1"], a["L0_gnn_bias2"]
    for n in ("gate_w", "gate_b", "w1", "w2", "b2"):
        o["L0_ffn_" + n] = a["L0_ffn_" + n]
    o["L0_ffn_b1"] = a["L0_ffn_b1"].reshape(EXPERTS, FF // P, P).transpose(2, 0, 1)
    for n in ("W1", "W2"):
        o["L1_gnn_" + n], o["L1_gnn_" + n + "T"] = a["L1_gnn_" + n], a["L1_gnn_" + n].T
    o["L1_ffn_W_gat"] = a["L1_ffn_W_gat"]
    o["gate_att"] = np.stack([a["L1_ffn_att_src"].reshape(-1), a["L1_ffn_att_dst"].reshape(-1)])
    o["gate_norm"] = np.stack([a["L1_ffn_b_gat"], a["L1_ffn_ln_gamma"], a["L1_ffn_ln_beta"]])
    o["src2"], o["dst2"] = a["L1_ffn_edge_index"].reshape(2, P, ROWS2)
    o["L1_ffn_W1"] = a["L1_ffn_W1"].reshape(EXPERTS2, 2, P, FF2).transpose(2, 0, 1, 3)
    o["L1_ffn_W2"] = a["L1_ffn_W2"].reshape(EXPERTS2, FF2 // P, P, D).transpose(2, 0, 1, 3)
    o["L1_ffn_b1"] = a["L1_ffn_b1"].reshape(EXPERTS2, FF2 // P, P).transpose(2, 0, 1)
    o["L1_ffn_b2"] = a["L1_ffn_b2"]
    return {k: np.ascontiguousarray(v) for k, v in o.items()}


def kernel(**inputs):
    from concourse import bacc
    from concourse.bass_utils import run_bass_kernel_spmd

    nc = bacc.Bacc("TRN2", target_bir_lowering=False, num_devices=1)
    arrays = {f"in_{k}": v for k, v in _layout(inputs).items()}
    args = {k[3:]: nc.dram_tensor(k, v.shape, mybir.dt.from_np(v.dtype), kind="ExternalInput").ap() for k, v in arrays.items()}
    out = nc.dram_tensor("out", [N, D], F32, kind="ExternalOutput").ap()
    build(nc, args, out)
    return run_bass_kernel_spmd(nc, [arrays], core_ids=[0]).results[0]["out"]
```

```python
from contextlib import ExitStack

import numpy as np

import concourse.bass as bass
from concourse import mybir
from concourse.alu_op_type import AluOpType as ALU

F32 = mybir.dt.float32
I32 = mybir.dt.int32
ACT = mybir.ActivationFunctionType
AX = mybir.AxisListType.X
RED = bass.bass_isa.ReduceOp
DVE = mybir.EngineType.DVE
PE = mybir.EngineType.PE

P = 128
N = 6250
D = 256
T = (N + P - 1) // P
NPAD = T * P
LAST = N - (T - 1) * P
E = 100000
ROWS = (E + P - 1) // P
G = 8
SPREAD = 50.0
AHEAD = 3
BIG = 3.0e38
LN_EPS = 1e-5
E2 = 131072
ROWS2 = E2 // P
N2MAX = 8192

EXPERTS = 8
CAP = 977
CPAD = 1024
SLOTS = EXPERTS * CPAD
FF = 1024
EXPERTS2 = 4
FF2 = 512
HEADS2 = 4


class Steps:

    def __init__(self, eng, sem):
        self.eng, self.sem, self.n, self.base = eng, sem, 0, 0

    def __call__(self, ins):
        ins.then_inc(self.sem, 1)
        self.n += 1

    def point(self):
        return self.sem, self.base + self.n

    def wait(self):
        self.eng.wait_ge(*self.point())

    def turn(self, i, before, period):
        self.base, self.n = i * period + before, 0

    def leave(self, turns, before, period):
        self.base, self.n = 0, before + turns * period


def loop(eng, turns, body, *steps, peel=False):
    before = [s.n for s in steps]
    body(0)
    periods = [s.n - b for s, b in zip(steps, before)]
    end = turns - 1 if peel else turns
    if end > 1:
        with eng.Fori(1, end) as i:
            for s, b, p in zip(steps, before, periods):
                s.turn(i, b, p)
            body(i)
    for s, b, p in zip(steps, before, periods):
        s.leave(end, b, p)
    if peel:
        body(end)


def early(t):
    return isinstance(t, int) and t < 2


def ahead_tiles(lead, body, eng, n=T):
    lead(0, 0, 0)

    def tile(t, s, i):
        if not (isinstance(t, int) and t == n - 1):
            lead(t + 1, 1 - s, i)
        body(t, s, i)
    tiles(tile, eng, n)


def tiles(body, eng, n=T):
    body(0, 0, 0)
    body(1, 1, 0)
    with eng.Fori(1, n // 2) as i:
        body(i * 2, 0, i)
        body(i * 2 + 1, 1, i)
    body(n - 1, 0, n // 2)


def in_unit(u, W):
    return T - u * W if isinstance(u, int) and (u + 1) * W > T else W


def place_rows(v, h, u, W, dst, s_rows, s_turned):
    if not early(u):
        v.wait_ge(s_turned, u - 1)
    nt = in_unit(u, W)
    v.tensor_copy(dst[:, 0:nt, :], h[:, at(u * W, nt), :]).then_inc(s_rows, 1)


def at(i, n=1):
    return bass.ds(i, n)


class Chip:

    def __init__(self, nc, ctx):
        self.nc, self.ctx = nc, ctx
        self.sems = ctx.enter_context(ExitStack())
        self.lowest = self.next = min(nc.free_semaphores)
        self.highest = max(nc.free_semaphores)
        self.held = self.dma_sem("held")

    def sb(self, name, shape, dt=F32, ctx=None):
        return (ctx or self.ctx).enter_context(self.nc.sbuf_tensor(name, list(shape), dt))

    def ps(self, name, shape, ctx, dt=F32):
        return ctx.enter_context(self.nc.psum_tensor(name, list(shape), dt))

    def sem(self, name):
        self.next += 1
        return self.sems.enter_context(self.nc.semaphore(name, self.next - 1))

    def dma_sem(self, name):
        self.highest -= 1
        return self.ctx.enter_context(self.nc.semaphore(name, self.highest + 1))

    def hold(self, eng, sem, value):
        eng.wait_ge(sem, value)
        eng.sem_inc(self.held, 1)

    def renew(self):
        self.sems.close()
        used, self.next = range(self.lowest, self.next), self.lowest
        with self.nc.Block() as block:

            @block.gpsimd
            def _(pool):
                pool.sem_clear(used)


class Edges:

    def __init__(self, c, name, rows, groups_per_turn, ctx):
        self.name, self.rows, self.R = name, rows, groups_per_turn
        most = rows + T - 1
        self.NG = -(-most // (G * self.R)) * self.R
        self.Q = -(-(self.NG + AHEAD) * G // P)
        self.dram = c.nc.dram_tensor(name + "edges", [rows * P, 2], I32).ap()
        self.ids_dram = c.nc.dram_tensor(name + "ids", [self.Q, P], I32).ap()
        self.start = c.sb(name + "start", [P, T + 1], F32, ctx)
        self.first_slot = c.sb(name + "first_slot", [P, T + 1], F32, ctx)

    def columns(self, c, ctx):
        self.src_cols = c.sb(self.name + "src_cols", [P, self.Q * P], I32, ctx)
        self.dst_cols = c.sb(self.name + "dst_cols", [P, self.Q * P], F32, ctx)
        self.ids = c.sb(self.name + "ids_row", [1, self.Q * P], I32, ctx)


class Order:

    def __init__(self, c, name, e, tile_f, packed, ctx):
        self.c, self.e, self.tile_f, self.packed = c, e, tile_f, packed
        self.place, self.run = (c.sb(name + x, [P, e.rows], F32, ctx) for x in ("place", "run"))
        self.hot = c.sb(name + "hot", [P, e.rows], I32, ctx)

    STEPS = 3

    def begin(self, v, st):
        st(v.memset(self.place[:], 0.0))
        st.wait()

    def end(self, v, st):
        st(v.tensor_scalar(self.packed[:, 0:self.e.rows, 0], self.place[:], -1.0, None, ALU.add))
        st.wait()

    def tile(self, v, st, K, t):
        st(v.tensor_scalar(self.hot[:], self.tile_f, K.iota[:, at(t)], None, ALU.is_equal))
        st.wait()
        st(v.tensor_tensor_scan(self.run[:], self.hot[:], self.hot[:], self.e.first_slot[:, at(t)], ALU.add, ALU.max))
        self.c.hold(v, *st.point())
        st(v.copy_predicated(self.place[:], self.hot[:], self.run[:]))


class Sender:

    def __init__(self, c, name, e, packed, ctx):
        self.c, self.e, self.packed, self.done = c, e, packed, 0
        self.stage = c.sb(name + "stage", [P, 2, G, 3], I32, ctx)
        self.sent = [c.dma_sem(f"{name}sent{s}") for s in range(2)]
        self.name = name

    def send(self, pool, turns, key):
        c, first, before = self.c, self.done, self.done * 16 * G
        s_staged = c.sem(f"{self.name}staged{key}")
        self.done += turns

        def turn(i):
            for s in range(2):
                if not (isinstance(i, int) and first == 0):
                    c.hold(pool, self.sent[s], i * (16 * G) + before)
                pool.tensor_copy(self.stage[:, s], self.packed[:, at((i * 2 + first * 2 + s) * G, G), :]).then_inc(s_staged, 1)
                c.hold(pool, s_staged, i * 2 + s + 1)
                for k in range(G):
                    pool.indirect_dma_start(
                        out=self.e.dram, out_offset=bass.IndirectOffsetOnAxis(ap=self.stage[:, s, k, 0:1], axis=0),
                        in_=self.stage[:, s, k, 1:3], in_offset=None, bounds_check=self.e.rows * P - 1,
                        oob_is_err=False).then_inc(self.sent[s], 16)
        loop(pool, turns, turn)

    def finish(self, pool):
        for s in range(2):
            pool.wait_ge(self.sent[s], self.done * 16 * G)


def five(eng, body, *steps):
    assert (T + 1) % 5 == 0

    def turn(i):
        for n in range(5):
            body(i * 5 + n)
    loop(eng, (T + 1) // 5, turn, *steps)


def prepare(c, a, K, X, acc, e1, e2, slot_rows, packed2, tile2):
    nc = c.nc
    sem = lambda x: c.sem("p_" + x)
    s_const, s_load, s_dve, s_sum, s_pool, s_zero = (sem(x) for x in ("const", "load", "dve", "sum", "pool", "zero"))
    s_x, s_zout, s_copy, s_act, s_load2, s_pre, s_flag = (sem(x) for x in ("x", "zout", "copy", "act", "load2", "pre", "flag"))
    s_general = sem("general")
    COLS = -(-ROWS // (2 * G)) * 2 * G
    mark = {}
    with ExitStack() as ctx:
        sb = lambda n, sh, dt=F32: c.sb("p_" + n, sh, dt, ctx)
        iota_i, part_i = sb("iota_i", [P, P], I32), sb("part_i", [P, 1], I32)
        thr, nthr = sb("thr", [P, T + 1]), sb("nthr", [P, T + 1])
        src_i, dst_i, next_i = (sb(x, [P, ROWS], I32) for x in ("src_i", "dst_i", "next_i"))
        whole_i = sb("whole_i", [P, ROWS], I32)
        dst_f, junk = sb("dst_f", [P, ROWS]), sb("junk", [P, ROWS])
        src2_i, dst2_i = sb("src2_i", [P, ROWS2], I32), sb("dst2_i", [P, ROWS2], I32)
        spare = acc[:].rearrange("p t f -> p (t f)")
        junk2, dst2_f, junk3 = (spare[:, k * ROWS2:(k + 1) * ROWS2] for k in range(3))
        zero = spare[:, 3 * ROWS2:3 * ROWS2 + 2048]
        cnt, own = sb("cnt", [P, 2, T + 1]), sb("own", [P, 2, T + 1])
        bad, bad_all, flag = sb("bad", [P, 1]), sb("bad_all", [P, 1]), sb("flag", [P, 1], I32)
        packed1 = sb("packed1", [P, COLS, 3], I32)
        order1 = Order(c, "p_o1", e1, dst_f[:], packed1, ctx)
        send1 = Sender(c, "p_s1", e1, packed1, ctx)
        ps_sum, ps_pre = c.ps("ps_sum", [P, 512], ctx), c.ps("ps_pre", [P, 512], ctx)
        with nc.Block() as block:

            @block.gpsimd
            def _(pool):
                pool.iota(iota_i[:], [[1, P]], base=0, channel_multiplier=0).then_inc(s_pool, 1)
                pool.iota(part_i[:], [[0, 1]], base=0, channel_multiplier=1).then_inc(s_pool, 1)
                pool.memset(K.ident[:], 0.0).then_inc(s_zero, 1)
                pool.memset(K.ones[:], 1.0).then_inc(s_zero, 1)
                pool.memset(zero, 0.0).then_inc(s_zero, 1)
                pool.memset(X[:, T - 1, :], 0.0).then_inc(s_zero, 1)
                pool.wait_ge(s_zero, 4)
                pool.affine_select(out=K.ident[:], in_=K.ident[:], compare_op=ALU.not_equal, fill=1.0, base=0,
                                   pattern=[[-1, P]], channel_multiplier=1).then_inc(s_const, 1)
                pool.affine_select(out=K.upto[:], in_=K.ones[:], compare_op=ALU.is_ge, fill=0.0, base=0,
                                   pattern=[[1, P]], channel_multiplier=-1).then_inc(s_const, 1)
                pool.wait_ge(s_flag, 1)
                pool.partition_all_reduce(bad_all[:], bad[:], P, RED.max).then_inc(s_flag, 1)

            @block.sync
            def _(sp):
                flat = lambda x, n: x.rearrange("r e -> (r e)")[n:n + ROWS * P].rearrange("(p j) -> p j", p=P)
                sp.dma_start(dst_i[:], flat(a["dst"], 0)).then_inc(s_load, 16)
                sp.dma_start(next_i[:], flat(a["dst"], 1)).then_inc(s_load, 16)
                sp.dma_start(dst2_i[:], a["dst2"]).then_inc(s_load2, 16)
                sp.dma_start(src2_i[:], a["src2"]).then_inc(s_load2, 16)
                sp.dma_start(src_i[:], flat(a["src"], 0)).then_inc(s_copy, 16)
                sp.dma_start(e1.dram.rearrange("(p n) e -> p (n e)", p=P), a["edges1"].rearrange("(p n) e -> p (n e)", p=P)).then_inc(s_copy, 16)
                sp.dma_start(X[:, 0:T - 1, :], a["x"][0:(T - 1) * P, :].rearrange("(t p) d -> p t d", p=P)).then_inc(s_x, 16)
                sp.wait_ge(s_zero, 4)
                sp.dma_start(X[0:LAST, T - 1, :], a["x"][(T - 1) * P:N, :]).then_inc(s_x, 16)
                for n in range(SLOTS // 1024):
                    sp.dma_start(slot_rows[n * 1024:(n + 1) * 1024, :].rearrange("(p a) d -> p (a d)", p=P),
                                 zero).then_inc(s_zout, 16)
                sp.wait_ge(s_copy, 32)
                sp.wait_ge(s_x, 32)
                sp.wait_ge(s_zout, 16 * (SLOTS // 1024))

            @block.vector
            def _(v):
                st = Steps(v, s_dve)
                v.wait_ge(s_pool, 2)
                st(v.tensor_copy(K.iota[:], iota_i[:]))
                st(v.tensor_copy(K.part[:], part_i[:]))
                st(v.tensor_scalar(K.iota_low[:], iota_i[:], float(-P), None, ALU.add))
                st.wait()
                st(v.tensor_scalar(thr[:], K.iota[:, 0:T + 1], float(P), None, ALU.mult))
                st(v.tensor_scalar(nthr[:], K.iota[:, 0:T + 1], float(-P), 0.5, ALU.mult, ALU.add))
                mark["thresholds"] = st.n
                v.wait_ge(s_load, 32)
                st(v.tensor_copy(dst_f[:], dst_i[:]))
                st.wait()
                st(v.tensor_copy(whole_i[:], dst_i[:]))
                st.wait()
                st(v.tensor_scalar(dst_i[:], dst_i[:], 7, None, ALU.arith_shift_right))
                st(v.tensor_scalar(next_i[:], next_i[:], 7, None, ALU.arith_shift_right))
                st.wait()
                st(v.tensor_tensor(junk[:], dst_i[:], next_i[:], ALU.is_gt))
                st.wait()
                v.tensor_reduce(bad[:], junk[:], AX, ALU.max).then_inc(s_flag, 1)
                v.wait_ge(s_flag, 1)

                def count(t):
                    st(v.tensor_scalar(junk[:], dst_f[:], thr[:, at(t)], 0.0, ALU.is_lt, ALU.add,
                                       accum_out=cnt[:, 0, at(t)]))
                    st.wait()
                five(v, count, st)
                v.wait_ge(s_act, T + 1)
                st(v.tensor_scalar(cnt[:, 1, :], cnt[:, 1, :], -0.5, ROWS2 / 2.0, ALU.mult, ALU.add))
                st.wait()
                st(v.tensor_tensor(own[:, :, 0:T], cnt[:, :, 1:T + 1], cnt[:, :, 0:T], ALU.subtract))
                st(v.tensor_scalar(own[:, 0, T:T + 1], cnt[:, 0, T:T + 1], -1.0, float(ROWS), ALU.mult, ALU.add))
                st(v.tensor_scalar(own[:, 1, T:T + 1], cnt[:, 1, T:T + 1], -1.0, float(ROWS2), ALU.mult, ALU.add))
                st.wait()
                mark["counts"] = st.n
                v.wait_ge(s_load2, 32)
                v.wait_ge(s_pre, 1)
                st(v.tensor_copy(packed2[:, :, 2], dst2_i[:]))
                st(v.tensor_copy(junk2, src2_i[:]))
                st(v.tensor_scalar(dst2_i[:], dst2_i[:], 7, None, ALU.arith_shift_right))
                st.wait()
                st(v.tensor_scalar(packed2[:, :, 1], junk2, float(N - 1), None, ALU.min))
                st(v.tensor_copy(tile2[:], dst2_i[:]))
                st.wait()
                st(v.tensor_scalar(tile2[:], tile2[:], float(T), None, ALU.min))
                v.wait_ge(s_sum, 1)
                for k, e in enumerate((e1, e2)):
                    st(v.tensor_copy(e.start[:], ps_sum[:, k * 64:k * 64 + T + 1]))
                    st(v.tensor_tensor(e.first_slot[:], ps_pre[:, k * 64:k * 64 + T + 1], own[:, k, :], ALU.subtract))
                    st.wait()
                    st(v.tensor_tensor(e.first_slot[:], e.first_slot[:], e.start[:], ALU.add))
                v.wait_ge(s_flag, 2)
                st(v.tensor_copy(flag[:], bad_all[:]))
                st.wait()

            @block.scalar
            def _(act):
                act.wait_ge(s_dve, mark["thresholds"])
                act.wait_ge(s_load2, 32)

                def count(t):
                    if not (isinstance(t, int) and t == 0):
                        c.hold(act, s_act, t)
                    act.activation(junk3, dst2_f, ACT.Sign, bias=nthr[:, at(t)],
                                   accum_out=cnt[:, 1, at(t)]).then_inc(s_act, 1)
                act.copy(dst2_f, dst2_i[:]).then_inc(s_pre, 1)
                act.wait_ge(s_pre, 1)
                five(act, count)

            @block.tensor
            def _(pe):
                pe.wait_ge(s_const, 2)
                pe.wait_ge(s_dve, mark["counts"])
                for k in range(2):
                    pe.matmul(ps_sum[:, k * 64:k * 64 + T + 1], K.ones[:], cnt[:, k, :], start=True, stop=True)
                    mm = pe.matmul(ps_pre[:, k * 64:k * 64 + T + 1], K.upto[:], own[:, k, :], start=True, stop=True)
                mm.then_inc(s_sum, 1)

        with nc.Block() as block:

            @block.vector
            def _(v):
                disorder = v.value_load(flag[0:1, 0:1], min_val=0, max_val=1)
                with v.If(disorder > 0):
                    st = Steps(v, s_general)
                    st(v.tensor_copy(dst_f[:], dst_i[:]))
                    st(v.memset(packed1[:], 1 << 22))
                    st.wait()
                    st(v.tensor_scalar(dst_f[:], dst_f[:], float(T), None, ALU.min))
                    order1.begin(v, st)

                    def one(t):
                        order1.tile(v, st, K, t)
                        st.wait()
                    loop(v, T + 1, one, st)
                    order1.end(v, st)
                    st(v.tensor_copy(packed1[:, 0:ROWS, 1], src_i[:]))
                    v.tensor_copy(packed1[:, 0:ROWS, 2], whole_i[:]).then_inc(s_pool, 1)
                    st.wait()
                    mark["packed"] = st.n

            @block.gpsimd
            def _(pool):
                disorder = pool.value_load(flag[0:1, 0:1], min_val=0, max_val=1)
                with pool.If(disorder > 0):
                    pool.wait_ge(s_pool, 3)
                    pool.wait_ge(s_general, mark["packed"])
                    send1.send(pool, COLS // (2 * G), "")
                    send1.finish(pool)


def make_columns(c, K, e):
    nc = c.nc
    name, Q = e.name, e.Q
    sem = lambda x: c.sem(name + x)
    s_dve, s_rows, s_gath, s_turned, s_ids, s_io, s_k = sem("dve"), sem("rows"), c.dma_sem(name + "gath"), sem("turned"), sem("ids_"), sem("io"), sem("k")
    mark = {}
    with ExitStack() as ctx:
        sb = lambda n, sh, dt=F32: c.sb(name + n, sh, dt, ctx)
        k_i = sb("k_i", [P, Q], I32)
        first_i, last_i = sb("first_i", [P, T], I32), sb("last_i", [P, T], I32)
        first, last, some, num = (sb(x, [P, T]) for x in ("first", "last", "some", "num"))
        cum, shift, junk = sb("cum", [P, T]), sb("shift", [P, T]), sb("junk", [P, 2, T])
        kf, tk, dk, row_f, base, tid, past = (sb(x, [P, Q]) for x in ("kf", "tk", "dk", "row_f", "base", "tid", "past"))
        row_i, ids_i = sb("row_i", [P, Q], I32), sb("ids_i", [Q, P], I32)
        edges, loc = sb("edge_rows", [P, Q, 2 * P], I32), sb("loc", [P, Q, 2, P])
        banks = -(-Q // 4)
        ps = [c.ps(f"{name}ps{i}", [P, banks, 512], ctx) for i in range(2)]
        ps_ids = c.ps(name + "ps_ids", [P, 512], ctx)
        with nc.Block() as block:

            @block.gpsimd
            def _(pool):
                pool.iota(k_i[:], [[P, Q]], base=0, channel_multiplier=1).then_inc(s_k, 1)
                pool.wait_ge(s_rows, 1)
                for q in range(Q):
                    pool.indirect_dma_start(
                        out=edges[:, q, :], out_offset=None, in_=e.dram.rearrange("(r p) e -> r (p e)", p=P),
                        in_offset=bass.IndirectOffsetOnAxis(ap=row_i[:, q:q + 1], axis=0)).then_inc(s_gath, 16)

            @block.vector
            def _(v):
                st = Steps(v, s_dve)
                start = e.start

                def do(ins):
                    st(ins)
                    st.wait()
                v.wait_ge(s_k, 1)
                st(v.tensor_copy(kf[:], k_i[:]))
                st(v.tensor_copy(first_i[:], start[:, 0:T]))
                st(v.tensor_scalar(last_i[:], start[:, 1:T + 1], float(P - 1), None, ALU.add))
                st(v.tensor_tensor(some[:], start[:, 1:T + 1], start[:, 0:T], ALU.is_gt))
                st.wait()
                st(v.tensor_scalar(first_i[:], first_i[:], 7, None, ALU.arith_shift_right))
                st(v.tensor_scalar(last_i[:], last_i[:], 7, None, ALU.arith_shift_right))
                st.wait()
                st(v.tensor_copy(first[:], first_i[:]))
                st(v.tensor_copy(last[:], last_i[:]))
                st.wait()
                do(v.tensor_tensor(num[:], last[:], first[:], ALU.subtract))
                do(v.tensor_tensor(num[:], num[:], some[:], ALU.mult))
                do(v.tensor_tensor_scan(cum[:], K.ones[:, 0:T], num[:], 0.0, ALU.mult, ALU.add))
                do(v.tensor_tensor(shift[:], num[:], cum[:], ALU.subtract))
                do(v.tensor_tensor(shift[:], shift[:], first[:], ALU.add))
                for q in range(Q):
                    do(v.tensor_scalar(junk[:, q % 2, :], cum[:], kf[:, q:q + 1], 0.0, ALU.is_le, ALU.add,
                                       accum_out=tk[:, q:q + 1]))
                    do(v.scalar_tensor_tensor(junk[:, q % 2, :], K.iota[:, 0:T], tk[:, q:q + 1], shift[:],
                                              ALU.is_equal, ALU.mult, accum_out=dk[:, q:q + 1]))
                st(v.tensor_tensor(row_f[:], kf[:], dk[:], ALU.add))
                st(v.tensor_scalar(past[:], tk[:], float(T), float(1 << 22), ALU.is_ge, ALU.mult))
                st(v.tensor_scalar(base[:], tk[:], float(P), None, ALU.mult))
                st(v.tensor_scalar(tid[:], tk[:], float(T - 1), None, ALU.min))
                st.wait()
                st(v.tensor_tensor(base[:], base[:], past[:], ALU.add))
                do(v.tensor_scalar(row_f[:], row_f[:], float(e.rows - 1), None, ALU.min))
                v.tensor_copy(row_i[:], row_f[:]).then_inc(s_rows, 1)
                v.wait_ge(s_gath, 16 * Q)
                for side in range(2):
                    st(v.tensor_copy(loc[:, :, side, :], edges[:].rearrange("p q (e s) -> p q s e", s=2)[:, :, side, :]))
                st.wait()
                for q in range(Q):
                    st(v.tensor_scalar(loc[:, q, 1, :], loc[:, q, 1, :], base[:, q:q + 1], None, ALU.subtract))
                mark["locals"] = st.n
                v.wait_ge(s_turned, 1)
                for q in range(Q):
                    for side, cols in ((0, e.src_cols), (1, e.dst_cols)):
                        st(v.tensor_copy(cols[:, q * P:(q + 1) * P], ps[side][:, q // 4, (q % 4) * P:(q % 4 + 1) * P]))
                v.tensor_copy(ids_i[:], ps_ids[0:Q, 0:P]).then_inc(s_ids, 1)

            @block.sync
            def _(sp):
                sp.wait_ge(s_ids, 1)
                sp.dma_start(e.ids_dram, ids_i[:]).then_inc(s_io, 16)
                sp.wait_ge(s_io, 16)
                sp.dma_start(e.ids[:], e.ids_dram.rearrange("q k -> (q k)").rearrange("(a k) -> a k", a=1)).then_inc(s_io, 16)
                sp.wait_ge(s_io, 32)

            @block.tensor
            def _(pe):
                pe.wait_ge(s_dve, mark["locals"])
                for q in range(Q):
                    for side in range(2):
                        pe.transpose(ps[side][:, q // 4, (q % 4) * P:(q % 4 + 1) * P], loc[:, q, side, :], K.ident[:])
                pe.transpose(ps_ids[0:Q, 0:P], tid[:], K.ident[:]).then_inc(s_turned, 1)


class Base:

    def __init__(self, weights, bias, out):
        self.weights, self.bias, self.out, self.n = weights, bias, out, out.shape[1]


def extremes(v, st, elm, elv, vm, done):
    st.wait()
    st(v.tensor_reduce(elm[:, 0, :], elv[:].rearrange("p t h -> p h t"), AX, ALU.max))
    st.wait()
    st(v.tensor_scalar(elv[:], elv[:], -1.0, None, ALU.mult))
    st.wait()
    st(v.tensor_scalar(elv[:, T - 1, :], elv[:, T - 1, :], vm[:, 0:1], vm[:, 1:2], ALU.mult, ALU.add))
    st.wait()
    v.tensor_reduce(elm[:, 1, :], elv[:].rearrange("p t h -> p h t"), AX, ALU.max).then_inc(done, 1)


def shifts(v, st, K, er, gmax, heads):
    m = er[:, :, heads:2 * heads]
    st(v.tensor_copy(K.low[:, 0:heads], gmax[:, 1, :]))
    st(v.tensor_tensor(K.spread[:, 0:heads], gmax[:, 0, :], gmax[:, 1, :], ALU.add))
    st(v.tensor_tensor(m, er[:, :, 0:heads], gmax[:, 0, :].unsqueeze(1).to_broadcast([P, T, heads]), ALU.add))
    st.wait()
    st(v.tensor_reduce(K.most[:], K.spread[:, 0:heads], AX, ALU.max))
    st(v.scalar_tensor_tensor(m, m, 0.2, m, ALU.mult, ALU.max))
    st.wait()
    st(v.tensor_scalar(K.far[:], K.most[:], SPREAD, None, ALU.is_gt))
    st.wait()


def exact_shifts(c, name, K, edges, table, heads, F, er, own=None):
    nc = c.nc
    width = table.shape[1]
    el = F + 1 if heads == 1 else F
    PAIRS = edges.NG * G
    sem = lambda x: c.sem(name + x)
    s_idx, s_dve, s_wide, s_turned = (sem(x) for x in ("idx", "dve", "wide", "turned"))
    s_gat = c.dma_sem(name + "gat")
    banks = -(-heads // 4)
    per = heads // banks
    with ExitStack() as ctx:
        sb = lambda n, sh, dt=F32: c.sb(name + n, sh, dt, ctx)
        idx, row, hot, rel = sb("idx", [P, 1], I32), sb("row", [P, width]), sb("hot", [P, P]), sb("rel", [P, heads])
        wide, best, most = sb("wide", [P, heads, P]), sb("best", [P, heads]), sb("most", [P, T, heads])
        ps = c.ps(name + "ps", [P, banks, 512], ctx)
        with nc.Block() as block:

            @block.gpsimd
            def _(pool):
                far = pool.value_load(K.far[0:1, 0:1], min_val=0, max_val=1)
                with pool.If(far > 0):
                    def pair(k):
                        c.hold(pool, s_idx, k + 1)
                        pool.indirect_dma_start(out=row[:], out_offset=None, in_=table,
                                                in_offset=bass.IndirectOffsetOnAxis(ap=idx[:, 0:1], axis=0)).then_inc(s_gat, 16)
                    loop(pool, PAIRS, pair)

            @block.tensor
            def _(pe):
                far = pe.value_load(K.far[0:1, 0:1], min_val=0, max_val=1)
                with pe.If(far > 0):
                    def pair(k):
                        pe.wait_ge(s_wide, k + 1)
                        for h in range(heads):
                            mm = pe.transpose(ps[:, h // per, (h % per) * P:(h % per + 1) * P], wide[:, h, :], K.ident[:])
                        mm.then_inc(s_turned, 1)
                    loop(pe, PAIRS, pair)

            @block.vector
            def _(v):
                far = v.value_load(K.far[0:1, 0:1], min_val=0, max_val=1)
                with v.If(far > 0):
                    st = Steps(v, s_dve)

                    def do(ins):
                        st(ins)
                        st.wait()
                    if own is None:
                        do(v.memset(most[:], 0.0))
                    else:
                        do(v.tensor_tensor(most[:], own, K.low[:, 0:heads].unsqueeze(1).to_broadcast([P, T, heads]), ALU.add))

                    def pair(k):
                        v.tensor_copy(idx[:], edges.src_cols[:, at(k)]).then_inc(s_idx, 1)
                        tile = v.value_load(edges.ids[0:1, at(k)], min_val=0, max_val=T - 1)
                        st(v.tensor_scalar(hot[:], K.iota[:], edges.dst_cols[:, at(k)], None, ALU.is_equal))
                        v.wait_ge(s_gat, (k + 1) * 16)
                        do(v.tensor_tensor(rel[:], row[:, el:el + heads], K.low[:, 0:heads], ALU.add))
                        v.tensor_tensor(wide[:], hot[:].unsqueeze(1).to_broadcast([P, heads, P]),
                                        rel[:].unsqueeze(2).to_broadcast([P, heads, P]), ALU.mult).then_inc(s_wide, 1)
                        v.wait_ge(s_turned, k + 1)
                        for b in range(banks):
                            st(v.tensor_reduce(best[:, b * per:(b + 1) * per], ps[:, b, 0:per * P].rearrange("p (h e) -> p h e", h=per), AX, ALU.max))
                        st.wait()
                        o = most[:, at(tile), :].rearrange("p a h -> p (a h)")
                        do(v.tensor_tensor(o, o, best[:], ALU.max))
                    loop(v, PAIRS, pair, st)
                    do(v.tensor_tensor(most[:], most[:], K.low[:, 0:heads].unsqueeze(1).to_broadcast([P, T, heads]), ALU.subtract))
                    m = er[:, :, heads:2 * heads]
                    do(v.tensor_tensor(m, er[:, :, 0:heads], most[:], ALU.add))
                    do(v.scalar_tensor_tensor(m, m, 0.2, m, ALU.mult, ALU.max))


def project(c, name, K, h, w_t, w_nat, attn_dram, heads, table, base=None, spare=None, order=None):
    nc = c.nc
    one = heads == 1
    width = table.shape[1]
    nb = base.n if base else 0
    W = 1 if nb > D else 2
    U = -(-T // W)
    sem = lambda n: c.sem(name + n)
    s_w, s_fold, s_folded, s_beside, s_hT, s_hTc = sem("w"), sem("fold"), sem("folded"), sem("beside"), sem("hT"), sem("hTc")
    s_mm, s_out, s_store, s_dve, s_max, s_aux = sem("mm"), sem("out"), [sem("store0"), sem("store1")], sem("dve"), sem("max"), sem("aux")
    s_rows, mark = sem("rows"), {}
    nout = 3 + (1 if one else 0) + (1 if base else 0)
    nf = D + 2 * heads
    with ExitStack() as ctx:
        sb = lambda n, sh, dt=F32: c.sb(name + n, sh, dt, ctx)
        w = sb("w", [P, 2, nf])
        wn, attn = sb("wn", [P, 2, D]), sb("attn", [P, 2, 2])
        fold, off_i, off, ge = sb("fold", [P, 2, 2, heads]), sb("off_i", [P, 2, heads], I32), sb("off", [P, 2, heads]), sb("ge", [P, 2, heads])
        rows, hT, stage = sb("rows", [P, 2, W, D]), sb("hT", [P, 2, W, D]), sb("stage", [P, 2, W, width])
        elv, elm, gmax = sb("elv", [P, T, heads]), sb("elm", [P, 2, heads]), sb("gmax", [P, 2, heads])
        vm = sb("vm", [P, 2])
        if nb:
            wb, bstage = sb("wb", [P, 2, nb]), sb("bstage", [P, 2, W, nb])
            bias = sb("bias", [1, nb]) if base.bias is not None else None
        ps_t = [c.ps(f"{name}pt{i}", [P, W, D], ctx) for i in range(2)]
        ps_f = [c.ps(f"{name}pf{i}", [P, W, 512], ctx) for i in range(2)]
        ps_b = [c.ps(f"{name}pb{i}", [P, W, nb], ctx) for i in range(2)] if nb else None
        nload = 16 * (3 + (1 if nb else 0) + (1 if nb and bias is not None else 0))
        with nc.Block() as block:

            @block.sync
            def _(sp):
                sp.dma_start(w[:, :, 0:D], w_t.rearrange("(c p) n -> p c n", p=P)).then_inc(s_w, 16)
                sp.dma_start(wn[:], w_nat.rearrange("(c p) n -> p c n", p=P)).then_inc(s_w, 16)
                sp.dma_start(attn[:], attn_dram).then_inc(s_w, 16)
                if nb:
                    sp.dma_start(wb[:], base.weights.rearrange("(c p) n -> p c n", p=P)).then_inc(s_w, 16)
                    if bias is not None:
                        sp.dma_start(bias[:], base.bias).then_inc(s_w, 16)
                per = 32 if nb else 16

                def store(u, s, i):
                    nt = in_unit(u, W)
                    for out, staged in ((table, stage), (base.out, bstage)) if nb else ((table, stage),):
                        sp.wait_ge(s_out, (u + 1) * nout)
                        sp.dma_start(out[at(u * W * P, nt * P), :].rearrange("(t p) n -> p t n", p=P), staged[:, s, 0:nt, :]) \
                            .then_inc(s_store[s], 16)
                tiles(store, sp, U)
                for s in range(2):
                    sp.wait_ge(s_store[s], per * ((U + 1 - s) // 2))

            @block.gpsimd
            def _(pool):
                pool.iota(off_i[:], [[P, 2], [-(D // heads), heads]], base=0, channel_multiplier=1).then_inc(s_aux, 1)
                pool.memset(stage[:], 1.0).then_inc(s_aux, 1)
                if spare:
                    spare(pool)
                pool.wait_ge(s_max, 1)
                pool.partition_all_reduce(gmax[:].rearrange("p a h -> p (a h)"), elm[:].rearrange("p a h -> p (a h)"), P, RED.max).then_inc(s_max, 1)

            @block.vector
            def _(v):
                st = Steps(v, s_dve)
                v.wait_ge(s_aux, 2)
                st(v.tensor_copy(off[:], off_i[:]))
                v.wait_ge(s_w, nload)
                st.wait()
                st(v.tensor_scalar(ge[:], off[:], 0.0, None, ALU.is_ge))
                st(v.tensor_scalar(off[:], off[:], float(D // heads), None, ALU.is_lt))
                st.wait()
                st(v.tensor_tensor(ge[:], ge[:], off[:], ALU.mult))
                st.wait()
                for side in range(2):
                    ins = v.tensor_tensor(fold[:, side], ge[:], attn[:, :, side:side + 1].to_broadcast([P, 2, heads]), ALU.mult)
                    ins.then_inc(s_fold, 1)
                if order:
                    order.begin(v, st)
                    mark["ordered"] = st.n
                    steps = order.STEPS

                def rows_and_order(t, s, i):
                    place_rows(v, h, t, W, rows[:, s], s_rows, s_hT)
                    if order:
                        st.turn(t, mark["ordered"], steps)
                        order.tile(v, st, K, t)
                        st.wait()
                tiles(rows_and_order, v, U)
                if order:
                    st.leave(T, mark["ordered"], steps)
                    order.tile(v, st, K, T)
                    st.wait()
                    order.end(v, st)
                v.wait_ge(s_out, U * nout)
                st(v.tensor_scalar(vm[:, 0:1], K.part[:], float(LAST), None, ALU.is_lt))
                st.wait()
                st(v.tensor_scalar(vm[:, 1:2], vm[:, 0:1], BIG, -BIG, ALU.mult, ALU.add))
                st.wait()
                st(v.tensor_scalar(elv[:, T - 1, :], elv[:, T - 1, :], vm[:, 0:1], vm[:, 1:2], ALU.mult, ALU.add))
                st.wait()
                extremes(v, st, elm, elv, vm, s_max)
                v.wait_ge(s_max, 2)
                shifts(v, st, K, K.er, gmax, heads)

            @block.tensor
            def _(pe):
                pe.wait_ge(s_fold, 2)
                pe.wait_ge(s_w, nload)
                for k in range(2):
                    for side in range(2):
                        for o in range(2):
                            mm = pe.matmul(ps_f[0][:, 0, (2 * k + side) * heads:(2 * k + side + 1) * heads],
                                           wn[:, o, k * P:(k + 1) * P], fold[:, side, o, :], start=(o == 0), stop=(o == 1))
                mm.then_inc(s_folded, 1)
                pe.wait_ge(s_beside, 4)

                def turn(t, s, i):
                    pe.wait_ge(s_rows, t + 1)
                    if not early(t):
                        pe.wait_ge(s_hTc, t - 1)
                    for n in range(in_unit(t, W)):
                        for k in range(2):
                            mm = pe.transpose(ps_t[s][:, n, k * P:(k + 1) * P], rows[:, s, n, k * P:(k + 1) * P], K.ident[:])
                    mm.then_inc(s_hT, 1)

                def tile(t, s, i):
                    pe.wait_ge(s_hTc, t + 1)
                    if not early(t):
                        pe.wait_ge(s_out, (t - 1) * nout)
                    for n in range(in_unit(t, W)):
                        turned = [hT[:, s, n, k * P:(k + 1) * P] for k in range(2)]
                        for k in range(2):
                            mm = pe.matmul(ps_f[s][:, n, 0:nf], turned[k], w[:, k, :], start=(k == 0), stop=(k == 1))
                        if nb:
                            for k in range(2):
                                mm = pe.matmul(ps_b[s][:, n, :], turned[k], wb[:, k, :], start=(k == 0), stop=(k == 1 and bias is None))
                            if bias is not None:
                                mm = pe.matmul(ps_b[s][:, n, :], K.ones[0:1, :], bias[:], start=False, stop=True)
                    mm.then_inc(s_mm, 1)
                ahead_tiles(turn, tile, pe, U)

            @block.scalar
            def _(act):
                act.wait_ge(s_folded, 1)
                for k in range(2):
                    for side in range(2):
                        ins = act.copy(w[:, k, D + side * heads:D + (side + 1) * heads],
                                       ps_f[0][:, 0, (2 * k + side) * heads:(2 * k + side + 1) * heads])
                        ins.then_inc(s_beside, 1)

                def turned(t, s, i):
                    act.wait_ge(s_hT, t + 1)
                    if not early(t):
                        act.wait_ge(s_mm, t - 1)
                    nt = in_unit(t, W)
                    act.copy(hT[:, s, 0:nt], ps_t[s][:, 0:nt]).then_inc(s_hTc, 1)

                def tile(t, s, i):
                    act.wait_ge(s_mm, t + 1)
                    if isinstance(t, int) and t == 0:
                        act.wait_ge(s_aux, 2)
                    if not early(t):
                        act.wait_ge(s_store[s], i * (32 if nb else 16))
                    nt = in_unit(t, W)
                    f = ps_f[s][:, 0:nt]
                    if one:
                        ins = [act.copy(stage[:, s, 0:nt, 0:D], f[:, :, 0:D]), act.copy(stage[:, s, 0:nt, D + 1:D + 2], f[:, :, D:D + 1])]
                    else:
                        ins = [act.copy(stage[:, s, 0:nt, 0:D + heads], f[:, :, 0:D + heads])]
                    ins += [act.copy(elv[:, at(t * W, nt), :], f[:, :, D:D + heads]),
                            act.copy(K.er[:, at(t * W, nt), 0:heads], f[:, :, D + heads:D + 2 * heads])]
                    if nb:
                        ins += [act.copy(bstage[:, s, 0:nt], ps_b[s][:, 0:nt])]
                    for x in ins:
                        x.then_inc(s_out, 1)
                ahead_tiles(turned, tile, act, U)


def attend(c, name, K, edges, table, heads, F, er, acc, side=None):
    nc = c.nc
    one = heads == 1
    width = table.shape[1]
    nr = F + 1 if one else F + heads + 1
    el = F + 1 if one else F
    slot = F + heads + 1 if not one else F + 2
    R, NG = edges.R, edges.NG
    TURNS = NG // R
    helped = {8: 2, 4: 4}.get(heads, 0) if F == D else 0
    mid = (G - helped) // 2
    narrow_ = F < D
    MB = 4
    sem = lambda n: c.sem(name + n)
    s_stage, s_M, s_T, s_MT, s_er, s_z, s_w = sem("stage"), sem("M"), sem("T"), sem("MT"), sem("er"), sem("z"), sem("w")
    s_sc, s_main, s_add, s_init = sem("sc"), sem("main"), sem("add"), sem("init")
    s_gat = [c.dma_sem(f"{name}gat{r}") for r in range(R)]
    s_zd, s_sa = sem("zd"), sem("sa")
    with ExitStack() as ctx:
        sb = lambda n, sh, dt=F32: c.sb(name + n, sh, dt, ctx)
        idx = sb("idx", [P, R, G], I32)
        ring = sb("ring", [P, R, G, slot])
        M, MT = sb("M", [P, MB, G, P]), sb("MT", [P, 2, G, P])
        z, wt = sb("z", [P, 2, G, heads]), sb("wt", [P, 2, G, 1])
        ps_T = [c.ps(f"{name}pT{i}", [P, 4, P], ctx) for i in range(2)]
        if narrow_:
            ps_eo = [c.ps(f"{name}{x}", [P, 512], ctx) for x in ("pe", "po")]
            ps_e = 2 * [ps_eo[0][:, 0:G * 2 * heads].rearrange("p (g h) -> p g h", g=G)]
            ps_o = [ps_eo[1][:, k * 64:k * 64 + nr] for k in range(G)]
        else:
            ps_e = [c.ps(f"{name}pe{i}", [P, G, 2 * heads], ctx) for i in range(2)]
            ps_o = 2 * [c.ps(f"{name}po{i}", [P, 512], ctx) for i in range(4)]
        if side:
            side.place(c, ctx)
        first = lambda i: isinstance(i, int) and i == 0
        below = lambda g, n: isinstance(g, int) and g < n
        with nc.Block() as block:

            if side:
                @block.sync
                def _(sp):
                    side.sync(sp)

            @block.gpsimd
            def _(pool):
                def turn(i):
                    for r in range(R):
                        g = i * R + r
                        if first(i) and r == 0:
                            pool.wait_ge(s_init, 1)
                        c.hold(pool, s_stage, g + 1)
                        for k in range(G):
                            pool.indirect_dma_start(
                                out=ring[:, r, k, 0:width], out_offset=None, in_=table,
                                in_offset=bass.IndirectOffsetOnAxis(ap=idx[:, r, k:k + 1], axis=0)).then_inc(s_gat[r], 16)
                loop(pool, TURNS, turn, peel=bool(side))

            @block.scalar
            def _(act):
                def stage(g, r):
                    act.copy(idx[:, r, :], edges.src_cols[:, at(g * G, G)]).then_inc(s_stage, 1)

                def turned(g, b):
                    for half in range(2):
                        act.wait_ge(s_T, g * 2 + half + 1)
                        act.copy(MT[:, b, 4 * half:4 * half + 4, :], ps_T[half][:]).then_inc(s_MT, 1)
                for g in range(AHEAD):
                    stage(g, g)
                turned(0, 0)

                def turn(i):
                    for r in range(R):
                        g = i * R + r
                        r2 = (r + AHEAD) % R
                        act.wait_ge(s_z, g + 1)
                        if one:
                            act.activation(wt[:, r % 2], z[:, r % 2], ACT.Exp).then_inc(s_w, 1)
                            act.wait_ge(s_T, g * 2 + 2)
                            act.wait_ge(s_w, g + 1)
                            for k in range(G):
                                act.activation(M[:, r % MB, k, :], M[:, r % MB, k, :], ACT.Copy, scale=wt[:, r % 2, k, :]).then_inc(s_sc, 1)
                        else:
                            act.activation(ring[:, r, :, F:F + heads], z[:, r % 2], ACT.Exp).then_inc(s_w, 1)
                            if helped:
                                act.wait_ge(s_w, g + 1)
                            for k in range(G - helped, G):
                                for h in range(heads):
                                    f = ring[:, r, k, h * (F // heads):(h + 1) * (F // heads)]
                                    act.activation(f, f, ACT.Copy, scale=ring[:, r, k, F + h:F + h + 1]).then_inc(s_sa, 1)
                        turned(g + 1, (r + 1) % 2)
                        if not (first(i) and r + AHEAD < R):
                            act.wait_ge(s_main, (g + AHEAD - R + 1) * G)
                        stage(g + AHEAD, r2)
                        if side:
                            side.scalar(act, i, r)
                loop(act, TURNS, turn, peel=bool(side))

            @block.tensor
            def _(pe):
                def turn_hots(g, m):
                    for k in range(G):
                        if k % 4 == 0:
                            pe.wait_ge(s_M, g * 2 + k // 4 + 1)
                            if not below(g, 1):
                                pe.wait_ge(s_MT, g * 2 - 1 + k // 4)
                        mm = pe.transpose(ps_T[k // 4][:, k % 4, :], M[:, m, k, :], K.ident[:])
                        if k % 4 == 3:
                            mm.then_inc(s_T, 1)

                def dest_terms(g, b):
                    _, ids = nc.values_load_multi_w_load_instructions(
                        edges.ids[0:1, at(g * G, G)], engines=[PE], min_val=0, max_val=T - 1,
                        skip_runtime_bounds_check_because="tile numbers are cut to T - 1")
                    if narrow_:
                        if not below(g, 1):
                            pe.wait_ge(s_z, g)
                    elif not below(g, 2):
                        pe.wait_ge(s_z, g - 1)
                    for k in range(G):
                        if k % 4 == 0:
                            pe.wait_ge(s_MT, g * 2 + k // 4 + 1)
                        mm = pe.matmul(ps_e[b][:, k, :], MT[:, b, k, :],
                                       er[:, at(ids[k]), 0:2 * heads].rearrange("p a h -> p (a h)"), start=True, stop=True)
                    mm.then_inc(s_er, 1)
                turn_hots(0, 0)
                dest_terms(0, 0)

                def turn(i):
                    for r in range(R):
                        g = i * R + r
                        turn_hots(g + 1, (r + 1) % MB)
                        if side:
                            side.tensor(pe, i, r, 0)
                        dest_terms(g + 1, (r + 1) % 2)
                        if side:
                            side.tensor(pe, i, r, 1)
                        for k in range(G):
                            if one:
                                pe.wait_ge(s_sc, g * G + k + 1)
                            elif k in (0, mid):
                                pe.wait_ge(s_sc, g * 2 + k // mid + 1)
                            elif k >= G - helped:
                                pe.wait_ge(s_sa, (g * helped + k - (G - helped) + 1) * heads)
                            if narrow_:
                                if k == 0 and not (first(i) and r == 0):
                                    pe.wait_ge(s_add, g * G)
                            elif not (first(i) and r == 0 and k < 4):
                                pe.wait_ge(s_add, g * G + k - 3)
                            pe.matmul(ps_o[k][:, 0:nr], M[:, r % MB, k, :], ring[:, r, k, 0:nr],
                                      start=True, stop=True).then_inc(s_main, 1)
                loop(pe, TURNS, turn, peel=bool(side))

            @block.vector
            def _(v):
                st = Steps(v, s_zd)
                v.memset(ring[:], 1.0).then_inc(s_init, 1)
                st(v.memset(acc[:], 0.0))

                def hots(g, m):
                    for half in range(2):
                        cols = edges.dst_cols[:, at(g * G + 4 * half, 4)].unsqueeze(2).to_broadcast([P, 4, P])
                        v.tensor_tensor(M[:, m, 4 * half:4 * half + 4, :], K.iota[:].unsqueeze(1).to_broadcast([P, 4, P]), cols,
                                        ALU.is_equal).then_inc(s_M, 1)

                def load_ids(g):
                    return nc.values_load_multi_w_load_instructions(
                        edges.ids[0:1, at(g * G, G)], engines=[DVE], min_val=0, max_val=T - 1,
                        skip_runtime_bounds_check_because="tile numbers are cut to T - 1")[1]

                def add(g, k, tid):
                    if not narrow_:
                        v.wait_ge(s_main, g * G + k + 1)
                    elif k == 0:
                        v.wait_ge(s_main, (g + 1) * G)
                    if not (below(g, 1) and k == 0):
                        v.wait_ge(s_add, g * G + k)
                    a = acc[:, at(tid), 0:nr].rearrange("p a f -> p (a f)")
                    v.tensor_tensor(a, a, ps_o[k][:, 0:nr], ALU.add).then_inc(s_add, 1)

                hots(0, 0)
                if MB == 4:
                    hots(1, 1)

                def turn(i):
                    for r in range(R):
                        g, b = i * R + r, r % 2
                        if not (first(i) and r == 0):
                            ids = load_ids(g - 1)
                        v.wait_ge(s_gat[r], (i + 1) * 16 * G)
                        v.wait_ge(s_er, g + 1)
                        zb = z[:, b]
                        st(v.tensor_tensor(zb, ring[:, r, :, el:el + heads], ps_e[b][:, :, 0:heads], ALU.add))
                        st.wait()
                        st(v.scalar_tensor_tensor(zb, zb, 0.2, zb, ALU.mult, ALU.max))
                        st.wait()
                        v.tensor_tensor(zb, zb, ps_e[b][:, :, heads:2 * heads], ALU.subtract).then_inc(s_z, 1)
                        if MB == 4:
                            hots(g + 2, (r + 2) % MB)
                        for k in range(G):
                            if not (first(i) and r == 0):
                                add(g - 1, k, ids[k])
                        if MB == 2:
                            hots(g + 1, (r + 1) % MB)
                        if side:
                            side.vector_rows(v, i, r)
                        if not one:
                            v.wait_ge(s_w, g + 1)
                            for half in range(2):
                                hs = slice(mid * half, mid * half + mid)
                                f = ring[:, r, hs, 0:F].rearrange("p k (h f) -> p k h f", h=heads)
                                v.tensor_tensor(f, f, ring[:, r, hs, F:F + heads].unsqueeze(3).to_broadcast([P, mid, heads, F // heads]),
                                                ALU.mult).then_inc(s_sc, 1)
                        if side:
                            side.vector_results(v, i, r)
                st.wait()
                loop(v, TURNS, turn, st, peel=bool(side))
                ids = load_ids(NG - 1)
                for k in range(G):
                    add(NG - 1, k, ids[k])
                if side:
                    side.vector_results(v, TURNS, 0)


def combine(c, name, K, acc, heads, out, bias=None, bases=(), residual=False, relu=False, degree=False, spare=None):
    nc = c.nc
    C = 7
    sem = lambda n: c.sem(name + n)
    s_bias, s_dve, s_load = sem("bias"), sem("dve"), [sem("load0"), sem("load1")]
    per = {}
    with ExitStack() as ctx:
        sb = lambda n, sh, dt=F32: c.sb(name + n, sh, dt, ctx)
        rs = sb("rs", [P, T, heads])
        brow = sb("brow", [P, D]) if bias is not None else None
        ld = sb("ld", [P, 2, len(bases), C, D]) if bases else None
        with nc.Block() as block:

            @block.vector
            def _(v):
                st = Steps(v, s_dve)
                st(v.tensor_scalar(rs[:], acc[:, :, D:D + heads], 1e-37, None, ALU.max))
                if degree:
                    st(v.tensor_scalar(K.norm[:], acc[:, :, D + heads], 1.0, None, ALU.max))
                st.wait()
                st(v.reciprocal(rs[:], rs[:]))
                if degree:
                    st(v.reciprocal(K.norm[:], K.norm[:]))
                if bias is not None:
                    v.wait_ge(s_bias, 16)
                st.wait()
                per["before"] = st.n

                def seven(i, s):
                    y = acc[:, at(i * C, C), 0:D]
                    yh = y.rearrange("p t (h f) -> p t h f", h=heads)
                    st(v.tensor_tensor(yh, yh, rs[:, at(i * C, C), :].unsqueeze(3).to_broadcast([P, C, heads, D // heads]), ALU.mult))
                    st.wait()
                    if bias is not None:
                        st(v.tensor_tensor(y, y, brow[:].unsqueeze(1).to_broadcast([P, C, D]), ALU.add))
                    if bases:
                        v.wait_ge(s_load[s], (i // 2 + 1) * 16 * len(bases))
                        b = ld[:, s, 0]
                        if len(bases) > 1:
                            st(v.tensor_tensor(b, b, ld[:, s, 1], ALU.add))
                            st.wait()
                        st(v.tensor_tensor(b, b, K.norm[:, at(i * C, C)].unsqueeze(2).to_broadcast([P, C, D]), ALU.mult))
                        st.wait()
                        st(v.tensor_tensor(y, y, b, ALU.add))
                    st.wait()
                    o = out[:, at(i * C, C), :]
                    if relu:
                        st(v.tensor_scalar(o, y, 0.0, None, ALU.max))
                    elif residual:
                        st(v.tensor_tensor(o, o, y, ALU.add))
                    st.wait()
                for i in range(T // C):
                    seven(i, i % 2)
                    per.setdefault("period", st.n - per["before"])
            if spare:
                @block.gpsimd
                def _(pool):
                    spare(pool)
            if bias is not None or bases:
                @block.sync
                def _(sp):
                    if bias is not None:
                        sp.dma_start(brow[:], bias.partition_broadcast(P)).then_inc(s_bias, 16)
                    for i in range(T // C) if bases else ():
                        if i >= 2:
                            sp.wait_ge(s_dve, per["before"] + (i - 1) * per["period"])
                        for n, b in enumerate(bases):
                            sp.dma_start(ld[:, i % 2, n], b[i * C * P:(i + 1) * C * P, :].rearrange("(t p) d -> p t d", p=P)) \
                                .then_inc(s_load[i % 2], 16)
                    if bias is not None:
                        sp.wait_ge(s_bias, 16)


def layernorm(c, name, X, H, spare=None):
    nc = c.nc
    s_dve, s_sqrt = c.sem(name + "dve"), c.sem(name + "sqrt")
    mark = {}
    with ExitStack() as ctx:
        stats = c.sb(name + "stats", [P, T, 6], F32, ctx)
        mean, m2, rstd = (c.sb(name + x, [P, T], F32, ctx) for x in ("mean", "m2", "rstd"))
        with nc.Block() as block:

            if spare:
                @block.gpsimd
                def _(pool):
                    spare(pool)

            @block.vector
            def _(v):
                st = Steps(v, s_dve)
                rows = lambda A, t: A[:, at(t), :].rearrange("p a f -> p (a f)")

                def seven(one):
                    def turn(i):
                        for t in range(7):
                            st(one(i * 7 + t))
                    loop(v, T // 7, turn, st)
                seven(lambda t: v.bn_stats(rows(stats, t), rows(X, t)))
                st.wait()
                st(v.tensor_tensor(mean[:], stats[:, :, 1], stats[:, :, 4], ALU.add))
                st(v.tensor_tensor(rstd[:], stats[:, :, 1], stats[:, :, 4], ALU.subtract))
                st(v.tensor_tensor(m2[:], stats[:, :, 2], stats[:, :, 5], ALU.add))
                st.wait()
                st(v.tensor_scalar(mean[:], mean[:], 0.5, None, ALU.mult))
                st(v.tensor_tensor(rstd[:], rstd[:], rstd[:], ALU.mult))
                st(v.tensor_scalar(m2[:], m2[:], 1.0 / D, LN_EPS, ALU.mult, ALU.add))
                st.wait()
                st(v.scalar_tensor_tensor(rstd[:], rstd[:], 0.25, m2[:], ALU.mult, ALU.add))
                mark["var"] = st.n
                v.wait_ge(s_sqrt, 1)
                st(v.reciprocal(rstd[:], rstd[:]))
                st.wait()

                seven(lambda t: v.tensor_scalar(rows(H, t), rows(X, t), mean[:, at(t)], rstd[:, at(t)], ALU.subtract, ALU.mult))
                st.wait()

            @block.scalar
            def _(act):
                act.wait_ge(s_dve, mark["var"])
                act.activation(rstd[:], rstd[:], ACT.Sqrt).then_inc(s_sqrt, 1)


def narrow(c, name, K, h, weights, out, spare=None):
    nc = c.nc
    n = weights.shape[1]
    W = 2
    U = -(-T // W)
    s_w, s_hT, s_hTc, s_mm, s_out, s_rows = (c.sem(name + x) for x in ("w", "hT", "hTc", "mm", "out", "rows"))
    with ExitStack() as ctx:
        w, hT = c.sb(name + "w", [P, 2, n], F32, ctx), c.sb(name + "hT", [P, 2, W, D], F32, ctx)
        rows = c.sb(name + "rows", [P, 2, W, D], F32, ctx)
        ps_t = [c.ps(f"{name}pt{i}", [P, W, D], ctx) for i in range(2)]
        ps_f = [c.ps(f"{name}pf{i}", [P, W, n], ctx) for i in range(2)]
        with nc.Block() as block:

            if spare:
                @block.gpsimd
                def _(pool):
                    spare(pool)

            @block.sync
            def _(sp):
                sp.dma_start(w[:], weights.rearrange("(c p) n -> p c n", p=P)).then_inc(s_w, 16)
                sp.wait_ge(s_w, 16)

            @block.vector
            def _(v):
                tiles(lambda u, s, i: place_rows(v, h, u, W, rows[:, s], s_rows, s_hT), v, U)

            @block.tensor
            def _(pe):
                pe.wait_ge(s_w, 16)

                def turn(t, s, i):
                    pe.wait_ge(s_rows, t + 1)
                    if not early(t):
                        pe.wait_ge(s_hTc, t - 1)
                    for m in range(in_unit(t, W)):
                        for k in range(2):
                            mm = pe.transpose(ps_t[s][:, m, k * P:(k + 1) * P], rows[:, s, m, k * P:(k + 1) * P], K.ident[:])
                    mm.then_inc(s_hT, 1)

                def tile(t, s, i):
                    pe.wait_ge(s_hTc, t + 1)
                    if not early(t):
                        pe.wait_ge(s_out, t - 1)
                    for m in range(in_unit(t, W)):
                        for k in range(2):
                            mm = pe.matmul(ps_f[s][:, m, :], hT[:, s, m, k * P:(k + 1) * P], w[:, k, :], start=(k == 0), stop=(k == 1))
                    mm.then_inc(s_mm, 1)
                ahead_tiles(turn, tile, pe, U)

            @block.scalar
            def _(act):
                def turned(t, s, i):
                    act.wait_ge(s_hT, t + 1)
                    if not early(t):
                        act.wait_ge(s_mm, t - 1)
                    nt = in_unit(t, W)
                    act.copy(hT[:, s, 0:nt], ps_t[s][:, 0:nt]).then_inc(s_hTc, 1)

                def tile(t, s, i):
                    act.wait_ge(s_mm, t + 1)
                    nt = in_unit(t, W)
                    act.copy(out[:, at(t * W, nt), :], ps_f[s][:, 0:nt]).then_inc(s_out, 1)
                ahead_tiles(turned, tile, act, U)


def first_of_best(v, st, K, val, n, best, eq, low):
    v_b = lambda a: a.unsqueeze(2).to_broadcast([P, T, n])
    io = K.iota_low[:, P - n:P].unsqueeze(1).to_broadcast([P, T, n])
    st(v.tensor_reduce(best, val, AX, ALU.max))
    st.wait()
    st(v.tensor_tensor(eq, val, v_b(best), ALU.is_equal))
    st.wait()
    st(v.tensor_tensor(eq, eq, io, ALU.mult))
    st.wait()
    st(v.tensor_reduce(low, eq, AX, ALU.min))
    st.wait()
    st(v.tensor_tensor(eq, io, v_b(low), ALU.is_equal))
    st.wait()


def route(c, K, lg, gate_b, H, slot_rows):
    nc = c.nc
    n = EXPERTS
    C = 7
    s_b, s_dve, s_exp, s_cum, s_stage = (c.sem("r_" + x) for x in ("b", "dve", "exp", "cum", "stage"))
    s_sent = [c.dma_sem("r_sent0"), c.dma_sem("r_sent1")]
    mark = {}
    with ExitStack() as ctx:
        sb = lambda nm, sh, dt=F32: c.sb("r_" + nm, sh, dt, ctx)
        gb, pr, eq = sb("gb", [P, n]), sb("pr", [P, T, n]), sb("eq", [P, T, n])
        mx, low, sm = sb("mx", [P, T]), sb("low", [P, T]), sb("sm", [P, T])
        exc, pos, kept, slot = sb("exc", [P, T, n]), sb("pos", [P, T]), sb("kept", [P, T]), sb("slot", [P, T])
        send, stage, idx = sb("send", [P, T]), sb("stage", [P, 2, C, D]), sb("idx", [P, 2, C], I32)
        ps_cum, ps_tot = c.ps("ps_cum", [P, T * n], ctx), c.ps("ps_tot", [P, T * n], ctx)
        b3 = lambda a: a.unsqueeze(2).to_broadcast([P, T, n])
        with nc.Block() as block:

            @block.sync
            def _(sp):
                sp.dma_start(gb[:], gate_b.partition_broadcast(P)).then_inc(s_b, 16)
                sp.wait_ge(s_b, 16)

            @block.vector
            def _(v):
                st = Steps(v, s_dve)
                v.wait_ge(s_b, 16)
                st(v.tensor_tensor(lg[:], lg[:], gb[:].unsqueeze(1).to_broadcast([P, T, n]), ALU.add))
                st.wait()
                st(v.tensor_reduce(mx[:], lg[:], AX, ALU.max))
                st.wait()
                st(v.tensor_tensor(lg[:], lg[:], b3(mx[:]), ALU.subtract))
                mark["exp"] = st.n
                v.wait_ge(s_exp, 1)
                st(v.tensor_reduce(sm[:], pr[:], AX, ALU.add))
                st.wait()
                st(v.reciprocal(sm[:], sm[:]))
                st.wait()
                st(v.tensor_tensor(pr[:], pr[:], b3(sm[:]), ALU.mult))
                st.wait()
                first_of_best(v, st, K, pr[:], n, mx[:], eq[:], low[:])
                mark["hot"] = st.n
                v.wait_ge(s_cum, 1)
                for e in range(n):
                    st(v.tensor_tensor_scan(exc[:, :, e], K.ones[:, 0:T], ps_tot[:].rearrange("p (t n) -> p t n", n=n)[:, :, e],
                                            0.0, ALU.mult, ALU.add))
                st.wait()
                st(v.tensor_tensor(exc[:], exc[:], ps_tot[:].rearrange("p (t n) -> p t n", n=n), ALU.subtract))
                st.wait()
                st(v.tensor_tensor(exc[:], exc[:], ps_cum[:].rearrange("p (t n) -> p t n", n=n), ALU.add))
                st.wait()
                st(v.tensor_tensor(exc[:], exc[:], eq[:], ALU.mult))
                st.wait()
                st(v.tensor_reduce(pos[:], exc[:], AX, ALU.add))
                st.wait()
                st(v.tensor_scalar(pos[:], pos[:], -1.0, None, ALU.add))
                st(v.tensor_scalar(slot[:], low[:], float(CPAD), float(CPAD * n), ALU.mult, ALU.add))
                st.wait()
                st(v.tensor_scalar(kept[:], pos[:], float(CAP), None, ALU.is_lt))
                st(v.tensor_tensor(slot[:], slot[:], pos[:], ALU.add))
                st.wait()
                st(v.tensor_scalar(sm[:, 0:1], K.part[:], float(LAST), None, ALU.is_lt))
                st.wait()
                st(v.tensor_tensor(kept[:, T - 1:T], kept[:, T - 1:T], sm[:, 0:1], ALU.mult))
                st.wait()
                st(v.tensor_scalar(send[:], slot[:], float(-SLOTS), None, ALU.add))
                st(v.tensor_tensor(slot[:], slot[:], kept[:], ALU.mult))
                st.wait()
                st(v.tensor_tensor(send[:], send[:], kept[:], ALU.mult))
                st(v.tensor_copy(K.slot[:], slot[:]))
                st(v.tensor_tensor(K.share[:], mx[:], kept[:], ALU.mult))
                st.wait()
                st(v.tensor_scalar(send[:], send[:], float(SLOTS), None, ALU.add))
                st.wait()

                def seven(j, s, i):
                    if not early(j):
                        v.wait_ge(s_sent[s], i * 16 * C)
                    v.tensor_copy(idx[:, s], send[:, at(j * C, C)]).then_inc(s_stage, 1)
                    v.tensor_copy(stage[:, s], H[:, at(j * C, C), :]).then_inc(s_stage, 1)
                tiles(seven, v, T // C)

            @block.scalar
            def _(act):
                act.wait_ge(s_dve, mark["exp"])
                act.activation(pr[:], lg[:], ACT.Exp).then_inc(s_exp, 1)

            @block.tensor
            def _(pe):
                pe.wait_ge(s_dve, mark["hot"])
                hot = eq[:].rearrange("p t n -> p (t n)")
                pe.matmul(ps_cum[:], K.upto[:], hot, start=True, stop=True)
                pe.matmul(ps_tot[:], K.ones[:], hot, start=True, stop=True).then_inc(s_cum, 1)

            @block.gpsimd
            def _(pool):
                def seven(j, s, i):
                    c.hold(pool, s_stage, (j + 1) * 2)
                    for k in range(C):
                        pool.indirect_dma_start(out=slot_rows, out_offset=bass.IndirectOffsetOnAxis(ap=idx[:, s, k:k + 1], axis=0),
                                                in_=stage[:, s, k, :], in_offset=None, bounds_check=SLOTS - 1,
                                                oob_is_err=False).then_inc(s_sent[s], 16)
                tiles(seven, pool, T // C)
                for s in range(2):
                    pool.wait_ge(s_sent[s], 16 * C * ((T // C + 1 - s) // 2))


def experts(c, slot_rows, slot_out, w1, b1, w2, b2, K, acc, spare):
    nc = c.nc
    NF = FF // P
    sem = lambda x: c.sem("e_" + x)
    s_b, s_T, s_xT, s_h, s_relu, s_y, s_ys = (sem(x) for x in ("b", "T", "xT", "h", "relu", "y", "ys"))
    s_w, s_rows = ([sem(f"{x}0"), sem(f"{x}1")] for x in ("w", "rows"))
    s_store = [sem("store0"), sem("store1")]
    with ExitStack() as ctx:
        sb = lambda nm, sh, dt=F32: c.sb("e_" + nm, sh, dt, ctx)
        w1s, w2s = sb("w1s", [P, 2, 2, FF]), sb("w2s", [P, 2, NF, D])
        b1s, b2s = sb("b1s", [P, EXPERTS, NF]), sb("b2s", [P, EXPERTS, D])
        xT = sb("xT", [P, 2, 2, 512])
        free = acc[:].rearrange("p t f -> p (t f)")
        hT = free[:, 0:2 * NF * 512].rearrange("p (s f n) -> p s f n", s=2, f=NF)
        rows, ys = (free[:, 2 * NF * 512 + k * 8 * D:2 * NF * 512 + (k + 1) * 8 * D].rearrange("p (s t d) -> p s t d", s=2, t=4)
                    for k in range(2))
        ps_x = [c.ps(f"e_px{i}", [P, 512], ctx) for i in range(2)]
        ps_h = [c.ps(f"e_ph{i}", [P, 512], ctx) for i in range(2)]
        ps_y = [c.ps(f"e_py{i}", [P, 512], ctx) for i in range(4)]
        TURNS_E = EXPERTS // 2
        first = lambda i: isinstance(i, int) and i == 0

        def turns(eng, turn):
            turn(0, False)
            with eng.Fori(1, TURNS_E - 1) as i:
                turn(i, False)
            turn(TURNS_E - 1, True)
        units = lambda i: [(i * 4 + j, j % 2, i * 2 + j // 2, j // 2, j) for j in range(4)]
        with nc.Block() as block:

            @block.sync
            def _(sp):
                sp.dma_start(b1s[:], b1).then_inc(s_b, 16)
                sp.dma_start(b2s[:], b2.partition_broadcast(P)).then_inc(s_b, 16)

                def weights(e, se, u):
                    if not (isinstance(e, int) and e < 2):
                        sp.wait_ge(s_y, (u - 2) * 4)
                    sp.dma_start(w1s[:, se], w1[at(e), :, :].rearrange("a (c p) f -> p (a c) f", p=P)).then_inc(s_w[se], 16)
                    sp.dma_start(w2s[:, se], w2[at(e), :, :].rearrange("a (c p) d -> p (a c) d", p=P)).then_inc(s_w[se], 16)

                def unit_rows(u, s):
                    if not (isinstance(u, int) and u < 2):
                        sp.wait_ge(s_T, u - 1)
                    sp.dma_start(rows[:, s], slot_rows[at(u * 512, 512), :].rearrange("(t p) d -> p t d", p=P)).then_inc(s_rows[s], 16)

                def store(u, s):
                    sp.wait_ge(s_ys, (u + 1) * 4)
                    sp.dma_start(slot_out[at(u * 512, 512), :].rearrange("(t p) d -> p t d", p=P), ys[:, s]).then_inc(s_store[s], 16)

                def turn(i, last):
                    for u, s, e, se, j in units(i):
                        if not (last and j == 3):
                            unit_rows(u + 1, 1 - s)
                        if not (first(i) and j == 0):
                            store(u - 1, 1 - s)
                        if j % 2 == 0 and not (last and j == 2):
                            weights(e + 1, 1 - se, u + 2)
                unit_rows(0, 0)
                weights(0, 0, 0)
                turns(sp, turn)
                store(2 * EXPERTS - 1, 1)
                for s in range(2):
                    sp.wait_ge(s_store[s], 16 * EXPERTS)
                sp.wait_ge(s_b, 32)

            @block.gpsimd
            def _(pool):
                spare(pool)

            @block.tensor
            def _(pe):
                def turn_rows(i, j):
                    s = j % 2
                    pe.wait_ge(s_rows[s], (i * 2 + j // 2 + 1) * 16)
                    if not (first(i) and j == 0):
                        pe.wait_ge(s_xT, (i * 4 + j) * 2)
                    for t in range(4):
                        for k in range(2):
                            mm = pe.transpose(ps_x[k][:, t * P:(t + 1) * P], rows[:, s, t, k * P:(k + 1) * P], K.ident[:])
                    mm.then_inc(s_T, 1)

                def turn(i, last):
                    for u, s, e, se, j in units(i):
                        if j % 2 == 0:
                            pe.wait_ge(s_w[se], (i + 1) * 32)
                        pe.wait_ge(s_xT, (u + 1) * 2)
                        for f in range(NF):
                            if not (first(i) and j == 0 and f < 2):
                                pe.wait_ge(s_relu, u * NF + f - 1)
                            for k in range(2):
                                mm = pe.matmul(ps_h[f % 2][:], w1s[:, se, k, f * P:(f + 1) * P], xT[:, s, k, :], start=(k == 0), stop=(k == 1))
                            mm.then_inc(s_h, 1)
                        if not (last and j == 3):
                            turn_rows(i, j + 1)
                        pe.wait_ge(s_relu, (u + 1) * NF)
                        for t in range(4):
                            if not (first(i) and j == 0):
                                pe.wait_ge(s_ys, u * 4 + t - 3)
                            for f in range(NF):
                                mm = pe.matmul(ps_y[t][:, 0:D], hT[:, s, f, t * P:(t + 1) * P], w2s[:, se, f, :], start=(f == 0), stop=(f == NF - 1))
                            mm.then_inc(s_y, 1)
                turn_rows(0, 0)
                turns(pe, turn)

            @block.scalar
            def _(act):
                act.wait_ge(s_b, 32)

                def turned(u, s):
                    act.wait_ge(s_T, u + 1)
                    for k in range(2):
                        act.copy(xT[:, s, k, :], ps_x[k][:]).then_inc(s_xT, 1)

                def turn(i, last):
                    for u, s, e, se, j in units(i):
                        if not (first(i) and j < 2):
                            act.wait_ge(s_y, (u - 1) * 4)
                        for f in range(NF):
                            c.hold(act, s_h, u * NF + f + 1)
                            act.activation(hT[:, s, f, :], ps_h[f % 2][:], ACT.Relu,
                                           bias=b1s[:, at(e), f:f + 1].rearrange("p a f -> p (a f)")).then_inc(s_relu, 1)
                        if not (last and j == 3):
                            turned(u + 1, 1 - s)
                turned(0, 0)
                turns(act, turn)

            @block.vector
            def _(v):
                v.wait_ge(s_b, 32)

                def turn(i, last):
                    for u, s, e, se, j in units(i):
                        if not (first(i) and j < 2):
                            v.wait_ge(s_store[s], (i * 2 + j // 2) * 16)
                        for t in range(4):
                            v.wait_ge(s_y, u * 4 + t + 1)
                            v.tensor_tensor(ys[:, s, t, :], ps_y[t][:, 0:D], b2s[:, at(e), :].rearrange("p a d -> p (a d)"),
                                            ALU.add).then_inc(s_ys, 1)
                turns(v, turn)


def fetch_back(c, K, slot_out, X, spare):
    nc = c.nc
    C = 7
    s_dve, s_idx, s_share = c.sem("b_dve"), c.sem("b_idx"), c.sem("b_share")
    s_got = [c.dma_sem("b_got0"), c.dma_sem("b_got1")]
    FMAX = float(np.finfo(np.float32).max)
    STEPS = 6
    with ExitStack() as ctx:
        sb = lambda nm, sh, dt=F32: c.sb("b_" + nm, sh, dt, ctx)
        idx, y = sb("idx", [P, 2, C], I32), sb("y", [P, 2, C, D])
        z, low, m = sb("z", [P, C, D]), sb("low", [P, C, D]), sb("m", [P, C, D], I32)
        with nc.Block() as block:

            @block.gpsimd
            def _(pool):
                def seven(j, s, i):
                    c.hold(pool, s_idx, j + 1)
                    for k in range(C):
                        pool.indirect_dma_start(out=y[:, s, k, :], out_offset=None, in_=slot_out,
                                                in_offset=bass.IndirectOffsetOnAxis(ap=idx[:, s, k:k + 1], axis=0)).then_inc(s_got[s], 16)
                tiles(seven, pool, T // C)
                spare(pool)

            @block.scalar
            def _(act):
                def seven(j, s, i):
                    c.hold(act, s_got[s], (i + 1) * 16 * C)
                    for k in range(C):
                        act.activation(y[:, s, k, :], y[:, s, k, :], ACT.Copy, scale=K.share[:, at(j * C + k)]).then_inc(s_share, 1)
                tiles(seven, act, T // C)

            @block.vector
            def _(v):
                st = Steps(v, s_dve)

                def slots(j, s):
                    v.tensor_copy(idx[:, s], K.slot[:, at(j * C, C)]).then_inc(s_idx, 1)

                def seven(j, s, i):
                    st.turn(j, 0, STEPS)
                    if not (isinstance(j, int) and j == T // C - 1):
                        slots(j + 1, 1 - s)
                    v.wait_ge(s_share, (j + 1) * C)
                    ys = y[:, s]
                    st(v.tensor_scalar(z[:], ys, FMAX, 10000.0, ALU.is_gt, ALU.mult))
                    st(v.tensor_scalar(low[:], ys, -FMAX, 10000.0, ALU.is_lt, ALU.mult))
                    st(v.tensor_scalar(m[:], ys, 0.0, 0.0, ALU.mult, ALU.is_equal))
                    st.wait()
                    st(v.tensor_tensor(z[:], z[:], low[:], ALU.subtract))
                    c.hold(v, *st.point())
                    st(v.copy_predicated(z[:], m[:], ys))
                    st.wait()
                    o = X[:, at(j * C, C), :]
                    st(v.tensor_tensor(o, o, z[:], ALU.add))
                    st.wait()
                slots(0, 0)
                tiles(seven, v, T // C)


def gate_tables(c, K, hg, att, tab_s, ad):
    nc = c.nc
    h = HEADS2
    s_ld, s_dve, s_pool, s_st = (c.sem("t_" + x) for x in ("ld", "dve", "pool", "st"))
    mark = {}
    with ExitStack() as ctx:
        sb = lambda nm, sh, dt=F32: c.sb("t_" + nm, sh, dt, ctx)
        av, tmp, elv = sb("av", [P, 2, 16]), sb("tmp", [P, T, 16]), sb("elv", [P, T, h])
        vm, elm, gmax = sb("vm", [P, 2]), sb("elm", [P, 2, h]), sb("gmax", [P, 2, h])
        with nc.Block() as block:

            @block.vector
            def _(v):
                st = Steps(v, s_dve)
                v.wait_ge(s_ld, 16)
                for side in range(2):
                    st(v.tensor_tensor(tmp[:], hg[:, :, 0:16], av[:, side, :].unsqueeze(1).to_broadcast([P, T, 16]), ALU.mult))
                    st.wait()
                    o = hg[:, :, 16:20] if side == 0 else ad[:, :, 0:h]
                    st(v.tensor_reduce(o, tmp[:].rearrange("p t (h e) -> p t h e", h=h), AX, ALU.add))
                    st.wait()
                st(v.tensor_copy(elv[:], hg[:, :, 16:20]))
                st(v.tensor_scalar(vm[:, 0:1], K.part[:], float(LAST), None, ALU.is_lt))
                st.wait()
                st(v.tensor_scalar(vm[:, 1:2], vm[:, 0:1], BIG, -BIG, ALU.mult, ALU.add))
                st.wait()
                st(v.tensor_scalar(elv[:, T - 1, :], elv[:, T - 1, :], vm[:, 0:1], vm[:, 1:2], ALU.mult, ALU.add))
                extremes(v, st, elm, elv, vm, s_pool)
                v.wait_ge(s_pool, 2)
                shifts(v, st, K, ad, gmax, h)
                mark["tab"] = st.n

            @block.sync
            def _(sp):
                sp.dma_start(av[:], att.partition_broadcast(P)).then_inc(s_ld, 16)
                sp.wait_ge(s_dve, mark["tab"])
                sp.dma_start(tab_s.rearrange("(t p) n -> p t n", p=P), hg[:]).then_inc(s_st, 16)
                sp.wait_ge(s_st, 16)

            @block.gpsimd
            def _(pool):
                pool.wait_ge(s_pool, 1)
                pool.partition_all_reduce(gmax[:].rearrange("p a h -> p (a h)"), elm[:].rearrange("p a h -> p (a h)"), P, RED.max).then_inc(s_pool, 1)


def gate_scores(c, K, hg, ad, agg, consts, gates):
    nc = c.nc
    h, n = HEADS2, EXPERTS2
    s_ld, s_dve, s_act = (c.sem("u_" + x) for x in ("ld", "dve", "act"))
    mark = {}
    with ExitStack() as ctx:
        sb = lambda nm, sh, dt=F32: c.sb("u_" + nm, sh, dt, ctx)
        cs = sb("cs", [P, 3, 16])
        z, w, o, q = sb("z", [P, T, h]), sb("w", [P, T, h]), sb("o", [P, T, 16]), sb("q", [P, T, 16])
        mu, var, sc = sb("mu", [P, T]), sb("var", [P, T]), sb("sc", [P, T, n])
        b1, b2, low, e1, e2 = sb("b1", [P, T]), sb("b2", [P, T]), sb("low", [P, T]), sb("e1", [P, T, n]), sb("e2", [P, T, n])
        wide = lambda a, k: a.unsqueeze(2).to_broadcast([P, T, k])
        heads = lambda a: a.unsqueeze(3).to_broadcast([P, T, h, 4])
        each = lambda a: a.rearrange("p t (h e) -> p t h e", h=h)
        row = lambda k: cs[:, k, :].unsqueeze(1).to_broadcast([P, T, 16])
        with nc.Block() as block:

            @block.vector
            def _(v):
                st = Steps(v, s_dve)

                def do(ins):
                    st(ins)
                    st.wait()
                do(v.tensor_tensor(z[:], hg[:, :, 16:20], ad[:, :, 0:h], ALU.add))
                do(v.scalar_tensor_tensor(z[:], z[:], 0.2, z[:], ALU.mult, ALU.max))
                do(v.tensor_tensor(z[:], z[:], ad[:, :, h:2 * h], ALU.subtract))
                mark["z"] = st.n
                v.wait_ge(s_act, 1)
                v.wait_ge(s_ld, 16)
                do(v.tensor_tensor(each(o[:]), each(hg[:, :, 0:16]), heads(w[:]), ALU.mult))
                do(v.tensor_tensor(o[:], o[:], agg[:, :, 0:16], ALU.add))
                do(v.tensor_tensor(w[:], w[:], agg[:, :, 16:20], ALU.add))
                do(v.reciprocal(w[:], w[:]))
                do(v.tensor_tensor(each(o[:]), each(o[:]), heads(w[:]), ALU.mult))
                do(v.tensor_tensor(o[:], o[:], row(0), ALU.add))
                do(v.tensor_reduce(mu[:], o[:], AX, ALU.add))
                do(v.tensor_scalar(mu[:], mu[:], 1.0 / 16, None, ALU.mult))
                do(v.tensor_tensor(o[:], o[:], wide(mu[:], 16), ALU.subtract))
                do(v.tensor_tensor(q[:], o[:], o[:], ALU.mult))
                do(v.tensor_reduce(var[:], q[:], AX, ALU.add))
                do(v.tensor_scalar(var[:], var[:], 1.0 / 16, LN_EPS, ALU.mult, ALU.add))
                mark["var"] = st.n
                v.wait_ge(s_act, 2)
                do(v.reciprocal(var[:], var[:]))
                do(v.tensor_tensor(o[:], o[:], wide(var[:], 16), ALU.mult))
                do(v.tensor_tensor(o[:], o[:], row(1), ALU.mult))
                do(v.tensor_tensor(o[:], o[:], row(2), ALU.add))
                do(v.tensor_reduce(sc[:], o[:].rearrange("p t (h e) -> p t e h", h=h), AX, ALU.add))
                do(v.tensor_scalar(sc[:], sc[:], 1.0 / h, None, ALU.mult))
                first_of_best(v, st, K, sc[:], n, b1[:], e1[:], low[:])
                do(v.scalar_tensor_tensor(sc[:], e1[:], -BIG, sc[:], ALU.mult, ALU.add))
                first_of_best(v, st, K, sc[:], n, b2[:], e2[:], low[:])
                do(v.tensor_tensor(b2[:], b2[:], b1[:], ALU.subtract))
                mark["gap"] = st.n
                v.wait_ge(s_act, 3)
                do(v.tensor_scalar(b1[:], b2[:], 1.0, None, ALU.add))
                do(v.reciprocal(b1[:], b1[:]))
                do(v.tensor_tensor(b2[:], b2[:], b1[:], ALU.mult))
                do(v.tensor_tensor(e1[:], e1[:], wide(b1[:], n), ALU.mult))
                do(v.tensor_tensor(e2[:], e2[:], wide(b2[:], n), ALU.mult))
                do(v.tensor_tensor(gates[:], e1[:], e2[:], ALU.add))

            @block.sync
            def _(sp):
                sp.dma_start(cs[:], consts.partition_broadcast(P)).then_inc(s_ld, 16)
                sp.wait_ge(s_ld, 16)

            @block.scalar
            def _(act):
                act.wait_ge(s_dve, mark["z"])
                act.activation(w[:], z[:], ACT.Exp).then_inc(s_act, 1)
                act.wait_ge(s_dve, mark["var"])
                act.activation(var[:], var[:], ACT.Sqrt).then_inc(s_act, 1)
                act.wait_ge(s_dve, mark["gap"])
                act.activation(b2[:], b2[:], ACT.Exp).then_inc(s_act, 1)


class ExpertsTwo:

    def __init__(self, K, H, w1, b1, w2, b2, y_dram):
        self.K, self.H, self.w1, self.b1, self.w2, self.b2, self.y_dram = K, H, w1, b1, w2, b2, y_dram

    TILES, NF, NE = 3, FF2 // P, EXPERTS2
    UNITS = -(-T // TILES)
    LEFT = T - (UNITS - 1) * TILES

    def place(self, c, ctx):
        sb = lambda nm, sh, dt=F32: c.sb("v_" + nm, sh, dt, ctx)
        NE, NF, n = self.NE, self.NF, self.TILES
        self.w1s, self.w2s = sb("w1s", [P, NE, 2, FF2]), sb("w2s", [P, NE, NF, D])
        self.b1s, self.b2s = sb("b1s", [P, NE, NF]), sb("b2s", [P, NE, D])
        self.rows, self.xT, self.hT, self.ys = sb("rows", [P, n, D]), sb("xT", [P, 2, n * P]), sb("hT", [P, NF, n * P]), sb("ys", [P, n, D])
        self.ps_h = [c.ps(f"v_ph{i}", [P, 512], ctx) for i in range(2)]
        self.ps_y = [c.ps(f"v_py{i}", [P, 2, D], ctx) for i in range(2)]
        sem = lambda x: c.sem("v_" + x)
        (self.s_ld, self.s_place, self.s_T, self.s_xT, self.s_h, self.s_act, self.s_y, self.s_ys) = (
            sem(x) for x in ("ld", "place", "T", "xT", "h", "act", "y", "ys"))
        self.s_store = sem("store")

    def count(self, i):
        return (self.LEFT, 1) if isinstance(i, int) and i == self.UNITS - 1 else (self.TILES, 2)

    def sync(self, sp):
        for tile, source in ((self.w1s, self.w1), (self.w2s, self.w2), (self.b1s, self.b1)):
            sp.dma_start(tile[:], source).then_inc(self.s_ld, 16)
        sp.dma_start(self.b2s[:], self.b2.partition_broadcast(P)).then_inc(self.s_ld, 16)

        def unit(i):
            n, adds = self.count(i)
            for e in range(self.NE):
                sp.wait_ge(self.s_ys, i * 2 * self.NE + (e + 1) * adds)
                sp.dma_start(self.y_dram[e, at(i * self.TILES * P, n * P), :].rearrange("(t p) d -> p t d", p=P),
                             self.ys[:, 0:n, :]).then_inc(self.s_store, 16)
        loop(sp, self.UNITS, unit, peel=True)
        sp.wait_ge(self.s_store, 16 * self.UNITS * self.NE)
        sp.wait_ge(self.s_ld, 64)

    def vector_rows(self, v, i, r):
        if r == 0:
            n, _ = self.count(i)
            if not (isinstance(i, int) and i == 0):
                v.wait_ge(self.s_T, i)
            v.tensor_copy(self.rows[:, 0:n, :], self.H[:, at(i * self.TILES, n), :]).then_inc(self.s_place, 1)

    def vector_results(self, v, i, r):
        if r % 2 or (isinstance(i, int) and i == 0 and r == 0):
            return
        e = (r // 2 - 1) % self.NE
        unit = i if r else i - 1
        n, adds = self.count(unit)
        start = isinstance(i, int) and i == 0
        if start and r == 2:
            v.wait_ge(self.s_ld, 64)
        v.wait_ge(self.s_y, unit * self.NE + e + 1)
        if not (start and e == 0):
            v.wait_ge(self.s_store, (unit * self.NE + e) * 16)
        bias = self.b2s[:, e, :].unsqueeze(1)
        for half in range(adds):
            m = min(2, n - 2 * half)
            v.tensor_tensor(self.ys[:, 2 * half:2 * half + m, :], self.ps_y[half][:, 0:m, :],
                            bias.to_broadcast([P, m, D]), ALU.add).then_inc(self.s_ys, 1)

    def tensor(self, pe, i, r, part):
        K, NF, NE, e = self.K, self.NF, self.NE, r // 2
        n, adds = self.count(i)
        w = n * P
        start = isinstance(i, int) and i == 0
        if r == 0 and part == 0:
            if start:
                pe.wait_ge(self.s_ld, 64)
            else:
                pe.wait_ge(self.s_act, i * NE * NF)
            pe.wait_ge(self.s_place, i + 1)
            for t in range(n):
                for k in range(2):
                    mm = pe.transpose(self.ps_h[k][:, t * P:(t + 1) * P], self.rows[:, t, k * P:(k + 1) * P], K.ident[:])
            mm.then_inc(self.s_T, 1)
            pe.wait_ge(self.s_xT, (i + 1) * 2)
        if r % 2 == 0:
            for f in range(part * NF // 2, (part + 1) * NF // 2):
                if not (e == 0 and f < 2):
                    pe.wait_ge(self.s_act, (i * NE + e) * NF + f - 1)
                for k in range(2):
                    mm = pe.matmul(self.ps_h[f % 2][:, 0:w], self.w1s[:, e, k, f * P:(f + 1) * P], self.xT[:, k, 0:w], start=(k == 0), stop=(k == 1))
                mm.then_inc(self.s_h, 1)
        else:
            if part == 0:
                pe.wait_ge(self.s_act, (i * NE + e + 1) * NF)
                if not (start and e == 0):
                    pe.wait_ge(self.s_ys, i * 2 * NE + e * adds)
            for t in range(0, min(n, 2)) if part == 0 else range(2, n):
                for f in range(NF):
                    mm = pe.matmul(self.ps_y[t // 2][:, t % 2, :], self.hT[:, f, t * P:(t + 1) * P], self.w2s[:, e, f, :], start=(f == 0), stop=(f == NF - 1))
            if part == (n > 2):
                mm.then_inc(self.s_y, 1)

    def scalar(self, act, i, r):
        NF, NE, e = self.NF, self.NE, r // 2
        w = self.count(i)[0] * P
        start = isinstance(i, int) and i == 0
        if r == 0:
            act.wait_ge(self.s_T, i + 1)
            for k in range(2):
                act.copy(self.xT[:, k, 0:w], self.ps_h[k][:, 0:w]).then_inc(self.s_xT, 1)
        if r % 2 == 0:
            if start and e == 0:
                act.wait_ge(self.s_ld, 64)
            else:
                act.wait_ge(self.s_y, i * NE + e)
            for f in range(NF):
                act.wait_ge(self.s_h, (i * NE + e) * NF + f + 1)
                act.activation(self.hT[:, f, 0:w], self.ps_h[f % 2][:, 0:w], ACT.Gelu, bias=self.b1s[:, e, f:f + 1]).then_inc(self.s_act, 1)


def mix(c, X, gates, y_dram, out):
    nc = c.nc
    C, NE = 7, EXPERTS2
    s_y, s_dve, s_out = [c.sem("m_y0"), c.sem("m_y1")], c.sem("m_dve"), c.sem("m_out")
    with ExitStack() as ctx:
        y = c.sb("m_y", [P, 2, NE, C, D], F32, ctx)
        with nc.Block() as block:

            @block.scalar
            def _(act):
                def seven(j, s, i):
                    if not early(j):
                        act.wait_ge(s_dve, (j - 1) * NE * C)
                    for e in range(NE):
                        act.dma_start(y[:, s, e], y_dram[e, at(j * C * P, C * P), :].rearrange("(t p) d -> p t d", p=P)).then_inc(s_y[s], 16)
                tiles(seven, act, T // C)

            @block.vector
            def _(v):
                def seven(j, s, i):
                    v.wait_ge(s_y[s], (i + 1) * 16 * NE)
                    for e in range(NE):
                        if e:
                            v.wait_ge(s_dve, j * NE * C + e * C)
                        for t in range(C):
                            o = X[:, at(j * C + t), :].rearrange("p a d -> p (a d)")
                            v.scalar_tensor_tensor(o, y[:, s, e, t, :], gates[:, at(j * C + t), e], o, ALU.mult, ALU.add).then_inc(s_dve, 1)
                tiles(seven, v, T // C)

            @block.sync
            def _(sp):
                def seven(j, s, i):
                    sp.wait_ge(s_dve, (j + 1) * NE * C)
                    whole = C - 1 if isinstance(j, int) and j == T // C - 1 else C
                    sp.dma_start(out[at(j * C * P, whole * P), :].rearrange("(t p) d -> p t d", p=P), X[:, at(j * C, whole), :]).then_inc(s_out, 16)
                tiles(seven, sp, T // C)
                sp.dma_start(out[(T - 1) * P:N, :], X[0:LAST, T - 1, :]).then_inc(s_out, 16)
                sp.wait_ge(s_out, 16 * (T // C + 1))


def build(nc, a, out):
    with ExitStack() as ctx:
        c = Chip(nc, ctx)

        class K:
            ident, ones, upto, iota = (c.sb(n, [P, P]) for n in ("ident", "ones", "upto_", "iota"))
            part = c.sb("part", [P, 1])
            low, spread = c.sb("low_", [P, 8]), c.sb("spread", [P, 8])
            most, far = c.sb("most_", [P, 1]), c.sb("far", [P, 1], I32)
            iota_low = c.sb("iota_low", [P, P])
            norm, share, slot = c.sb("norm", [P, T]), c.sb("share", [P, T]), c.sb("slot", [P, T], I32)
        dram = lambda n, sh, dt=F32: nc.dram_tensor(n, list(sh), dt).ap()
        slot_rows, slot_out = dram("slot_rows", [SLOTS, D]), dram("slot_out", [SLOTS, D])
        table8, table4, table1 = dram("table8", [NPAD, D + 8]), dram("table4", [NPAD, D + 4]), dram("table1", [NPAD, D + 2])
        tab_s, y_dram = dram("tab_s", [NPAD, 20]), dram("y_dram", [EXPERTS2, NPAD, D])
        base_a, base_b = dram("base_a", [NPAD, 2 * D]), dram("base_b", [NPAD, D])
        X, acc = c.sb("X", [P, T, D]), c.sb("acc", [P, T, D + 9])
        H = acc[:, :, 0:D]
        e2 = Edges(c, "e2", ROWS2, 8, ctx)
        graph = ctx.enter_context(ExitStack())
        e1 = Edges(c, "e1", ROWS, 4, graph)
        packed2 = c.sb("packed2", [P, ROWS2, 3], I32, graph)
        send2 = Sender(c, "s2", e2, packed2, graph)
        K.er = c.sb("er", [P, T, 16], F32, graph)
        e1.columns(c, graph)
        ordering = ExitStack()
        tile2 = c.sb("tile2", [P, ROWS2], F32, ordering)
        order2 = Order(c, "o2", e2, tile2[:], packed2, ordering)
        prepare(c, a, K, X, acc, e1, e2, slot_rows, packed2, tile2)
        layernorm(c, "n1_", X, H)
        project(c, "a1_", K, H, a["L0_gnn_fc1_wT"], a["L0_gnn_fc1_w"], a["attn_a1"], 8,
                table8, Base(a["w_base"], a["b_base"], base_a), order=order2)
        ordering.close()
        make_columns(c, K, e1)
        exact_shifts(c, "x1_", K, e1, table8, 8, D, K.er)
        attend(c, "g1_", K, e1, table8, 8, D, K.er, acc)
        combine(c, "c1_", K, acc, 8, H, a["L0_gnn_bias1"], (base_a[:, 0:D],), relu=True, degree=True,
                spare=lambda pool: send2.send(pool, 5, "a"))
        project(c, "a2_", K, H, a["L0_gnn_fc2_wT"], a["L0_gnn_fc2_w"], a["attn_a2"], 1,
                table1, Base(a["w_base2"], None, base_b), spare=lambda pool: send2.send(pool, 5, "b"))
        exact_shifts(c, "x2_", K, e1, table1, 1, D, K.er)
        attend(c, "g2_", K, e1, table1, 1, D, K.er, acc)
        combine(c, "c2_", K, acc, 1, X, a["L0_gnn_bias2"], (base_a[:, D:2 * D], base_b), residual=True,
                spare=lambda pool: send2.send(pool, 5, "c"))
        c.renew()
        layernorm(c, "n2_", X, H, spare=lambda pool: send2.send(pool, 2, "n2"))
        with ExitStack() as gate:
            lg = c.sb("lg", [P, T, EXPERTS], F32, gate)
            narrow(c, "r1_", K, H, a["L0_ffn_gate_w"], lg, spare=lambda pool: send2.send(pool, 3, "d"))
            route(c, K, lg, a["L0_ffn_gate_b"], H, slot_rows)
        experts(c, slot_rows, slot_out, a["L0_ffn_w1"], a["L0_ffn_b1"], a["L0_ffn_w2"], a["L0_ffn_b2"], K, acc,
                spare=lambda pool: send2.send(pool, 28, "experts"))
        fetch_back(c, K, slot_out, X, spare=lambda pool: send2.send(pool, 2, "fetch"))
        c.renew()
        layernorm(c, "n3_", X, H, spare=lambda pool: send2.send(pool, 2, "n3"))
        project(c, "b1_", K, H, a["L1_gnn_W1T"], a["L1_gnn_W1"], a["attn_c1"], 4, table4,
                spare=lambda pool: send2.send(pool, 5, "e"))
        exact_shifts(c, "x3_", K, e1, table4, 4, D, K.er)
        attend(c, "g3_", K, e1, table4, 4, D, K.er, acc)

        def last_edges(pool):
            send2.send(pool, ROWS2 // (2 * G) - send2.done, "g")
            send2.finish(pool)
        combine(c, "c3_", K, acc, 4, H, relu=True, spare=lambda pool: send2.send(pool, 2, "f"))
        project(c, "b2_", K, H, a["L1_gnn_W2T"], a["L1_gnn_W2"], a["attn_c2"], 1, table1, spare=last_edges)
        exact_shifts(c, "x4_", K, e1, table1, 1, D, K.er)
        attend(c, "g4_", K, e1, table1, 1, D, K.er, acc)
        combine(c, "c4_", K, acc, 1, X, residual=True)
        graph.close()
        c.renew()
        layernorm(c, "n4_", X, H)
        hg, ad, agg = c.sb("hg", [P, T, 20]), c.sb("ad", [P, T, 8]), c.sb("agg", [P, T, 21])
        narrow(c, "r2_", K, H, a["L1_ffn_W_gat"], hg[:, :, 0:16])
        gate_tables(c, K, hg, a["gate_att"], tab_s, ad)
        with ExitStack() as lists:
            e2.columns(c, lists)
            make_columns(c, K, e2)
            assert e2.NG // e2.R == ExpertsTwo.UNITS and e2.R == 2 * EXPERTS2
            exact_shifts(c, "x5_", K, e2, tab_s, HEADS2, 16, ad, hg[:, :, 16:20])
            attend(c, "g5_", K, e2, tab_s, HEADS2, 16, ad, agg,
                   ExpertsTwo(K, H, a["L1_ffn_W1"], a["L1_ffn_b1"], a["L1_ffn_W2"], a["L1_ffn_b2"], y_dram))
        gates = c.sb("gates", [P, T, EXPERTS2])
        gate_scores(c, K, hg, ad, agg, a["gate_norm"], gates)
        mix(c, X, gates, y_dram, out)


def _layout(inputs):
    a = {k: np.ascontiguousarray(v) for k, v in inputs.items()}
    o = {"x": a["x"]}
    o["src"] = np.pad(a["src"], (0, ROWS * P - E)).reshape(ROWS, P)
    o["dst"] = np.pad(a["dst"], (0, (ROWS + 1) * P - E), constant_values=1 << 20).reshape(ROWS + 1, P)
    o["edges1"] = np.stack([o["src"].reshape(-1), o["dst"].reshape(-1)[:ROWS * P]], axis=1)
    o["L0_gnn_fc1_w"], o["L0_gnn_fc1_wT"] = a["L0_gnn_fc1_w"], a["L0_gnn_fc1_w"].T
    o["L0_gnn_fc2_w"], o["L0_gnn_fc2_wT"] = a["L0_gnn_fc2_w"], a["L0_gnn_fc2_w"].T
    for n, l, r in (("a1", "L0_gnn_attn_l1", "L0_gnn_attn_r1"), ("a2", "L0_gnn_attn_l2", "L0_gnn_attn_r2"),
                    ("c1", "L1_gnn_a1_src", "L1_gnn_a1_dst"), ("c2", "L1_gnn_a2_src", "L1_gnn_a2_dst")):
        o["attn_" + n] = np.stack([a[l].reshape(2, P).T, a[r].reshape(2, P).T], axis=2)
    o["w_base"] = np.concatenate([a["L0_gnn_wb0"].T, a["L0_gnn_wb1"][:, :D].T], axis=1)
    o["b_base"] = np.concatenate([a["L0_gnn_bb0"], a["L0_gnn_bb1"]]).reshape(1, 2 * D)
    o["w_base2"] = a["L0_gnn_wb1"][:, D:].T
    o["L0_gnn_bias1"], o["L0_gnn_bias2"] = a["L0_gnn_bias1"], a["L0_gnn_bias2"]
    for n in ("gate_w", "gate_b", "w1", "w2", "b2"):
        o["L0_ffn_" + n] = a["L0_ffn_" + n]
    o["L0_ffn_b1"] = a["L0_ffn_b1"].reshape(EXPERTS, FF // P, P).transpose(2, 0, 1)
    for n in ("W1", "W2"):
        o["L1_gnn_" + n], o["L1_gnn_" + n + "T"] = a["L1_gnn_" + n], a["L1_gnn_" + n].T
    o["L1_ffn_W_gat"] = a["L1_ffn_W_gat"]
    o["gate_att"] = np.stack([a["L1_ffn_att_src"].reshape(-1), a["L1_ffn_att_dst"].reshape(-1)])
    o["gate_norm"] = np.stack([a["L1_ffn_b_gat"], a["L1_ffn_ln_gamma"], a["L1_ffn_ln_beta"]])
    o["src2"], o["dst2"] = a["L1_ffn_edge_index"].reshape(2, P, ROWS2)
    o["L1_ffn_W1"] = a["L1_ffn_W1"].reshape(EXPERTS2, 2, P, FF2).transpose(2, 0, 1, 3)
    o["L1_ffn_W2"] = a["L1_ffn_W2"].reshape(EXPERTS2, FF2 // P, P, D).transpose(2, 0, 1, 3)
    o["L1_ffn_b1"] = a["L1_ffn_b1"].reshape(EXPERTS2, FF2 // P, P).transpose(2, 0, 1)
    o["L1_ffn_b2"] = a["L1_ffn_b2"]
    return {k: np.ascontiguousarray(v) for k, v in o.items()}


def kernel(**inputs):
    from concourse import bacc
    from concourse.bass_utils import run_bass_kernel_spmd

    nc = bacc.Bacc("TRN2", target_bir_lowering=False, num_devices=1)
    arrays = {f"in_{k}": v for k, v in _layout(inputs).items()}
    args = {k[3:]: nc.dram_tensor(k, v.shape, mybir.dt.from_np(v.dtype), kind="ExternalInput").ap() for k, v in arrays.items()}
    out = nc.dram_tensor("out", [N, D], F32, kind="ExternalOutput").ap()
    build(nc, args, out)
    return run_bass_kernel_spmd(nc, [arrays], core_ids=[0]).results[0]["out"]
```
